# Optimizing a Trainium2 kernel written in Bass

```python
import numpy as np
import jax
import jax.numpy as jnp

def _softmax(x, axis=-1):
    return jax.nn.softmax(x, axis=axis)

def _gelu(x):
    return jax.nn.gelu(x, approximate=True)

def _silu(x):
    return jax.nn.silu(x)

def _sigmoid(x):
    return jax.nn.sigmoid(x)

def _layernorm(x, axis=-1, eps=1e-05):
    m = jnp.mean(x, axis=axis, keepdims=True)
    v = jnp.var(x, axis=axis, keepdims=True)
    return (x - m) / jnp.sqrt(v + eps)

def _scatter_add(tgt, idx, src, axis=0):
    return tgt.at[idx].add(src)

def _segment_sum(src, seg, n):
    return jax.ops.segment_sum(src, seg, n)
kernel_name = 'mk_pixart_seq_d4_seqx_r8_919e9a'

def setup_inputs(seed: int=0):
    np.random.seed(seed)
    _w = jnp.asarray

    def _rec_inputs():
        import jax
        import jax.numpy as jnp
        _rk = jax.random.key(seed)
        x = -0.0005207 + 1.001 * jax.random.normal(jax.random.fold_in(_rk, 1), (8, 256, 128), jnp.float32)
        _lenS = 256 - jax.random.randint(jax.random.fold_in(_rk, 7), (8,), 0, max(1, 256 // 4) + 1, jnp.int32)
        _lenS2 = 1601 - jax.random.randint(jax.random.fold_in(_rk, 8), (8,), 0, max(1, 1601 // 4) + 1, jnp.int32)
        cond_1024 = 0.000887014 + 1.03683 * jax.random.normal(jax.random.fold_in(_rk, 11), (8, 128), jnp.float32)
        _ctx_768P = jax.random.normal(jax.random.fold_in(_rk, 12), (8, 16, 96), jnp.float32)
        _ctx_768c = jax.random.dirichlet(jax.random.fold_in(_rk, 512), 0.3 * jnp.ones((16,), jnp.float32), (8, 1601))
        _ctx_768t = jnp.einsum('bsk,bkd->bsd', _ctx_768c, _ctx_768P)
        _ctx_768t = _ctx_768t * jax.lax.rsqrt(jnp.mean(jnp.square(_ctx_768t)) + 1e-12) * 0.953939
        ctx_768 = 0.000599585 + 1.00006 * (_ctx_768t + 0.3 * jax.random.normal(jax.random.fold_in(_rk, 612), (8, 1601, 96), jnp.float32))
        return (x, cond_1024, ctx_768)
    x, cond_1024, ctx_768 = _rec_inputs()

    def _L0_xcond_setup():
        import jax, jax.numpy as jnp
        import numpy as np
        B, N, M = (2, 128, 64)
        D, H, DH = (128, 16, 64)
        MID = H * DH
        DC = 96
        MULT = 4
        EPS = 1e-05

        def _ln(x, w, b):
            mu = jnp.mean(x, -1, keepdims=True)
            var = jnp.mean((x - mu) ** 2, -1, keepdims=True)
            return (x - mu) * jax.lax.rsqrt(var + EPS) * w + b

        def _sincos(n, d):
            inv = 1.0 / 10000.0 ** (jnp.arange(0, d, 2, dtype=jnp.float32) / d)
            ang = jnp.arange(n, dtype=jnp.float32)[:, None] * inv[None, :]
            return (jnp.sin(ang), jnp.cos(ang))

        def _rope(x, sin, cos):
            s = sin[None, None]
            c = cos[None, None]
            xe = x[..., ::2]
            xo = x[..., 1::2]
            re = xe * c - xo * s
            ro = xe * s + xo * c
            return jnp.stack((re, ro), axis=-1).reshape(x.shape)

        def _heads(t):
            b, n, _ = t.shape
            return t.reshape(b, n, H, DH).transpose(0, 2, 1, 3)

        def _attn(xq, ctx, wq, wkv, wo, bo):
            q = _heads(xq @ wq)
            k, v = jnp.split(ctx @ wkv, 2, axis=-1)
            k = _heads(k)
            v = _heads(v)
            sq, cq = _sincos(q.shape[2], DH)
            sk, ck = _sincos(k.shape[2], DH)
            q = _rope(q, sq, cq)
            k = _rope(k, sk, ck)
            sim = jnp.einsum('bhnd,bhmd->bhnm', q, k) * DH ** (-0.5)
            a = jax.nn.softmax(sim, axis=-1)
            o = jnp.einsum('bhnm,bhmd->bhnd', a, v)
            o = o.transpose(0, 2, 1, 3).reshape(xq.shape[0], xq.shape[1], MID)
            return o @ wo + bo

        def _adaln(x, c, lw, lb, gw, gb, bw, bb):
            g = (c @ gw + gb)[:, None, :]
            bt = (c @ bw + bb)[:, None, :]
            return _ln(x, lw, lb) * (1.0 + g) + bt
        ks = jax.random.split(jax.random.key(seed), 24)
        s = 0.02
        inp = {'x': jax.random.normal(ks[0], (B, N, D), jnp.float32), 'cond': jax.random.normal(ks[1], (B, D), jnp.float32), 'context': jax.random.normal(ks[2], (B, M, DC), jnp.float32), 'ln1_w': jnp.ones((D,), jnp.float32), 'ln1_b': jnp.zeros((D,), jnp.float32), 'g1_w': jax.random.normal(ks[3], (D, D), jnp.float32) * s, 'g1_b': jnp.zeros((D,), jnp.float32), 'b1_w': jax.random.normal(ks[4], (D, D), jnp.float32) * s, 'b1_b': jnp.zeros((D,), jnp.float32), 'ln2_w': jnp.ones((D,), jnp.float32), 'ln2_b': jnp.zeros((D,), jnp.float32), 'g2_w': jax.random.normal(ks[5], (D, D), jnp.float32) * s, 'g2_b': jnp.zeros((D,), jnp.float32), 'b2_w': jax.random.normal(ks[6], (D, D), jnp.float32) * s, 'b2_b': jnp.zeros((D,), jnp.float32), 'sa_wq': jax.random.normal(ks[7], (D, MID), jnp.float32) * s, 'sa_wkv': jax.random.normal(ks[8], (D, 2 * MID), jnp.float32) * s, 'sa_wo': jax.random.normal(ks[9], (MID, D), jnp.float32) * s, 'sa_bo': jnp.zeros((D,), jnp.float32), 'ca_lnc_w': jnp.ones((DC,), jnp.float32), 'ca_lnc_b': jnp.zeros((DC,), jnp.float32), 'ca_wq': jax.random.normal(ks[10], (D, MID), jnp.float32) * s, 'ca_wkv': jax.random.normal(ks[11], (DC, 2 * MID), jnp.float32) * s, 'ca_wo': jax.random.normal(ks[12], (MID, D), jnp.float32) * s, 'ca_bo': jnp.zeros((D,), jnp.float32), 'ff_w1': jax.random.normal(ks[13], (D, MULT * D), jnp.float32) * s, 'ff_b1': jnp.zeros((MULT * D,), jnp.float32), 'ff_w2': jax.random.normal(ks[14], (MULT * D, D), jnp.float32) * s, 'ff_b2': jnp.zeros((D,), jnp.float32)}
        return inp
    _L0_xcond_all = _L0_xcond_setup()
    _L0_xcond_in = {k: v for k, v in _L0_xcond_all.items() if k in ('ln1_w', 'ln1_b', 'g1_w', 'g1_b', 'b1_w', 'b1_b', 'ln2_w', 'ln2_b', 'g2_w', 'g2_b', 'b2_w', 'b2_b', 'sa_wq', 'sa_wkv', 'sa_wo', 'sa_bo', 'ca_lnc_w', 'ca_lnc_b', 'ca_wq', 'ca_wkv', 'ca_wo', 'ca_bo', 'ff_w1', 'ff_b1', 'ff_w2', 'ff_b2')}
    del _L0_xcond_all

    def _L1_xcond_setup():
        import jax, jax.numpy as jnp
        import numpy as np
        B, N, D, H, TD, TL = (4, 128, 128, 16, 96, 77)
        HD = D // H
        EPS = 1e-06

        def _ln(x):
            mu = jnp.mean(x, axis=-1, keepdims=True)
            var = jnp.var(x, axis=-1, keepdims=True)
            return (x - mu) * jax.lax.rsqrt(var + EPS)

        def _modulate(x, shift, scale):
            return x * (1.0 + scale[:, None, :]) + shift[:, None, :]

        def _heads(t):
            return t.reshape(t.shape[0], t.shape[1], H, HD).transpose(0, 2, 1, 3)

        def _attend(q, k, v):
            sim = jnp.einsum('bhid,bhjd->bhij', q, k) * HD ** (-0.5)
            attn = jax.nn.softmax(sim, axis=-1)
            out = jnp.einsum('bhij,bhjd->bhid', attn, v)
            return out.transpose(0, 2, 1, 3).reshape(out.shape[0], -1, D)
        key = jax.random.key(seed)
        ks = jax.random.split(key, 16)
        s = 0.02
        return {'x': jax.random.normal(ks[0], (B, N, D), jnp.float32), 'c': jax.random.normal(ks[1], (B, D), jnp.float32), 'text_embed': jax.random.normal(ks[2], (B, TL, TD), jnp.float32), 'W_ada': jax.random.normal(ks[3], (D, 6 * D), jnp.float32) * s, 'b_ada': jnp.zeros((6 * D,), jnp.float32), 'W_qkv': jax.random.normal(ks[4], (D, 3 * D), jnp.float32) * s, 'b_qkv': jnp.zeros((3 * D,), jnp.float32), 'W_proj': jax.random.normal(ks[5], (D, D), jnp.float32) * s, 'b_proj': jnp.zeros((D,), jnp.float32), 'W_ctx': jax.random.normal(ks[6], (TD, D), jnp.float32) * s, 'b_ctx': jnp.zeros((D,), jnp.float32), 'W_q': jax.random.normal(ks[7], (D, D), jnp.float32) * s, 'W_k': jax.random.normal(ks[8], (D, D), jnp.float32) * s, 'W_v': jax.random.normal(ks[9], (D, D), jnp.float32) * s, 'W_out': jax.random.normal(ks[10], (D, D), jnp.float32) * s, 'b_out': jnp.zeros((D,), jnp.float32), 'W_fc1': jax.random.normal(ks[11], (D, 4 * D), jnp.float32) * s, 'b_fc1': jnp.zeros((4 * D,), jnp.float32), 'W_fc2': jax.random.normal(ks[12], (4 * D, D), jnp.float32) * s, 'b_fc2': jnp.zeros((D,), jnp.float32)}
    _L1_xcond_all = _L1_xcond_setup()
    _L1_xcond_in = {k: v for k, v in _L1_xcond_all.items() if k in ('W_ada', 'b_ada', 'W_qkv', 'b_qkv', 'W_proj', 'b_proj', 'W_ctx', 'b_ctx', 'W_q', 'W_k', 'W_v', 'W_out', 'b_out', 'W_fc1', 'b_fc1', 'W_fc2', 'b_fc2')}
    del _L1_xcond_all

    def _L2_xcond_setup():
        import jax, jax.numpy as jnp
        import numpy as np
        EPS = 1e-05

        def _ada_ln(x, t, W, b):
            emb = t @ W + b
            scale, shift = jnp.split(emb, 2, axis=-1)
            mu = x.mean(-1, keepdims=True)
            var = ((x - mu) ** 2).mean(-1, keepdims=True)
            xn = (x - mu) * jax.lax.rsqrt(var + EPS)
            return xn * (1.0 + scale) + shift

        def _attn(x, ctx, Wq, Wk, Wv, Wo, bo, heads):
            b, n, _ = x.shape
            j = ctx.shape[1]
            q = (x @ Wq).reshape(b, n, heads, -1)
            k = (ctx @ Wk).reshape(b, j, heads, -1)
            v = (ctx @ Wv).reshape(b, j, heads, -1)
            scale = q.shape[-1] ** (-0.5)
            sim = jnp.einsum('bihd,bjhd->bhij', q, k) * scale
            attn = jax.nn.softmax(sim, axis=-1)
            out = jnp.einsum('bhij,bjhd->bihd', attn, v).reshape(b, n, -1)
            return out @ Wo + bo

        def _ff(x, W1, b1, W2, b2):
            p = x @ W1 + b1
            a, gate = jnp.split(p, 2, axis=-1)
            return a * jax.nn.gelu(gate, approximate=False) @ W2 + b2
        key = jax.random.key(seed)
        ks = jax.random.split(key, 32)
        B, N, D = (4, 256, 128)
        J, CD = (32, 96)
        H, DH = (16, 64)
        INNER = H * DH
        FF = 4 * D
        w = lambda k, shp: jax.random.normal(k, shp, jnp.float32) * 0.02
        inp = {'x': jax.random.normal(ks[0], (B, N, D), jnp.float32), 't': jax.random.normal(ks[1], (B, 1, D), jnp.float32), 'context': jax.random.normal(ks[2], (B, J, CD), jnp.float32), 'n1_w': w(ks[3], (D, 2 * D)), 'n1_b': jnp.zeros((2 * D,), jnp.float32), 'n2_w': w(ks[4], (D, 2 * D)), 'n2_b': jnp.zeros((2 * D,), jnp.float32), 'n3_w': w(ks[5], (D, 2 * D)), 'n3_b': jnp.zeros((2 * D,), jnp.float32), 'q1': w(ks[6], (D, INNER)), 'k1': w(ks[7], (D, INNER)), 'v1': w(ks[8], (D, INNER)), 'o1_w': w(ks[9], (INNER, D)), 'o1_b': jnp.zeros((D,), jnp.float32), 'q2': w(ks[10], (D, INNER)), 'k2': w(ks[11], (CD, INNER)), 'v2': w(ks[12], (CD, INNER)), 'o2_w': w(ks[13], (INNER, D)), 'o2_b': jnp.zeros((D,), jnp.float32), 'ff_w1': w(ks[14], (D, 2 * FF)), 'ff_b1': jnp.zeros((2 * FF,), jnp.float32), 'ff_w2': w(ks[15], (FF, D)), 'ff_b2': jnp.zeros((D,), jnp.float32)}
        return inp
    _L2_xcond_all = _L2_xcond_setup()
    _L2_xcond_in = {k: v for k, v in _L2_xcond_all.items() if k in ('n1_w', 'n1_b', 'n2_w', 'n2_b', 'n3_w', 'n3_b', 'q1', 'k1', 'v1', 'o1_w', 'o1_b', 'q2', 'k2', 'v2', 'o2_w', 'o2_b', 'ff_w1', 'ff_b1', 'ff_w2', 'ff_b2')}
    del _L2_xcond_all

    def _L3_xcond_setup():
        import jax, jax.numpy as jnp
        import numpy as np
        EPS = 1e-06

        def ln(x, eps=EPS):
            m = jnp.mean(x, axis=-1, keepdims=True)
            v = jnp.mean(jnp.square(x - m), axis=-1, keepdims=True)
            return (x - m) * jax.lax.rsqrt(v + eps)

        def modulate(x, shift, scale):
            return x * (1.0 + scale[:, None, :]) + shift[:, None, :]

        def _heads(t, H):
            B, N, D = t.shape
            return t.reshape(B, N, H, D // H).transpose(0, 2, 1, 3)

        def _unheads(t):
            B, H, N, hd = t.shape
            return t.transpose(0, 2, 1, 3).reshape(B, N, H * hd)
        key = jax.random.key(seed)
        B, N, D, H, T, CD = (4, 128, 128, 16, 32, 96)
        FF = 4 * D
        ks = jax.random.split(key, 20)
        s = 0.02
        return {'x': jax.random.normal(ks[0], (B, N, D), jnp.float32), 'c': jax.random.normal(ks[1], (B, D), jnp.float32), 'brain_tokens': jax.random.normal(ks[2], (B, T, CD), jnp.float32), 'adaln_w': jax.random.normal(ks[3], (9 * D, D), jnp.float32) * s, 'adaln_b': jax.random.normal(ks[4], (9 * D,), jnp.float32) * s, 'qn_w': jnp.ones((D // H,), jnp.float32), 'qn_b': jnp.zeros((D // H,), jnp.float32), 'kn_w': jnp.ones((D // H,), jnp.float32), 'kn_b': jnp.zeros((D // H,), jnp.float32), 'ca_in_w': jax.random.normal(ks[5], (3 * D, D), jnp.float32) * s, 'ca_in_b': jax.random.normal(ks[6], (3 * D,), jnp.float32) * s, 'ca_out_w': jax.random.normal(ks[7], (D, D), jnp.float32) * s, 'ca_out_b': jax.random.normal(ks[8], (D,), jnp.float32) * s, 'cond_w': jax.random.normal(ks[9], (D, CD), jnp.float32) * s, 'cond_b': jax.random.normal(ks[10], (D,), jnp.float32) * s, 'w1': jax.random.normal(ks[11], (FF, D), jnp.float32) * s, 'w3': jax.random.normal(ks[12], (FF, D), jnp.float32) * s, 'w2': jax.random.normal(ks[13], (D, FF), jnp.float32) * s}
    _L3_xcond_all = _L3_xcond_setup()
    _L3_xcond_in = {k: v for k, v in _L3_xcond_all.items() if k in ('adaln_w', 'adaln_b', 'qn_w', 'qn_b', 'kn_w', 'kn_b', 'ca_in_w', 'ca_in_b', 'ca_out_w', 'ca_out_b', 'cond_w', 'cond_b', 'w1', 'w3', 'w2')}
    del _L3_xcond_all
    return {'x': x, 'cond_1024': cond_1024, 'ctx_768': ctx_768, 'L0_xcond_ln1_w': _L0_xcond_in['ln1_w'], 'L0_xcond_ln1_b': _L0_xcond_in['ln1_b'], 'L0_xcond_g1_w': _L0_xcond_in['g1_w'], 'L0_xcond_g1_b': _L0_xcond_in['g1_b'], 'L0_xcond_b1_w': _L0_xcond_in['b1_w'], 'L0_xcond_b1_b': _L0_xcond_in['b1_b'], 'L0_xcond_ln2_w': _L0_xcond_in['ln2_w'], 'L0_xcond_ln2_b': _L0_xcond_in['ln2_b'], 'L0_xcond_g2_w': _L0_xcond_in['g2_w'], 'L0_xcond_g2_b': _L0_xcond_in['g2_b'], 'L0_xcond_b2_w': _L0_xcond_in['b2_w'], 'L0_xcond_b2_b': _L0_xcond_in['b2_b'], 'L0_xcond_sa_wq': _L0_xcond_in['sa_wq'], 'L0_xcond_sa_wkv': _L0_xcond_in['sa_wkv'], 'L0_xcond_sa_wo': _L0_xcond_in['sa_wo'], 'L0_xcond_sa_bo': _L0_xcond_in['sa_bo'], 'L0_xcond_ca_lnc_w': _L0_xcond_in['ca_lnc_w'], 'L0_xcond_ca_lnc_b': _L0_xcond_in['ca_lnc_b'], 'L0_xcond_ca_wq': _L0_xcond_in['ca_wq'], 'L0_xcond_ca_wkv': _L0_xcond_in['ca_wkv'], 'L0_xcond_ca_wo': _L0_xcond_in['ca_wo'], 'L0_xcond_ca_bo': _L0_xcond_in['ca_bo'], 'L0_xcond_ff_w1': _L0_xcond_in['ff_w1'], 'L0_xcond_ff_b1': _L0_xcond_in['ff_b1'], 'L0_xcond_ff_w2': _L0_xcond_in['ff_w2'], 'L0_xcond_ff_b2': _L0_xcond_in['ff_b2'], 'L1_xcond_W_ada': _L1_xcond_in['W_ada'], 'L1_xcond_b_ada': _L1_xcond_in['b_ada'], 'L1_xcond_W_qkv': _L1_xcond_in['W_qkv'], 'L1_xcond_b_qkv': _L1_xcond_in['b_qkv'], 'L1_xcond_W_proj': _L1_xcond_in['W_proj'], 'L1_xcond_b_proj': _L1_xcond_in['b_proj'], 'L1_xcond_W_ctx': _L1_xcond_in['W_ctx'], 'L1_xcond_b_ctx': _L1_xcond_in['b_ctx'], 'L1_xcond_W_q': _L1_xcond_in['W_q'], 'L1_xcond_W_k': _L1_xcond_in['W_k'], 'L1_xcond_W_v': _L1_xcond_in['W_v'], 'L1_xcond_W_out': _L1_xcond_in['W_out'], 'L1_xcond_b_out': _L1_xcond_in['b_out'], 'L1_xcond_W_fc1': _L1_xcond_in['W_fc1'], 'L1_xcond_b_fc1': _L1_xcond_in['b_fc1'], 'L1_xcond_W_fc2': _L1_xcond_in['W_fc2'], 'L1_xcond_b_fc2': _L1_xcond_in['b_fc2'], 'L2_xcond_n1_w': _L2_xcond_in['n1_w'], 'L2_xcond_n1_b': _L2_xcond_in['n1_b'], 'L2_xcond_n2_w': _L2_xcond_in['n2_w'], 'L2_xcond_n2_b': _L2_xcond_in['n2_b'], 'L2_xcond_n3_w': _L2_xcond_in['n3_w'], 'L2_xcond_n3_b': _L2_xcond_in['n3_b'], 'L2_xcond_q1': _L2_xcond_in['q1'], 'L2_xcond_k1': _L2_xcond_in['k1'], 'L2_xcond_v1': _L2_xcond_in['v1'], 'L2_xcond_o1_w': _L2_xcond_in['o1_w'], 'L2_xcond_o1_b': _L2_xcond_in['o1_b'], 'L2_xcond_q2': _L2_xcond_in['q2'], 'L2_xcond_k2': _L2_xcond_in['k2'], 'L2_xcond_v2': _L2_xcond_in['v2'], 'L2_xcond_o2_w': _L2_xcond_in['o2_w'], 'L2_xcond_o2_b': _L2_xcond_in['o2_b'], 'L2_xcond_ff_w1': _L2_xcond_in['ff_w1'], 'L2_xcond_ff_b1': _L2_xcond_in['ff_b1'], 'L2_xcond_ff_w2': _L2_xcond_in['ff_w2'], 'L2_xcond_ff_b2': _L2_xcond_in['ff_b2'], 'L3_xcond_adaln_w': _L3_xcond_in['adaln_w'], 'L3_xcond_adaln_b': _L3_xcond_in['adaln_b'], 'L3_xcond_qn_w': _L3_xcond_in['qn_w'], 'L3_xcond_qn_b': _L3_xcond_in['qn_b'], 'L3_xcond_kn_w': _L3_xcond_in['kn_w'], 'L3_xcond_kn_b': _L3_xcond_in['kn_b'], 'L3_xcond_ca_in_w': _L3_xcond_in['ca_in_w'], 'L3_xcond_ca_in_b': _L3_xcond_in['ca_in_b'], 'L3_xcond_ca_out_w': _L3_xcond_in['ca_out_w'], 'L3_xcond_ca_out_b': _L3_xcond_in['ca_out_b'], 'L3_xcond_cond_w': _L3_xcond_in['cond_w'], 'L3_xcond_cond_b': _L3_xcond_in['cond_b'], 'L3_xcond_w1': _L3_xcond_in['w1'], 'L3_xcond_w3': _L3_xcond_in['w3'], 'L3_xcond_w2': _L3_xcond_in['w2']}

def reference(x, cond_1024, ctx_768, L0_xcond_ln1_w, L0_xcond_ln1_b, L0_xcond_g1_w, L0_xcond_g1_b, L0_xcond_b1_w, L0_xcond_b1_b, L0_xcond_ln2_w, L0_xcond_ln2_b, L0_xcond_g2_w, L0_xcond_g2_b, L0_xcond_b2_w, L0_xcond_b2_b, L0_xcond_sa_wq, L0_xcond_sa_wkv, L0_xcond_sa_wo, L0_xcond_sa_bo, L0_xcond_ca_lnc_w, L0_xcond_ca_lnc_b, L0_xcond_ca_wq, L0_xcond_ca_wkv, L0_xcond_ca_wo, L0_xcond_ca_bo, L0_xcond_ff_w1, L0_xcond_ff_b1, L0_xcond_ff_w2, L0_xcond_ff_b2, L1_xcond_W_ada, L1_xcond_b_ada, L1_xcond_W_qkv, L1_xcond_b_qkv, L1_xcond_W_proj, L1_xcond_b_proj, L1_xcond_W_ctx, L1_xcond_b_ctx, L1_xcond_W_q, L1_xcond_W_k, L1_xcond_W_v, L1_xcond_W_out, L1_xcond_b_out, L1_xcond_W_fc1, L1_xcond_b_fc1, L1_xcond_W_fc2, L1_xcond_b_fc2, L2_xcond_n1_w, L2_xcond_n1_b, L2_xcond_n2_w, L2_xcond_n2_b, L2_xcond_n3_w, L2_xcond_n3_b, L2_xcond_q1, L2_xcond_k1, L2_xcond_v1, L2_xcond_o1_w, L2_xcond_o1_b, L2_xcond_q2, L2_xcond_k2, L2_xcond_v2, L2_xcond_o2_w, L2_xcond_o2_b, L2_xcond_ff_w1, L2_xcond_ff_b1, L2_xcond_ff_w2, L2_xcond_ff_b2, L3_xcond_adaln_w, L3_xcond_adaln_b, L3_xcond_qn_w, L3_xcond_qn_b, L3_xcond_kn_w, L3_xcond_kn_b, L3_xcond_ca_in_w, L3_xcond_ca_in_b, L3_xcond_ca_out_w, L3_xcond_ca_out_b, L3_xcond_cond_w, L3_xcond_cond_b, L3_xcond_w1, L3_xcond_w3, L3_xcond_w2):
    import jax
    import jax.numpy as jnp

    def _L0_xcond_ref(x, cond, context, ln1_w, ln1_b, g1_w, g1_b, b1_w, b1_b, ln2_w, ln2_b, g2_w, g2_b, b2_w, b2_b, sa_wq, sa_wkv, sa_wo, sa_bo, ca_lnc_w, ca_lnc_b, ca_wq, ca_wkv, ca_wo, ca_bo, ff_w1, ff_b1, ff_w2, ff_b2):
        import jax, jax.numpy as jnp
        import numpy as np
        B, N, M = (2, 128, 64)
        D, H, DH = (128, 16, 64)
        MID = H * DH
        DC = 96
        MULT = 4
        EPS = 1e-05

        def _ln(x, w, b):
            mu = jnp.mean(x, -1, keepdims=True)
            var = jnp.mean((x - mu) ** 2, -1, keepdims=True)
            return (x - mu) * jax.lax.rsqrt(var + EPS) * w + b

        def _sincos(n, d):
            inv = 1.0 / 10000.0 ** (jnp.arange(0, d, 2, dtype=jnp.float32) / d)
            ang = jnp.arange(n, dtype=jnp.float32)[:, None] * inv[None, :]
            return (jnp.sin(ang), jnp.cos(ang))

        def _rope(x, sin, cos):
            s = sin[None, None]
            c = cos[None, None]
            xe = x[..., ::2]
            xo = x[..., 1::2]
            re = xe * c - xo * s
            ro = xe * s + xo * c
            return jnp.stack((re, ro), axis=-1).reshape(x.shape)

        def _heads(t):
            b, n, _ = t.shape
            return t.reshape(b, n, H, DH).transpose(0, 2, 1, 3)

        def _attn(xq, ctx, wq, wkv, wo, bo):
            q = _heads(xq @ wq)
            k, v = jnp.split(ctx @ wkv, 2, axis=-1)
            k = _heads(k)
            v = _heads(v)
            sq, cq = _sincos(q.shape[2], DH)
            sk, ck = _sincos(k.shape[2], DH)
            q = _rope(q, sq, cq)
            k = _rope(k, sk, ck)
            sim = jnp.einsum('bhnd,bhmd->bhnm', q, k) * DH ** (-0.5)
            a = jax.nn.softmax(sim, axis=-1)
            o = jnp.einsum('bhnm,bhmd->bhnd', a, v)
            o = o.transpose(0, 2, 1, 3).reshape(xq.shape[0], xq.shape[1], MID)
            return o @ wo + bo

        def _adaln(x, c, lw, lb, gw, gb, bw, bb):
            g = (c @ gw + gb)[:, None, :]
            bt = (c @ bw + bb)[:, None, :]
            return _ln(x, lw, lb) * (1.0 + g) + bt
        attn_in = _adaln(x, cond, ln1_w, ln1_b, g1_w, g1_b, b1_w, b1_b)
        x = _attn(attn_in, attn_in, sa_wq, sa_wkv, sa_wo, sa_bo) + x
        cross_in = _adaln(x, cond, ln1_w, ln1_b, g1_w, g1_b, b1_w, b1_b)
        ctx_n = _ln(context, ca_lnc_w, ca_lnc_b)
        x = _attn(cross_in, ctx_n, ca_wq, ca_wkv, ca_wo, ca_bo) + x
        ffn_in = _adaln(x, cond, ln2_w, ln2_b, g2_w, g2_b, b2_w, b2_b)
        h = jax.nn.gelu(ffn_in @ ff_w1 + ff_b1, approximate=False)
        x = h @ ff_w2 + ff_b2 + x
        return x

    def _L1_xcond_ref(x, c, text_embed, W_ada, b_ada, W_qkv, b_qkv, W_proj, b_proj, W_ctx, b_ctx, W_q, W_k, W_v, W_out, b_out, W_fc1, b_fc1, W_fc2, b_fc2):
        import jax, jax.numpy as jnp
        import numpy as np
        B, N, D, H, TD, TL = (4, 128, 128, 16, 96, 77)
        HD = D // H
        EPS = 1e-06

        def _ln(x):
            mu = jnp.mean(x, axis=-1, keepdims=True)
            var = jnp.var(x, axis=-1, keepdims=True)
            return (x - mu) * jax.lax.rsqrt(var + EPS)

        def _modulate(x, shift, scale):
            return x * (1.0 + scale[:, None, :]) + shift[:, None, :]

        def _heads(t):
            return t.reshape(t.shape[0], t.shape[1], H, HD).transpose(0, 2, 1, 3)

        def _attend(q, k, v):
            sim = jnp.einsum('bhid,bhjd->bhij', q, k) * HD ** (-0.5)
            attn = jax.nn.softmax(sim, axis=-1)
            out = jnp.einsum('bhij,bhjd->bhid', attn, v)
            return out.transpose(0, 2, 1, 3).reshape(out.shape[0], -1, D)
        mod = jax.nn.silu(c) @ W_ada + b_ada
        sh_msa, sc_msa, sh_x, sc_x, sh_mlp, sc_mlp = jnp.split(mod, 6, axis=-1)
        h1 = _modulate(_ln(x), sh_msa, sc_msa)
        qkv = h1 @ W_qkv + b_qkv
        q, k, v = jnp.split(qkv, 3, axis=-1)
        out = _attend(_heads(q), _heads(k), _heads(v))
        x = x + (out @ W_proj + b_proj)
        h2 = _modulate(_ln(x), sh_x, sc_x)
        ctx = text_embed @ W_ctx + b_ctx
        q = _heads(h2 @ W_q)
        k = _heads(ctx @ W_k)
        v = _heads(ctx @ W_v)
        out = _attend(q, k, v)
        x = x + (out @ W_out + b_out)
        h3 = _modulate(_ln(x), sh_mlp, sc_mlp)
        hidden = jax.nn.gelu(h3 @ W_fc1 + b_fc1, approximate=True)
        x = x + (hidden @ W_fc2 + b_fc2)
        return x

    def _L2_xcond_ref(x, t, context, n1_w, n1_b, n2_w, n2_b, n3_w, n3_b, q1, k1, v1, o1_w, o1_b, q2, k2, v2, o2_w, o2_b, ff_w1, ff_b1, ff_w2, ff_b2):
        import jax, jax.numpy as jnp
        import numpy as np
        EPS = 1e-05

        def _ada_ln(x, t, W, b):
            emb = t @ W + b
            scale, shift = jnp.split(emb, 2, axis=-1)
            mu = x.mean(-1, keepdims=True)
            var = ((x - mu) ** 2).mean(-1, keepdims=True)
            xn = (x - mu) * jax.lax.rsqrt(var + EPS)
            return xn * (1.0 + scale) + shift

        def _attn(x, ctx, Wq, Wk, Wv, Wo, bo, heads):
            b, n, _ = x.shape
            j = ctx.shape[1]
            q = (x @ Wq).reshape(b, n, heads, -1)
            k = (ctx @ Wk).reshape(b, j, heads, -1)
            v = (ctx @ Wv).reshape(b, j, heads, -1)
            scale = q.shape[-1] ** (-0.5)
            sim = jnp.einsum('bihd,bjhd->bhij', q, k) * scale
            attn = jax.nn.softmax(sim, axis=-1)
            out = jnp.einsum('bhij,bjhd->bihd', attn, v).reshape(b, n, -1)
            return out @ Wo + bo

        def _ff(x, W1, b1, W2, b2):
            p = x @ W1 + b1
            a, gate = jnp.split(p, 2, axis=-1)
            return a * jax.nn.gelu(gate, approximate=False) @ W2 + b2
        H = 16
        h = _ada_ln(x, t, n1_w, n1_b)
        x = _attn(h, h, q1, k1, v1, o1_w, o1_b, H) + x
        h = _ada_ln(x, t, n2_w, n2_b)
        x = _attn(h, context, q2, k2, v2, o2_w, o2_b, H) + x
        h = _ada_ln(x, t, n3_w, n3_b)
        x = _ff(h, ff_w1, ff_b1, ff_w2, ff_b2) + x
        return x

    def _L3_xcond_ref(x, c, brain_tokens, adaln_w, adaln_b, qn_w, qn_b, kn_w, kn_b, ca_in_w, ca_in_b, ca_out_w, ca_out_b, cond_w, cond_b, w1, w3, w2):
        import jax, jax.numpy as jnp
        import numpy as np
        EPS = 1e-06

        def ln(x, eps=EPS):
            m = jnp.mean(x, axis=-1, keepdims=True)
            v = jnp.mean(jnp.square(x - m), axis=-1, keepdims=True)
            return (x - m) * jax.lax.rsqrt(v + eps)

        def modulate(x, shift, scale):
            return x * (1.0 + scale[:, None, :]) + shift[:, None, :]

        def _heads(t, H):
            B, N, D = t.shape
            return t.reshape(B, N, H, D // H).transpose(0, 2, 1, 3)

        def _unheads(t):
            B, H, N, hd = t.shape
            return t.transpose(0, 2, 1, 3).reshape(B, N, H * hd)
        B, N, D = x.shape
        H = 16
        hd = D // H
        scale = hd ** (-0.5)
        mod = jax.nn.silu(c) @ adaln_w.T + adaln_b
        shift_sa, scale_sa, gate_sa, shift_ca, scale_ca, gate_ca, shift_ff, scale_ff, gate_ff = jnp.split(mod, 9, axis=-1)
        h = modulate(ln(x), shift_sa, scale_sa)
        q = ln(_heads(h, H)) * qn_w + qn_b
        k = ln(_heads(h, H)) * kn_w + kn_b
        v = _heads(h, H)
        attn = jax.nn.softmax(jnp.einsum('bhqd,bhkd->bhqk', q, k) * scale, axis=-1)
        h = _unheads(jnp.einsum('bhqk,bhkd->bhqd', attn, v))
        x = x + gate_sa[:, None, :] * h
        h = modulate(ln(x), shift_ca, scale_ca)
        kv = brain_tokens @ cond_w.T + cond_b
        wq, wk, wv = jnp.split(ca_in_w, 3, axis=0)
        bq, bk, bv = jnp.split(ca_in_b, 3, axis=0)
        q = _heads(h @ wq.T + bq, H)
        k = _heads(kv @ wk.T + bk, H)
        v = _heads(kv @ wv.T + bv, H)
        attn = jax.nn.softmax(jnp.einsum('bhqd,bhkd->bhqk', q, k) * scale, axis=-1)
        h = _unheads(jnp.einsum('bhqk,bhkd->bhqd', attn, v)) @ ca_out_w.T + ca_out_b
        x = x + gate_ca[:, None, :] * h
        h = modulate(ln(x), shift_ff, scale_ff)
        h = jax.nn.silu(h @ w1.T) * (h @ w3.T) @ w2.T
        x = x + gate_ff[:, None, :] * h
        return x
    x = _L0_xcond_ref(x, cond_1024, ctx_768, L0_xcond_ln1_w, L0_xcond_ln1_b, L0_xcond_g1_w, L0_xcond_g1_b, L0_xcond_b1_w, L0_xcond_b1_b, L0_xcond_ln2_w, L0_xcond_ln2_b, L0_xcond_g2_w, L0_xcond_g2_b, L0_xcond_b2_w, L0_xcond_b2_b, L0_xcond_sa_wq, L0_xcond_sa_wkv, L0_xcond_sa_wo, L0_xcond_sa_bo, L0_xcond_ca_lnc_w, L0_xcond_ca_lnc_b, L0_xcond_ca_wq, L0_xcond_ca_wkv, L0_xcond_ca_wo, L0_xcond_ca_bo, L0_xcond_ff_w1, L0_xcond_ff_b1, L0_xcond_ff_w2, L0_xcond_ff_b2)
    x = _L1_xcond_ref(x, cond_1024, ctx_768, L1_xcond_W_ada, L1_xcond_b_ada, L1_xcond_W_qkv, L1_xcond_b_qkv, L1_xcond_W_proj, L1_xcond_b_proj, L1_xcond_W_ctx, L1_xcond_b_ctx, L1_xcond_W_q, L1_xcond_W_k, L1_xcond_W_v, L1_xcond_W_out, L1_xcond_b_out, L1_xcond_W_fc1, L1_xcond_b_fc1, L1_xcond_W_fc2, L1_xcond_b_fc2)
    x = _L2_xcond_ref(x, cond_1024[:, None, :], ctx_768, L2_xcond_n1_w, L2_xcond_n1_b, L2_xcond_n2_w, L2_xcond_n2_b, L2_xcond_n3_w, L2_xcond_n3_b, L2_xcond_q1, L2_xcond_k1, L2_xcond_v1, L2_xcond_o1_w, L2_xcond_o1_b, L2_xcond_q2, L2_xcond_k2, L2_xcond_v2, L2_xcond_o2_w, L2_xcond_o2_b, L2_xcond_ff_w1, L2_xcond_ff_b1, L2_xcond_ff_w2, L2_xcond_ff_b2)
    x = _L3_xcond_ref(x, cond_1024, ctx_768, L3_xcond_adaln_w, L3_xcond_adaln_b, L3_xcond_qn_w, L3_xcond_qn_b, L3_xcond_kn_w, L3_xcond_kn_b, L3_xcond_ca_in_w, L3_xcond_ca_in_b, L3_xcond_ca_out_w, L3_xcond_ca_out_b, L3_xcond_cond_w, L3_xcond_cond_b, L3_xcond_w1, L3_xcond_w3, L3_xcond_w2)
    return x

_drawn_inputs = setup_inputs


def setup_inputs(seed=0):
    import zlib

    import numpy as np

    out = dict(_drawn_inputs(seed))
    spreads = {'L0_xcond_ln1_w': (1.0, 0.6),
     'L0_xcond_ln1_b': (0.0, 0.582),
     'L0_xcond_g1_b': (0.0, 0.8),
     'L0_xcond_b1_b': (0.0, 0.522),
     'L0_xcond_ln2_w': (1.0, 0.6),
     'L0_xcond_ln2_b': (0.0, 0.8),
     'L0_xcond_g2_b': (0.0, 0.8),
     'L0_xcond_b2_b': (0.0, 0.8),
     'L0_xcond_sa_bo': (0.0, 0.1),
     'L0_xcond_ca_lnc_w': (1.0, 0.6),
     'L0_xcond_ca_lnc_b': (0.0, 0.638),
     'L0_xcond_ca_bo': (0.0, 0.1),
     'L0_xcond_ff_b1': (0.0, 0.357),
     'L0_xcond_ff_b2': (0.0, 0.1),
     'L1_xcond_b_ada': (0.0, 0.8),
     'L1_xcond_b_qkv': (0.0, 0.343),
     'L1_xcond_b_proj': (0.0, 0.1),
     'L1_xcond_b_ctx': (0.0, 0.8),
     'L1_xcond_b_out': (0.0, 0.565),
     'L1_xcond_b_fc1': (0.0, 1.682),
     'L1_xcond_b_fc2': (0.0, 0.521),
     'L2_xcond_n1_b': (0.0, 2.0),
     'L2_xcond_n2_b': (0.0, 2.0),
     'L2_xcond_n3_b': (0.0, 0.8),
     'L2_xcond_o1_b': (0.0, 0.548),
     'L2_xcond_o2_b': (0.0, 0.541),
     'L2_xcond_ff_b1': (0.0, 0.8),
     'L2_xcond_ff_b2': (0.0, 0.8),
     'L3_xcond_qn_w': (1.0, 0.6),
     'L3_xcond_qn_b': (0.0, 2.0),
     'L3_xcond_kn_w': (1.0, 0.6),
     'L3_xcond_kn_b': (0.0, 2.0)}
    factors = {'L0_xcond_g1_w': 8.0,
     'L0_xcond_g2_w': 4.461,
     'L0_xcond_b2_w': 4.574,
     'L0_xcond_sa_wq': 8.0,
     'L0_xcond_ca_wq': 8.0,
     'L1_xcond_W_ada': 4.368,
     'L1_xcond_W_qkv': 4.21,
     'L1_xcond_W_ctx': 8.0,
     'L1_xcond_W_q': 8.0,
     'L1_xcond_W_k': 8.0,
     'L1_xcond_W_v': 7.842,
     'L1_xcond_W_out': 7.842,
     'L2_xcond_n2_w': 21.88,
     'L2_xcond_n3_w': 8.0,
     'L2_xcond_q1': 28.583,
     'L2_xcond_k1': 27.64,
     'L2_xcond_q2': 8.0,
     'L2_xcond_k2': 8.0,
     'L2_xcond_ff_w1': 3.681,
     'L2_xcond_ff_w2': 3.664,
     'L3_xcond_adaln_b': 5.46,
     'L3_xcond_ca_in_w': 8.0,
     'L3_xcond_ca_in_b': 31.958,
     'L3_xcond_ca_out_w': 8.0,
     'L3_xcond_ca_out_b': 64.0,
     'L3_xcond_cond_w': 8.0,
     'L3_xcond_cond_b': 47.027,
     'L3_xcond_w1': 8.0,
     'L3_xcond_w3': 8.0,
     'L3_xcond_w2': 8.0,
     'L1_xcond_W_fc1': 3.737,
     'L1_xcond_W_fc2': 2.752,
     'L2_xcond_n1_w': 5.473}
    for name, (base, spread) in spreads.items():
        noise = np.random.default_rng([zlib.crc32(name.encode()), seed]).standard_normal(out[name].shape)
        drawn = base * np.exp(spread * noise) if base else spread * noise
        out[name] = jnp.asarray(drawn.astype(out[name].dtype))
    for name, factor in factors.items():
        out[name] = (out[name] * factor).astype(out[name].dtype)
    return out
```

```python
from contextlib import ExitStack

import concourse.bass as bass
from concourse import mybir

F32 = mybir.dt.float32
BF16 = mybir.dt.bfloat16
F16 = mybir.dt.float16
ALU = mybir.AluOpType
ACT = mybir.ActivationFunctionType
AX = mybir.AxisListType

P = 128
B, N, D = 8, 256, 128
M, DC = 1601, 96
H = 16
QT = N // P
CT = -(-M // P)
LAST = M - (CT - 1) * P
MP = CT * P
FF = 4
BANK = 512
EPS0, EPS1 = 1e-5, 1e-6


class Attention:

    def __init__(self, sub, wide, cross, rope=False, src=None, vbias=False):
        self.sub, self.wide, self.cross, self.rope = sub, wide, cross, rope
        self.src, self.vbias = src, vbias
        self.heads = 2 if wide else 4
        self.groups = H // self.heads
        self.keys = M if cross else N
        self.kt = -(-self.keys // P)
        self.scale = float((64 if wide else 8) ** -0.5)
        self.dk = DC if (cross and wide) else D
        self.kc = [(a, min(BANK, self.keys - a)) for a in range(0, self.keys, BANK)]
        jobs = []
        for o in range(1 + len(self.kc)):
            jobs.append(("op", o, 0))
            if rope:
                jobs.append(("op", o, 1))
        self.ops = 1 + len(self.kc)
        per = 4 if wide else self.kt
        self.vjobs = [(t, min(per, self.kt - t)) for t in range(0, self.kt, per)]
        jobs += [("val", v, 0) for v in range(len(self.vjobs))]
        if cross:
            for h in range(self.heads):
                for q in range(QT):
                    jobs += [("max", (h, q), k) for k in range(len(self.kc))]
        else:
            jobs += [("max", (h, None), 0) for h in range(self.heads)]
        self.jobs = jobs
        full = [t for t in range(self.kt) if (t + 1) * P <= self.keys]
        rest = [t for t in range(self.kt) if (t + 1) * P > self.keys]
        if wide:
            banks = [[(h, full[i]), (h, full[i + 1])] for h in range(2) for i in range(0, len(full), 2)]
            self.chunks = [banks[i:i + 2] for i in range(0, len(banks), 2)]
            self.chunks += [[[(0, t), (1, t)]] for t in rest]
        else:
            self.chunks = [[[(0, t), (1, t)], [(2, t), (3, t)]] for t in range(self.kt)]
        c = len(self.chunks) + 1
        self.cuts = [len(jobs) * i // c for i in range(c + 1)]

    def rows(self, t):
        return min(P, self.keys - t * P)

    def slot_uses(self, r):
        return len(self.jobs[r::2])


WIDE = {0: Attention(0, True, False, rope=True), 1: Attention(1, True, True, rope=True),
        6: Attention(6, True, False), 7: Attention(7, True, True)}
NARROW = {3: Attention(3, False, False, vbias=True), 4: Attention(4, False, True, src=0),
          9: Attention(9, False, False), 10: Attention(10, False, True, src=1, vbias=True)}
ATT = {**WIDE, **NARROW}
FFN = {2: 0, 5: 1, 8: 2, 11: 3}
GATED = {2, 3}
SUBS = range(12)
NARROW_AT = {s: i for i, s in enumerate(NARROW)}
WIDE_AT = {s: i for i, s in enumerate(WIDE)}

SQ, SK, SV, SO, SQS, SKS = 0, 256, 384, 512, 640, 896
STAGE = 1024

NQ, NK, NO, NV = 0, 4 * P, 8 * P, 12 * P
NCOLS = 12 * P + 4 * 32

N_MOD = 27
C_MODB = 0
C_LNW = C_MODB + N_MOD
C_LNB = C_LNW + 12
C_CLNW = C_LNB + 12
C_CLNB = C_CLNW + 1
C_SRCB = C_CLNB + 1
C_FFB = C_SRCB + 2
C_QB = C_FFB + 4 * 8
C_KB = C_QB + 16
C_NEGK = C_KB + 16
C_NEGQ = C_NEGK + 1
C_HEAD = C_NEGQ + 1
C_COND = C_HEAD + 4
C_END = C_COND + B

R_OUT = 0
R_VB = 12 * P
R_END = R_VB + 4 * P

K_ID, K_SEL, K_SELP = 0, P, 2 * P
K_END = 2 * P + 4 * P

FF1_AT = [0, 512, 1024, 2048]
FF1_COLS = 3072


class Count:

    def __init__(self, sem, phases, credit=0):
        self.sem, self.credit = sem, credit
        self.base, self.inc, total = {}, {}, 0
        for name, groups, inc in phases:
            self.base[name], self.inc[name] = total, inc
            total += groups * inc
        self.total = total

    def at(self, b, phase, g=(0, 0), c=0):
        it, u = g
        inc = self.inc[phase]
        fixed = self.base[phase] + u * inc + c + self.credit
        if isinstance(it, int):
            return b * self.total + (fixed + it * 2 * inc)
        return b * self.total + it * (2 * inc) + fixed


def build(nc, a):
    with ExitStack() as ctx:
        def sb(name, shape, dt=F32):
            return ctx.enter_context(nc.sbuf_tensor(name, shape, dt))

        def psum(name, shape):
            return ctx.enter_context(nc.psum_tensor(name, shape, F32))

        def sem(name):
            return ctx.enter_context(nc.semaphore(name))

        cols = sb("cols", [P, C_END])
        rows = sb("rows", [1, R_END])
        squares = sb("squares", [P, K_END])
        ident = squares[:, K_ID:K_ID + P]
        sum_row = squares[:, K_SEL:K_SEL + P]
        head_dims = squares[:, K_SELP:K_SELP + 4 * P].rearrange("p (g d) -> p g d", g=4)
        ones = sb("ones", [P, P])
        ones_bf = sb("ones_bf", [P, P], BF16)
        ident_bf = sb("ident_bf", [P, P], BF16)
        minus_half = sb("minus_half", [P, 32])
        eps0 = sb("eps0", [P, CT])
        eps1 = sb("eps1", [P, 32])
        rope_cos = sb("rope_cos", [P, M])
        rope_sin = sb("rope_sin", [P, M])
        narrow_w = sb("narrow_w", [P, 4, NCOLS])
        src_w = sb("src_w", [DC, 2, P])
        ff1_w = sb("ff1_w", [P, FF1_COLS])
        ff2_w = sb("ff2_w", [P, 4, FF, P])
        mod_ab = sb("mod_ab", [P, B, N_MOD])
        x_in = sb("x_in", [P, QT, D])
        ctx_in = sb("ctx_in", [P, CT, DC])
        x = sb("x", [P, QT, D])
        x_out = sb("x_out", [P, QT, D])
        ab = sb("ab", [P, N_MOD])
        ctx_t = sb("ctx_t", [DC, MP])
        ctx_norm_t = sb("ctx_norm_t", [DC, MP])
        src_t = sb("src_t", [P, MP])
        ctx_stats = sb("ctx_stats", [P, CT, 6])
        ctx_mv = sb("ctx_mv", [P, CT, 2])
        ctx_var = sb("ctx_var", [P, CT])
        ctx_rstd = sb("ctx_rstd", [P, CT])
        stats = sb("stats", [P, QT, 6])
        mv = sb("mv", [P, QT, 2])
        var = sb("var", [P, QT])
        rstd = sb("rstd", [P, QT])
        xn = sb("xn", [P, QT, D])
        h_t = sb("h_t", [D, N])
        gated_wo = sb("gated_wo", [P, 2, 4, P])
        gated_w2 = sb("gated_w2", [P, FF, P])
        gated_bo = sb("gated_bo", [1, P])
        hn_sum = sb("hn_sum", [P, 32])
        hn_var = sb("hn_var", [P, 32])
        hn_rstd = sb("hn_rstd", [P, 32])
        n_t = sb("n_t", [D, N])
        stage = sb("stage", [P, 2, STAGE])
        kop = sb("kop", [P, 2, 2, MP], F16)
        qop = sb("qop", [P, 2, 4, N], F16)
        qsplit = sb("qsplit", [P, N], F16)
        wide_v = sb("wide_v", [P, 2, CT, 4, 64])
        narrow_v = sb("narrow_v", [P, 2, CT, 4, 32])
        raw = sb("raw", [P, 2, BANK])
        raw_swap = sb("raw_swap", [P, BANK])
        max_part = sb("max_part", [P, 2, 8, 4])
        max_neg = sb("max_neg", [P, 2, 8])
        shift = sb("shift", [P, 2, 4, N], BF16)
        probs = sb("probs", [P, 2, 2 * BANK])
        o_raw = sb("o_raw", [P, N])
        o_inv = sb("o_inv", [P, N])
        attn = sb("attn", [P, 2, N])
        ff_h = sb("ff_h", [P, FF, N])
        ff_g = sb("ff_g", [P, FF, N])

        ctx_norm = probs[:, :, :].rearrange("p s k -> p (s k)")[:, 0:CT * DC].rearrange("p (t d) -> p t d", d=DC)
        high = raw_swap[:, :].bitcast(F16).rearrange("p (s k) -> p s k", s=2)
        ff_h_flat = ff_h[:, :, :].rearrange("p f n -> p (f n)")
        ff_g_flat = ff_g[:, :, :].rearrange("p f n -> p (f n)")
        gate_diag = ff_g_flat[:, 0:3 * P].rearrange("p (a d) -> p a d", a=3)
        gate_rows = ff_h_flat[:, 0:3 * P].rearrange("p (a d) -> p a d", a=3)
        hn = ff_h_flat[:, 0:N].rearrange("p (h d) -> p h d", d=8)
        hn_cen = ff_g_flat[:, 0:N].rearrange("p (h d) -> p h d", d=8)
        hn_sq = ff_g_flat[:, N:2 * N].rearrange("p (h d) -> p h d", d=8)

        scores = psum("scores", [P, 2, 2 * BANK])
        ring = psum("ring", [P, 2, BANK])
        o_acc = psum("o_acc", [P, BANK])
        y_acc = psum("y_acc", [P, BANK])

        mod_w = wide_v[:, :, :, :, :].rearrange("p u t f c -> p (u t f c)")[:, 0:N_MOD * P]
        cond_silu = o_raw[:, 0:B]
        mod_raw = ff_h_flat[:, 0:N_MOD * B].rearrange("p (m b) -> p m b", b=B)
        mod_scale = ff_g_flat[:, 0:12 * B].rearrange("p (m b) -> p m b", b=B)

        ring_phases = {"prep": (1, 8), "gate": (1, 1)}

        def phases(of):
            order = ["prep", "gate"]
            for s in SUBS:
                order += [("ln", s)]
                if s == 9:
                    order += ["headnorm"]
                if s in ATT and ATT[s].src is not None:
                    order += [("src", s)]
                order += [("att", s) if s in ATT else ("ff", s)]
            return [(p, *of(p)) for p in order if of(p)]

        def ring_jobs(r):
            def of(p):
                if p == "prep":
                    return 1, 4
                if p == "gate":
                    return (1, 1) if r == 1 else None
                if p == "headnorm":
                    return 1, 1
                kind, s = p
                if kind == "ln":
                    return (1, 1) if r == 0 else None
                if kind == "src":
                    return 1, 2
                if kind == "ff":
                    return 1, (1 if FFN[s] < 2 else 2)
                return ATT[s].groups, ATT[s].slot_uses(r)
            return of

        def all_ring_jobs(p):
            n = [ring_jobs(r)(p) for r in range(2)]
            n = [x for x in n if x]
            return n[0][0], sum(x[1] for x in n)

        def attentions(per):
            def of(p):
                if isinstance(p, tuple) and p[0] == "att" and per(ATT[p[1]]):
                    return ATT[p[1]].groups, per(ATT[p[1]])
            return of

        def only(kind, n=1):
            def of(p):
                if p == kind or (isinstance(p, tuple) and p[0] == kind):
                    return 1, n
            return of

        def count(name, of, credit=0):
            return Count(sem(name), phases(of), credit)

        job_full = count("job_full", all_ring_jobs)
        slot_free = [count(f"slot_free{r}", ring_jobs(r), 1) for r in range(2)]
        op_ready = count("op_ready", attentions(lambda t: t.ops), 1)
        rope_sum = count("rope_sum", attentions(lambda t: t.ops if t.rope else 0))
        rope_high = count("rope_high", attentions(lambda t: t.ops if t.rope else 0))
        q_split = count("q_split", attentions(lambda t: 0 if t.wide else 1))
        max_ready = count("max_ready", attentions(lambda t: 1))
        shift_ready = count("shift_ready", attentions(lambda t: 1))
        scores_full = count("scores_full", attentions(lambda t: len(t.chunks)))
        exp_done = count("exp_done", attentions(lambda t: len(t.chunks)), 2)
        av_done = count("av_done", attentions(lambda t: len(t.chunks)), 2)
        o_copied = count("o_copied", attentions(lambda t: 0 if t.wide else 1))
        sums_spread = count("sums_spread", attentions(lambda t: 0 if t.wide else 1))
        inv_ready = count("inv_ready", attentions(lambda t: 1))
        attn_ready = count("attn_ready", attentions(lambda t: 1), 1)
        wide_projected = count("wide_projected", attentions(lambda t: 1 if t.wide else 0), 2)
        narrow_projected = count("narrow_projected", attentions(lambda t: 0 if t.wide else 1))
        stage_in = [count(f"stage_in{u}", attentions(lambda t: 8 if t.wide else 0)) for u in range(2)]
        x_in_done = count("x_in_done", only("prep", 16))
        ctx_in_done = count("ctx_in_done", only("prep", 32))
        x_done = Count(sem("x_done"), [("x", 1, 12)])
        x_out_ready = Count(sem("x_out_ready"), [("x", 1, 1)], 1)
        x_out_sent = Count(sem("x_out_sent"), [("x", 1, 16)])
        x_out_free = Count(sem("x_out_free"), [("x", 1, 1)], 1)
        ab_ready = count("ab_ready", only("prep"))
        ctx_stat = count("ctx_stat", only("prep"))
        ctx_mv_ready = count("ctx_mv_ready", only("prep"))
        ctx_var_ready = count("ctx_var_ready", only("prep"))
        ctx_rstd_ready = count("ctx_rstd_ready", only("prep"))
        ctx_norm_ready = count("ctx_norm_ready", only("prep"))
        stat = count("stat", only("ln"))
        mv_ready = count("mv_ready", only("ln"))
        var_ready = count("var_ready", only("ln"))
        rstd_ready = count("rstd_ready", only("ln"))
        xn_ready = count("xn_ready", only("ln"))
        ff_done = count("ff_done", only("ff"))
        diag_ready = count("diag_ready", only("gate"))
        gated_ready = count("gated_ready", only("gate"))
        hn_step = count("hn_step", only("headnorm", 5))
        hn_rstd_ready = count("hn_rstd_ready", only("headnorm", 2))
        const_in = sem("const_in")
        init_done = sem("init_done")
        cond_ready = sem("cond_ready")
        mod_full = sem("mod_full")
        mod_step = sem("mod_step")
        waited_sp, waited_dve = sem("waited_sp"), sem("waited_dve")
        N_CONST = 9

        block = ctx.enter_context(nc.Block())

        def groups(eng, t, first, pair):
            first((0, 0))
            if t.groups > 4:
                with eng.Fori(0, t.groups // 2 - 1) as it:
                    pair((it, 0), (it, 1))
                    pair((it, 1), (it + 1, 0))
            else:
                for it in range(t.groups // 2 - 1):
                    pair((it, 0), (it, 1))
                    pair((it, 1), (it + 1, 0))
            last = t.groups // 2 - 1
            pair((last, 0), (last, 1))
            pair((last, 1), None)

        def src_of(t):
            if not t.cross:
                return n_t if t.sub == 9 else h_t
            if t.src is not None:
                return src_t
            return ctx_norm_t if t.sub == 1 else ctx_t

        @block.sync
        def _(sp):
            for dst, name in ((cols[:, :], "cols"), (rows[:, :], "rows"), (squares[:, :], "squares"),
                              (mod_w, "mod_w"), (rope_cos[:, :], "rope_cos"), (rope_sin[:, :], "rope_sin"),
                              (narrow_w[:, :, :].rearrange("p a c -> p (a c)"), "narrow_w"),
                              (src_w[:, :, :].rearrange("p a c -> p (a c)"), "src_w"),
                              (ff1_w[:, :], "ff1_w")):
                sp.dma_start(dst, a[name]).then_inc(const_in, 16)
            sp.dma_start(ff2_w[:, :, :, :].rearrange("p l f d -> p (l f d)"), a["ff2_w"]).then_inc(const_in, 16)

            def load(b):
                sp.dma_start(x_in[:, :, :], a["x"][b, :, :].rearrange("(t p) d -> p t d", p=P))\
                    .then_inc(x_in_done.sem, 16)
                full = (CT - 1) * P
                sp.dma_start(ctx_in[:, 0:CT - 1, :], a["ctx"][b, 0:full, :].rearrange("(t p) d -> p t d", p=P))\
                    .then_inc(ctx_in_done.sem, 16)
                sp.dma_start(ctx_in[0:LAST, CT - 1, :], a["ctx"][b, full:M, :]).then_inc(ctx_in_done.sem, 16)

            def weights(b, t):
                w = STAGE if t.rope else SQS
                blob = a[f"wide{t.sub}"]

                def one(g):
                    sp.wait_ge(wide_projected.sem, wide_projected.at(b, ("att", t.sub), g, -1))
                    sp.sem_inc(waited_sp, 1)
                    sp.dma_start(stage[:, g[1], 0:w], blob[g[0] * 2 + g[1], :, :]).then_inc(stage_in[g[1]].sem, 16)

                with sp.Fori(0, t.groups // 2) as it:
                    one((it, 0))
                    one((it, 1))

            def sample(b, more):
                for s in WIDE:
                    weights(b, WIDE[s])
                if more:
                    sp.wait_ge(job_full.sem, job_full.at(b, "prep", c=8))
                    sp.sem_inc(waited_sp, 1)
                    load(b + 1)
                sp.wait_ge(x_out_ready.sem, x_out_ready.at(b, "x", c=1))
                sp.sem_inc(waited_sp, 1)
                sp.dma_start(a["out"][b, :, :].rearrange("(t p) d -> p t d", p=P), x_out[:, :, :])\
                    .then_inc(x_out_sent.sem, 16)
                sp.wait_ge(x_out_sent.sem, x_out_sent.at(b, "x", c=16))
                sp.sem_inc(x_out_free.sem, 1)

            sp.sem_inc(x_out_free.sem, 1)
            load(0)
            with sp.Fori(0, B - 1) as b:
                sample(b, True)
            sample(B - 1, False)

        @block.gpsimd
        def _(pool):
            pool.memset(ones[:, :], 1.0)
            pool.memset(ones_bf[:, :], 1.0)
            pool.memset(minus_half[:, :], -0.5)
            pool.memset(eps0[:, :], EPS0)
            pool.memset(eps1[:, :], EPS1)
            pool.memset(ctx_mv[:, :, :], 1.0)
            pool.memset(narrow_v[:, :, :, :, :], 1.0).then_inc(init_done, 2)
            pool.wait_ge(init_done, 2)
            with pool.Fori(0, B) as b:
                pool.wait_ge(ctx_mv_ready.sem, ctx_mv_ready.at(b, "prep", c=1))
                pool.tensor_tensor(ctx_var[:, :], ctx_mv[:, :, 1], eps0[:, 0:CT], ALU.add).then_inc(ctx_var_ready.sem, 1)
                pool.wait_ge(ctx_var_ready.sem, ctx_var_ready.at(b, "prep", c=1))
                pool.tensor_tensor(ctx_rstd[:, :], ctx_var[:, :], minus_half[:, 0:CT], ALU.pow)\
                    .then_inc(ctx_rstd_ready.sem, 1)
                for s in SUBS:
                    eps = eps0 if s // 3 in (0, 2) else eps1
                    pool.wait_ge(mv_ready.sem, mv_ready.at(b, ("ln", s), c=1))
                    pool.tensor_tensor(var[:, :], mv[:, :, 1], eps[:, 0:QT], ALU.add).then_inc(var_ready.sem, 1)
                    pool.wait_ge(var_ready.sem, var_ready.at(b, ("ln", s), c=1))
                    pool.tensor_tensor(rstd[:, :], var[:, :], minus_half[:, 0:QT], ALU.pow).then_inc(rstd_ready.sem, 1)
                    if s == 9:
                        pool.wait_ge(hn_step.sem, hn_step.at(b, "headnorm", c=4))
                        pool.tensor_tensor(hn_var[:, :], hn_var[:, :], eps1[:, :], ALU.add)\
                            .then_inc(hn_rstd_ready.sem, 1)
                        pool.wait_ge(hn_rstd_ready.sem, hn_rstd_ready.at(b, "headnorm", c=1))
                        pool.tensor_tensor(hn_rstd[:, :], hn_var[:, :], minus_half[:, 0:32], ALU.pow)\
                            .then_inc(hn_rstd_ready.sem, 1)

        @block.tensor
        def _(pe):
            def mm(out, lhs, rhs, start, stop):
                return pe.matmul(out, lhs, rhs, start=start, stop=stop, skip_group_check=True)

            pe.sem_inc(av_done.sem, 2)
            pe.sem_inc(wide_projected.sem, 2)
            pe.wait_ge(const_in, 16 * (N_CONST + 1))
            pe.wait_ge(cond_ready, 1)
            for m in range(N_MOD):
                silu = 6 <= m < 12 or m >= 18
                last = mm(scores[:, 0, m * B:(m + 1) * B], mod_w[:, m * P:(m + 1) * P],
                          cond_silu if silu else cols[:, C_COND:C_COND + B], True, True)
            last.then_inc(mod_full, 1)
            pe.wait_ge(init_done, 3)

            def take_slot(b, phase, j, g=(0, 0), r=None):
                r = j % 2 if r is None else r
                pe.wait_ge(slot_free[r].sem, slot_free[r].at(b, phase, g, j // 2))
                return ring[:, r, :]

            def stored(b, phase, j, g=(0, 0), r=None):
                r = j % 2 if r is None else r
                pe.wait_ge(slot_free[r].sem, slot_free[r].at(b, phase, g, j // 2 + 1))

            def prep(b):
                pe.wait_ge(ctx_in_done.sem, ctx_in_done.at(b, "prep", c=32))
                for j in range(8):
                    if j == 4:
                        pe.wait_ge(ctx_norm_ready.sem, ctx_norm_ready.at(b, "prep", c=1))
                    src = ctx_in if j < 4 else ctx_norm
                    out = take_slot(b, "prep", j)
                    for i, t in enumerate(range(4 * (j % 4), min(4 * (j % 4) + 4, CT))):
                        n = P if t < CT - 1 else LAST
                        last = pe.transpose(out[0:DC, i * P:i * P + n], src[0:n, t, :], ident[0:n, 0:n])
                    last.then_inc(job_full.sem, 1)
                for j in (6, 7):
                    stored(b, "prep", j)

            def gate(b):
                pe.wait_ge(diag_ready.sem, diag_ready.at(b, "gate", c=1))
                out = take_slot(b, "gate", 0, r=1)
                mm(out[:, 0:3 * P], ones[:, :], gate_diag[:, :, :].rearrange("p a d -> p (a d)"), True, True)\
                    .then_inc(job_full.sem, 1)

            def layernorm(b, s):
                pe.wait_ge(xn_ready.sem, xn_ready.at(b, ("ln", s), c=1))
                out = take_slot(b, ("ln", s), 0)
                for q in range(QT):
                    last = pe.transpose(out[:, q * P:(q + 1) * P], xn[:, q, :], ident)
                last.then_inc(job_full.sem, 1)
                stored(b, ("ln", s), 0)

            def headnorm(b):
                out = take_slot(b, "headnorm", 0, r=1)
                for q in range(QT):
                    last = pe.transpose(out[:, q * P:(q + 1) * P], h_t[:, q * P:(q + 1) * P], ident)
                last.then_inc(job_full.sem, 1)
                pe.wait_ge(hn_step.sem, hn_step.at(b, "headnorm", c=5))
                out = take_slot(b, "headnorm", 0)
                flat = hn[:, :, :].rearrange("p (t h) d -> p t (h d)", t=QT)
                for q in range(QT):
                    last = pe.transpose(out[:, q * P:(q + 1) * P], flat[:, q, :], ident)
                last.then_inc(job_full.sem, 1)
                stored(b, "headnorm", 0)

            def source(b, s):
                for j, (k, w) in enumerate(ATT[s].kc):
                    out = take_slot(b, ("src", s), j)
                    mm(out[:, 0:w], src_w[:, ATT[s].src, :], ctx_t[:, k:k + w], True, True).then_inc(job_full.sem, 1)
                for j in (2, 3):
                    stored(b, ("src", s), j)

            def init_y(s, bias):
                for q in range(QT):
                    mm(y_acc[:, q * P:(q + 1) * P], ones[0:1, :], bias, q == 0, False)

            def attention(b, t):
                ph = ("att", t.sub)
                C = len(t.chunks)
                src = src_of(t)
                qsrc = n_t if t.sub == 9 else h_t
                vsrc = h_t if t.sub == 9 else src
                if t.sub >= 9:
                    pe.wait_ge(gated_ready.sem, gated_ready.at(b, "gate", c=1))
                init_y(t.sub, gated_bo[:, :] if t.sub == 10 else rows[:, R_OUT + t.sub * P:R_OUT + (t.sub + 1) * P])

                def weight(g, col, n):
                    if t.wide:
                        return stage[0:n, g[1], col:col + P]
                    i = 2 * g[0] + g[1]
                    base = {SQ: NQ, SK: NK}[col] + i * P
                    return narrow_w[0:n, NARROW_AT[t.sub], base:base + P]

                def job(g, j):
                    kind, i, k = t.jobs[j]
                    u = g[1]
                    out = take_slot(b, ph, j, g)
                    if kind == "op" and i == 0:
                        if t.wide:
                            for h in range(2):
                                last = mm(out[:, h * N:(h + 1) * N], weight(g, (SQS if k else SQ) + h * P, D),
                                          qsrc[:, :], True, True)
                        else:
                            last = mm(out[:, 0:N], weight(g, SQ, D), qsrc[:, :], True, True)
                    elif kind == "op":
                        a0, w = t.kc[i - 1]
                        last = mm(out[:, 0:w], weight(g, SKS if k else SK, t.dk), src[0:t.dk, a0:a0 + w], True, True)
                    elif kind == "val" and t.wide:
                        t0, nt = t.vjobs[i]
                        for m in range(nt):
                            n = t.rows(t0 + m)
                            last = mm(out[0:n, m * P:(m + 1) * P], src[0:t.dk, (t0 + m) * P:(t0 + m) * P + n],
                                      stage[0:t.dk, u, SV:SV + P], True, True)
                    elif kind == "val":
                        gi = 2 * g[0] + g[1]
                        wv = narrow_w[:, NARROW_AT[t.sub], NV + gi * 32:NV + gi * 32 + 32]
                        if t.vbias:
                            c0 = R_VB + NARROW_AT[t.sub] * P + gi * 32
                            bias = rows[:, c0:c0 + 32].unsqueeze(1).broadcast_to([1, t.kt, 32])
                            mm(out[:, 0:t.kt * 32], ones[0:1, :], bias, True, False)
                        for m in range(t.kt):
                            n = t.rows(m)
                            last = mm(out[0:n, m * 32:(m + 1) * 32], vsrc[:, m * P:m * P + n], wv,
                                      not t.vbias, m == t.kt - 1)
                    else:
                        h, q = i
                        kh = h if t.wide else 0
                        if j == 0 or t.jobs[j - 1][0] != "max":
                            pe.wait_ge(op_ready.sem, op_ready.at(b, ph, g, t.ops))
                        a0, w = t.kc[k]
                        for m, qq in enumerate(range(QT) if q is None else [q]):
                            last = mm(out[:, m * w:(m + 1) * w], qop[:, u, h, qq * P:(qq + 1) * P],
                                      kop[:, u, kh, a0:a0 + w], True, True)
                    last.then_inc(job_full.sem, 1)

                def jobs(g, c):
                    if g is not None:
                        for j in range(t.cuts[c], t.cuts[c + 1]):
                            job(g, j)

                def make_scores(g, c):
                    u = g[1]
                    if c == 0:
                        pe.wait_ge(shift_ready.sem, shift_ready.at(b, ph, g, 1))
                    pe.wait_ge(exp_done.sem, exp_done.at(b, ph, g, c - 1))
                    for i, bank in enumerate(t.chunks[c]):
                        (h0, k0), (h1, k1) = bank
                        n = t.rows(k0)
                        out = scores[0:n, slot(g, c), i * BANK:(i + 1) * BANK]
                        if h0 == h1:
                            rhs = shift[:, u, h0, :].unsqueeze(1).broadcast_to([P, 2, N])
                        else:
                            rhs = shift[:, u, h0:h0 + 2, :]
                        mm(out, ones_bf[:, 0:n], rhs, True, False)
                        if t.wide:
                            for m, (h, k) in enumerate(bank):
                                for part in range(2):
                                    last = mm(out[:, m * N:(m + 1) * N], kop[:, u, h, k * P:k * P + n],
                                              qop[:, u, 2 * part + h, :], False, part == 1)
                        else:
                            last = mm(out, kop[:, u, 0, k0 * P:k0 * P + n], qop[:, u, h0:h0 + 2, :], False, True)
                    last.then_inc(scores_full.sem, 1)

                def slot(g, c):
                    return chunk_slot(t, g, c)

                def weigh_values(g, c):
                    u = g[1]
                    if c == 0:
                        stored(b, ph, max(j for j, one in enumerate(t.jobs) if one[0] == "val"), g)
                        pe.wait_ge(attn_ready.sem, attn_ready.at(b, ph, g, 0))
                    pe.wait_ge(exp_done.sem, exp_done.at(b, ph, g, c + 1))
                    for i, bank in enumerate(t.chunks[c]):
                        for m, (h, k) in enumerate(bank):
                            n = t.rows(k)
                            w = probs[0:n, slot(g, c), (2 * i + m) * N:(2 * i + m + 1) * N]
                            if t.wide:
                                vals = wide_v[0:n, u, k, 2 * h:2 * h + 2, :].rearrange("p f c -> p (f c)")
                                last = mm(o_acc[:, h * N:(h + 1) * N], vals, w, h == 0 and k == 0, k == t.kt - 1)
                            else:
                                last = mm(o_acc[h * 32:(h + 1) * 32, 0:N], narrow_v[0:n, u, k, h, :], w,
                                          k == 0, k == t.kt - 1)
                    last.then_inc(av_done.sem, 1)

                def project(g):
                    u = g[1]
                    if not t.wide:
                        pe.wait_ge(o_copied.sem, o_copied.at(b, ph, g, 1))
                        mm(o_acc[:, N:2 * N], sum_row, o_raw[:, :], True, True).then_inc(sums_spread.sem, 1)
                        gi = 2 * g[0] + g[1]
                        wo = narrow_w[:, NARROW_AT[t.sub], NO + gi * P:NO + (gi + 1) * P]
                        if t.sub >= 9:
                            wo = gated_wo[:, t.sub - 9, gi, :]
                    else:
                        wo = stage[:, u, SO:SO + P]
                    pe.wait_ge(attn_ready.sem, attn_ready.at(b, ph, g, 1))
                    for q in range(QT):
                        last = mm(y_acc[:, q * P:(q + 1) * P], attn[:, u, q * P:(q + 1) * P], wo, False, False)
                    last.then_inc((wide_projected if t.wide else narrow_projected).sem, 1)

                def stage_wait(g):
                    if t.wide:
                        pe.wait_ge(stage_in[g[1]].sem, stage_in[g[1]].at(b, ph, (g[0], 0), 16))

                def first(g):
                    stage_wait(g)
                    for j in range(len(t.jobs)):
                        job(g, j)

                def pair(g, nxt):
                    if nxt is not None:
                        stage_wait(nxt)
                    for c in range(C):
                        make_scores(g, c)
                        jobs(nxt, c)
                        if c >= 1:
                            weigh_values(g, c - 1)
                    weigh_values(g, C - 1)
                    jobs(nxt, C)
                    project(g)

                groups(pe, t, first, pair)

            def feed_forward(b, s):
                l = FFN[s]
                ph = ("ff", s)
                bias = rows[:, R_OUT + s * P:R_OUT + (s + 1) * P]
                init_y(s, bias)
                w1 = ff1_w[:, FF1_AT[l]:FF1_AT[l] + (512 if l < 2 else 1024)].rearrange("p (c d) -> p c d", d=P)
                for j in range(2 if l < 2 else 4):
                    out = take_slot(b, ph, j)
                    c0 = 2 * j if l < 2 else 2 * (j // 2) + FF * (j % 2)
                    for m in range(2):
                        last = mm(out[:, m * N:(m + 1) * N], w1[:, c0 + m, :], h_t[:, :], True, True)
                    last.then_inc(job_full.sem, 1)
                if l == 3:
                    pe.wait_ge(gated_ready.sem, gated_ready.at(b, "gate", c=1))
                for c in range(FF):
                    if c % 2 == 0:
                        stored(b, ph, c // 2 if l < 2 else c + 1)
                    w2 = gated_w2[:, c, :] if l == 3 else ff2_w[:, l, c, :]
                    for q in range(QT):
                        last = mm(y_acc[:, q * P:(q + 1) * P], ff_h[:, c, q * P:(q + 1) * P], w2, False, c == FF - 1)
                last.then_inc(ff_done.sem, 1)

            with pe.Fori(0, B) as b:
                prep(b)
                gate(b)
                for s in SUBS:
                    layernorm(b, s)
                    if s == 9:
                        headnorm(b)
                    if s in ATT:
                        if ATT[s].src is not None:
                            source(b, s)
                        attention(b, ATT[s])
                    else:
                        feed_forward(b, s)

        @block.scalar
        def _(act):
            act.sem_inc(exp_done.sem, 2)
            act.wait_ge(const_in, 16 * (N_CONST + 1))
            act.activation(cond_silu, cols[:, C_COND:C_COND + B], ACT.Silu).then_inc(cond_ready, 1)

            def copy(out, src, **kw):
                return act.activation(out, src, ACT.Identity, **kw)

            def prep(b):
                for j in range(8):
                    act.wait_ge(job_full.sem, job_full.at(b, "prep", c=j + 1))
                    dst = (ctx_t if j < 4 else ctx_norm_t)
                    a0 = (j % 4) * BANK
                    w = min(BANK, M - a0)
                    src = ring[0:DC, j % 2, 0:w]
                    if j < 4:
                        last = copy(dst[:, a0:a0 + w], src)
                    else:
                        last = copy(dst[:, a0:a0 + w], src, scale=cols[0:DC, C_CLNW:C_CLNW + 1],
                                    bias=cols[0:DC, C_CLNB:C_CLNB + 1])
                    last.then_inc(slot_free[j % 2].sem, 1)

            def source(b, s):
                t = ATT[s]
                for j, (k, w) in enumerate(t.kc):
                    act.wait_ge(job_full.sem, job_full.at(b, ("src", s), c=j + 1))
                    copy(src_t[:, k:k + w], ring[:, j % 2, 0:w], bias=cols[:, C_SRCB + t.src:C_SRCB + t.src + 1])\
                        .then_inc(slot_free[j % 2].sem, 1)

            def attention(b, t):
                ph = ("att", t.sub)
                C = len(t.chunks)

                def job(g, j):
                    kind, i, k = t.jobs[j]
                    u, r = g[1], j % 2
                    if kind == "max" or (kind == "op" and t.rope):
                        return
                    act.wait_ge(job_full.sem, job_full.at(b, ph, g, j + 1))
                    if kind == "op":
                        if i == 0:
                            act.wait_ge(op_ready.sem, op_ready.at(b, ph, g, 0))
                        if i >= 2:
                            act.wait_ge(op_ready.sem, op_ready.at(b, ph, g, i - 1))
                        a0, w = (0, 2 * N if t.wide else N) if i == 0 else t.kc[i - 1]
                        out = ring[:, r, 0:w]
                        if t.wide:
                            copy(raw[:, i % 2, 0:w], out)
                            if i == 0:
                                last = copy(qop[:, u, 0:2, :].rearrange("p h n -> p (h n)"), out)
                            else:
                                copy(kop[0:64, u, 0, a0:a0 + w], out[0:64, :])
                                last = copy(kop[64:128, u, 1, a0:a0 + w], out[64:128, :])
                        else:
                            col = (C_QB if i == 0 else C_KB) + NARROW_AT[t.sub] * 4 + 2 * g[0] + g[1]
                            copy(raw[:, i % 2, 0:w], out, bias=cols[:, col:col + 1])
                            last = copy(high[:, i % 2, 0:w], out, bias=cols[:, col:col + 1])
                        last.then_inc(slot_free[r].sem, 1)
                    else:
                        t0, nt = t.vjobs[i]
                        whole = sum(t.rows(t0 + m) == P for m in range(nt))
                        for m0, m1, n in ((0, whole, P), (whole, nt, t.rows(t0 + nt - 1))):
                            if m1 == m0:
                                continue
                            if t.wide:
                                src = ring[0:n, r, m0 * P:m1 * P].rearrange("p (m h c) -> p m h c", h=2, c=64)
                                dst = wide_v[0:n, u, t0 + m0:t0 + m1, 0:4:3, :]
                            else:
                                src = ring[0:n, r, m0 * 32:m1 * 32].rearrange("p (m h c) -> p m h c", h=4, c=8)
                                dst = narrow_v[0:n, u, m0:m1, :, 0:8]
                            last = copy(dst, src)
                        last.then_inc(slot_free[r].sem, 1)

                def jobs(g, c):
                    if g is not None:
                        for j in range(t.cuts[c], t.cuts[c + 1]):
                            job(g, j)

                def exps(g, c):
                    act.wait_ge(scores_full.sem, scores_full.at(b, ph, g, c + 1))
                    act.wait_ge(av_done.sem, av_done.at(b, ph, g, c - 1))
                    n = t.rows(t.chunks[c][0][0][1])
                    w = len(t.chunks[c]) * BANK
                    s = chunk_slot(t, g, c)
                    act.activation(probs[0:n, s, 0:w], scores[0:n, s, 0:w], ACT.Exp, scale=t.scale)\
                        .then_inc(exp_done.sem, 1)

                def first(g):
                    for j in range(len(t.jobs)):
                        job(g, j)

                def pair(g, nxt):
                    for c in range(C):
                        exps(g, c)
                        jobs(nxt, c)
                    if not t.wide:
                        act.wait_ge(av_done.sem, av_done.at(b, ph, g, C))
                        copy(o_raw[:, :], o_acc[:, 0:N]).then_inc(o_copied.sem, 1)
                    jobs(nxt, C)

                groups(act, t, first, pair)

            def feed_forward(b, s):
                l = FFN[s]
                ph = ("ff", s)
                func = [ACT.Gelu, ACT.Gelu_apprx_tanh, ACT.Gelu, ACT.Silu][l]
                for j in range(2) if l < 2 else (0, 2):
                    act.wait_ge(job_full.sem, job_full.at(b, ph, c=j + 1))
                    for m in range(2):
                        c = 2 * j + m if l < 2 else j + m
                        col = C_FFB + l * 8 + c
                        dst = ff_h if l < 2 else ff_g
                        last = act.activation(dst[:, c, :], ring[:, j % 2, m * N:(m + 1) * N], func,
                                              bias=cols[:, col:col + 1])
                    last.then_inc(slot_free[j % 2].sem, 1)

            with act.Fori(0, B) as b:
                prep(b)
                for s in SUBS:
                    if s in ATT:
                        if ATT[s].src is not None:
                            source(b, s)
                        attention(b, ATT[s])
                    else:
                        feed_forward(b, s)

        @block.vector
        def _(dve):
            dve.sem_inc(slot_free[0].sem, 1)
            dve.sem_inc(slot_free[1].sem, 1)
            dve.sem_inc(op_ready.sem, 1)
            dve.sem_inc(attn_ready.sem, 1)
            dve.sem_inc(x_out_ready.sem, 1)
            dve.wait_ge(const_in, 16 * (N_CONST + 1))
            dve.wait_ge(init_done, 2)
            dve.tensor_copy(ident_bf[:, :], ident)

            def wide_cols(c, n):
                return cols[:, c:c + n].unsqueeze(2).broadcast_to([P, n, B])

            by_mod = mod_ab[:, :, :].rearrange("p b m -> p m b")
            dve.wait_ge(mod_full, 1)
            mod_psum = scores[:, 0, 0:N_MOD * B].rearrange("p (m b) -> p m b", b=B)
            dve.tensor_tensor(mod_raw, mod_psum, wide_cols(C_MODB, N_MOD), ALU.add).then_inc(mod_step, 1)
            dve.wait_ge(mod_step, 1)
            dve.tensor_scalar(mod_scale, mod_raw[:, 0:24:2, :], 1.0, None, ALU.add).then_inc(mod_step, 1)
            dve.wait_ge(mod_step, 2)
            dve.tensor_tensor(by_mod[:, 0:24:2, :], mod_scale, wide_cols(C_LNW, 12), ALU.mult)
            dve.tensor_copy(by_mod[:, 24:27, :], mod_raw[:, 24:27, :])
            dve.tensor_tensor(mod_scale, mod_scale, wide_cols(C_LNB, 12), ALU.mult).then_inc(mod_step, 1)
            dve.wait_ge(mod_step, 3)
            dve.tensor_tensor(by_mod[:, 1:24:2, :], mod_scale, mod_raw[:, 1:24:2, :], ALU.add).then_inc(mod_step, 1)
            dve.memset(wide_v[:, :, :, 1:3, :], 1.0).then_inc(init_done, 1)
            dve.wait_ge(mod_step, 4)

            def prep(b):
                dve.tensor_copy(ab[:, :], mod_ab[:, b, :]).then_inc(ab_ready.sem, 1)
                dve.wait_ge(x_out_ready.sem, x_out_ready.at(b, "x", c=0))
                dve.wait_ge(x_in_done.sem, x_in_done.at(b, "prep", c=16))
                dve.tensor_copy(x[:, :, :], x_in[:, :, :]).then_inc(x_done.sem, 1)
                dve.wait_ge(ctx_in_done.sem, ctx_in_done.at(b, "prep", c=32))
                tiles = [(t, P if t < CT - 1 else LAST) for t in range(CT)]
                for t, n in tiles:
                    last = dve.bn_stats(ctx_stats[0:n, t, :], ctx_in[0:n, t, :])
                last.then_inc(ctx_stat.sem, 1)
                dve.wait_ge(ctx_stat.sem, ctx_stat.at(b, "prep", c=1))
                dve.sem_inc(waited_dve, 1)
                for t, n in tiles:
                    last = dve.bn_aggr(ctx_mv[0:n, t, :], ctx_stats[0:n, t, :])
                last.then_inc(ctx_mv_ready.sem, 1)
                dve.wait_ge(ctx_mv_ready.sem, ctx_mv_ready.at(b, "prep", c=1))
                dve.wait_ge(ctx_rstd_ready.sem, ctx_rstd_ready.at(b, "prep", c=1))
                for t, n in tiles:
                    last = dve.tensor_scalar(ctx_norm[0:n, t, :], ctx_in[0:n, t, :], ctx_mv[0:n, t, 0:1],
                                             ctx_rstd[0:n, t:t + 1], ALU.subtract, ALU.mult)
                last.then_inc(ctx_norm_ready.sem, 1)

            def gate(b):
                dve.wait_ge(ab_ready.sem, ab_ready.at(b, "prep", c=1))
                dve.tensor_tensor(gate_diag[:, :, :], ident.unsqueeze(1).broadcast_to([P, 3, P]),
                                  ab[:, 24:27].unsqueeze(2).broadcast_to([P, 3, P]), ALU.mult)\
                    .then_inc(diag_ready.sem, 1)
                dve.wait_ge(job_full.sem, job_full.at(b, "gate", c=1))
                dve.tensor_copy(gate_rows[:, :, :], ring[:, 1, 0:3 * P].rearrange("p (a d) -> p a d", a=3))\
                    .then_inc(slot_free[1].sem, 1)
                dve.wait_ge(slot_free[1].sem, slot_free[1].at(b, "gate", c=1))

                def gated(out, w, i):
                    return dve.tensor_tensor(out, w, gate_rows[:, i, :].unsqueeze(1).broadcast_to([P, 4, P]), ALU.mult)

                gated(gated_wo[:, 0, :, :], head_dims, 0)
                gated(gated_wo[:, 1, :, :], narrow_w[:, NARROW_AT[10], NO:NO + 4 * P].rearrange("p (g d) -> p g d", g=4), 1)
                gated(gated_w2[:, :, :], ff2_w[:, 3, :, :], 2)
                dve.tensor_tensor(gated_bo[:, :], rows[:, R_OUT + 10 * P:R_OUT + 11 * P], gate_rows[0:1, 1, :], ALU.mult)\
                    .then_inc(gated_ready.sem, 1)

            def layernorm(b, s):
                ph = ("ln", s)
                dve.wait_ge(x_done.sem, x_done.at(b, "x", c=s + 1))
                for q in range(QT):
                    last = dve.bn_stats(stats[:, q, :], x[:, q, :])
                last.then_inc(stat.sem, 1)
                dve.wait_ge(stat.sem, stat.at(b, ph, c=1))
                dve.sem_inc(waited_dve, 1)
                for q in range(QT):
                    last = dve.bn_aggr(mv[:, q, :], stats[:, q, :])
                last.then_inc(mv_ready.sem, 1)
                dve.wait_ge(mv_ready.sem, mv_ready.at(b, ph, c=1))
                dve.wait_ge(rstd_ready.sem, rstd_ready.at(b, ph, c=1))
                for q in range(QT):
                    last = dve.tensor_scalar(xn[:, q, :], x[:, q, :], mv[:, q, 0:1], rstd[:, q:q + 1],
                                             ALU.subtract, ALU.mult)
                last.then_inc(xn_ready.sem, 1)
                dve.wait_ge(job_full.sem, job_full.at(b, ph, c=1))
                dve.wait_ge(ab_ready.sem, ab_ready.at(b, "prep", c=1))
                dve.tensor_scalar(h_t[:, :], ring[:, 0, 0:N], ab[:, 2 * s:2 * s + 1], ab[:, 2 * s + 1:2 * s + 2],
                                  ALU.mult, ALU.add).then_inc(slot_free[0].sem, 1)

            def headnorm(b):
                def step(n):
                    dve.wait_ge(hn_step.sem, hn_step.at(b, "headnorm", c=n))

                def spread(v):
                    return v[:, :].unsqueeze(2).broadcast_to([P, 32, 8])

                dve.wait_ge(job_full.sem, job_full.at(b, "headnorm", c=1))
                dve.tensor_copy(hn[:, :, :], ring[:, 1, 0:N].rearrange("p (h d) -> p h d", d=8))\
                    .then_inc(slot_free[1].sem, 1)
                dve.wait_ge(slot_free[1].sem, slot_free[1].at(b, "headnorm", c=1))
                dve.tensor_reduce(hn_sum[:, :], hn[:, :, :], AX.X, ALU.add).then_inc(hn_step.sem, 1)
                step(1)
                dve.scalar_tensor_tensor(hn_cen[:, :, :], spread(hn_sum), -1.0 / 8, hn[:, :, :], ALU.mult, ALU.add)\
                    .then_inc(hn_step.sem, 1)
                step(2)
                dve.scalar_tensor_tensor(hn_sq[:, :, :], hn_cen[:, :, :], 1.0 / 8, hn_cen[:, :, :], ALU.mult, ALU.mult)\
                    .then_inc(hn_step.sem, 1)
                step(3)
                dve.tensor_reduce(hn_var[:, :], hn_sq[:, :, :], AX.X, ALU.add).then_inc(hn_step.sem, 1)
                dve.wait_ge(hn_rstd_ready.sem, hn_rstd_ready.at(b, "headnorm", c=2))
                dve.tensor_tensor(hn[:, :, :], hn_cen[:, :, :], spread(hn_rstd), ALU.mult)\
                    .then_inc(hn_step.sem, 1)
                dve.wait_ge(job_full.sem, job_full.at(b, "headnorm", c=2))
                dve.tensor_copy(n_t[:, :], ring[:, 0, 0:N]).then_inc(slot_free[0].sem, 1)

            def attention(b, t):
                ph = ("att", t.sub)
                C = len(t.chunks)
                nq = t.heads * QT
                parts = len(t.kc) if t.cross else 1

                def job(g, j):
                    kind, i, k = t.jobs[j]
                    u, r = g[1], j % 2
                    if kind == "val":
                        return
                    if kind == "max":
                        h, q = i
                        dve.wait_ge(job_full.sem, job_full.at(b, ph, g, j + 1))
                        w = t.kc[k][1]
                        if q is None:
                            src = ring[:, r, 0:QT * w].rearrange("p (q k) -> p q k", q=QT)
                            dst = max_part[:, u, 2 * h:2 * h + 2, 0]
                        else:
                            src, dst = ring[:, r, 0:w], max_part[:, u, 2 * h + q, k:k + 1]
                        dve.tensor_reduce(dst, src, AX.X, ALU.max).then_inc(slot_free[r].sem, 1)
                        return
                    a0, w = (0, 2 * N if t.wide else N) if i == 0 else t.kc[i - 1]
                    v = raw[:, i % 2, 0:w]
                    if t.rope:
                        dve.wait_ge(job_full.sem, job_full.at(b, ph, g, j + 1))
                        table = rope_sin if k else rope_cos
                        tab, src = table[:, a0:a0 + w], ring[:, r, 0:w]
                        dst = raw_swap[:, 0:w] if k else v
                        if i == 0:
                            tab = table[:, 0:N].unsqueeze(1).broadcast_to([P, 2, N])
                            src = src.rearrange("p (h n) -> p h n", h=2)
                            dst = dst.rearrange("p (h n) -> p h n", h=2)
                        dve.tensor_tensor(dst, src, tab, ALU.mult).then_inc(slot_free[r].sem, 1)
                        if k == 0:
                            return
                        for rr, jj in ((r, j), (1 - r, j - 1)):
                            dve.wait_ge(slot_free[rr].sem, slot_free[rr].at(b, ph, g, jj // 2 + 1))
                        dve.tensor_tensor(v, v, raw_swap[:, 0:w], ALU.add).then_inc(rope_sum.sem, 1)
                        dve.wait_ge(rope_sum.sem, rope_sum.at(b, ph, g, i + 1))
                        if i == 0:
                            last = dve.tensor_copy(qop[:, u, 0:2, :].rearrange("p h n -> p (h n)"), v)
                        else:
                            dve.tensor_copy(kop[0:64, u, 0, a0:a0 + w], v[0:64, :])
                            last = dve.tensor_copy(kop[64:128, u, 1, a0:a0 + w], v[64:128, :])
                        last.then_inc(rope_high.sem, 1)
                        dve.wait_ge(rope_high.sem, rope_high.at(b, ph, g, i + 1))
                    else:
                        dve.wait_ge(slot_free[r].sem, slot_free[r].at(b, ph, g, j // 2 + 1))
                    if t.wide and i == 0:
                        last = dve.tensor_tensor(qop[:, u, 2:4, :].rearrange("p h n -> p (h n)"), v,
                                                 qop[:, u, 0:2, :].rearrange("p h n -> p (h n)"), ALU.subtract)
                    elif t.wide:
                        dve.tensor_tensor(kop[64:128, u, 0, a0:a0 + w], v[0:64, :], kop[0:64, u, 0, a0:a0 + w],
                                          ALU.subtract)
                        last = dve.tensor_tensor(kop[0:64, u, 1, a0:a0 + w], v[64:128, :],
                                                 kop[64:128, u, 1, a0:a0 + w], ALU.subtract)
                    elif i == 0:
                        dve.scalar_tensor_tensor(qsplit[:, :], high[:, 0, 0:w], cols[:, C_NEGQ:C_NEGQ + 1], v,
                                                 ALU.mult, ALU.add).then_inc(q_split.sem, 1)
                        dve.wait_ge(q_split.sem, q_split.at(b, ph, g, 1))
                        for h in range(4):
                            last = dve.tensor_scalar(qop[:, u, h, :], qsplit[:, :], cols[:, C_HEAD + h:C_HEAD + h + 1],
                                                     None, ALU.mult)
                    else:
                        last = dve.scalar_tensor_tensor(kop[:, u, 0, a0:a0 + w], high[:, i % 2, 0:w],
                                                        cols[:, C_NEGK:C_NEGK + 1], v, ALU.mult, ALU.add)
                    last.then_inc(op_ready.sem, 1)

                def jobs(g, c):
                    if g is not None:
                        for j in range(t.cuts[c], t.cuts[c + 1]):
                            job(g, j)

                def shifts(g):
                    u = g[1]
                    j = len(t.jobs) - 1
                    dve.wait_ge(slot_free[j % 2].sem, slot_free[j % 2].at(b, ph, g, j // 2 + 1))
                    dve.tensor_reduce(max_neg[:, u, 0:nq], max_part[:, u, 0:nq, 0:parts], AX.X, ALU.max, negate=True)\
                        .then_inc(max_ready.sem, 1)
                    dve.wait_ge(max_ready.sem, max_ready.at(b, ph, g, 1))
                    dve.tensor_tensor(shift[:, u, 0:t.heads, :].rearrange("p h (q k) -> p (h q) k", q=QT),
                                      ident_bf[:, :].unsqueeze(1).broadcast_to([P, nq, P]),
                                      max_neg[:, u, 0:nq].unsqueeze(2).broadcast_to([P, nq, P]), ALU.mult)\
                        .then_inc(shift_ready.sem, 1)

                def normalise(g):
                    u = g[1]
                    if t.wide:
                        dve.wait_ge(av_done.sem, av_done.at(b, ph, g, C))
                        dve.reciprocal(o_inv[0:64, :], o_acc[64:128, 0:N])
                        dve.reciprocal(o_inv[64:128, :], o_acc[0:64, N:2 * N]).then_inc(inv_ready.sem, 1)
                        dve.wait_ge(inv_ready.sem, inv_ready.at(b, ph, g, 1))
                        dve.tensor_tensor(attn[0:64, u, :], o_acc[0:64, 0:N], o_inv[0:64, :], ALU.mult)
                        dve.tensor_tensor(attn[64:128, u, :], o_acc[64:128, N:2 * N], o_inv[64:128, :], ALU.mult)\
                            .then_inc(attn_ready.sem, 1)
                    else:
                        dve.wait_ge(sums_spread.sem, sums_spread.at(b, ph, g, 1))
                        dve.reciprocal(o_inv[:, :], o_acc[:, N:2 * N]).then_inc(inv_ready.sem, 1)
                        dve.wait_ge(inv_ready.sem, inv_ready.at(b, ph, g, 1))
                        dve.tensor_tensor(attn[:, u, :], o_raw[:, :], o_inv[:, :], ALU.mult).then_inc(attn_ready.sem, 1)

                def first(g):
                    for j in range(len(t.jobs)):
                        job(g, j)
                    shifts(g)

                def pair(g, nxt):
                    for c in range(C):
                        jobs(nxt, c)
                    if t.wide:
                        normalise(g)
                        jobs(nxt, C)
                    else:
                        jobs(nxt, C)
                        normalise(g)
                    if nxt is not None:
                        shifts(nxt)

                groups(dve, t, first, pair)
                projected = wide_projected if t.wide else narrow_projected
                dve.wait_ge(projected.sem, projected.at(b, ph, (t.groups // 2 - 1, 1), 1))
                add_y(b, t.sub)

            def add_y(b, s):
                y = y_acc[:, 0:QT * D].rearrange("p (q d) -> p q d", q=QT)
                if s == SUBS[-1]:
                    dve.wait_ge(x_out_free.sem, x_out_free.at(b, "x", c=0))
                    dve.tensor_tensor(x_out[:, :, :], x[:, :, :], y, ALU.add).then_inc(x_out_ready.sem, 1)
                else:
                    dve.tensor_tensor(x[:, :, :], x[:, :, :], y, ALU.add).then_inc(x_done.sem, 1)

            def feed_forward(b, s):
                l = FFN[s]
                ph = ("ff", s)
                if l >= 2:
                    for j in (1, 3):
                        dve.wait_ge(job_full.sem, job_full.at(b, ph, c=j + 1))
                        dve.wait_ge(slot_free[0].sem, slot_free[0].at(b, ph, c=j // 2 + 1))
                        for m in range(2):
                            c = j - 1 + m
                            col = C_FFB + l * 8 + FF + c
                            last = dve.scalar_tensor_tensor(ff_h[:, c, :], ring[:, 1, m * N:(m + 1) * N],
                                                            cols[:, col:col + 1], ff_g[:, c, :], ALU.add, ALU.mult)
                        last.then_inc(slot_free[1].sem, 1)
                dve.wait_ge(ff_done.sem, ff_done.at(b, ph, c=1))
                add_y(b, s)

            with dve.Fori(0, B) as b:
                prep(b)
                gate(b)
                for s in SUBS:
                    layernorm(b, s)
                    if s == 9:
                        headnorm(b)
                    if s in ATT:
                        attention(b, ATT[s])
                    else:
                        feed_forward(b, s)


def chunk_slot(t, g, c):
    return (c + g[1] * len(t.chunks)) % 2



def _pad(w, n):
    import numpy as np
    out = np.zeros((n, *w.shape[1:]), np.float32)
    out[:w.shape[0]] = w
    return out


def _swapped(w):
    return w.reshape(w.shape[0], -1, 2)[:, :, ::-1].reshape(w.shape)


def _wide_blob(wq, wk, wv, wo, rope):
    import numpy as np
    out = np.zeros((H // 2, P, STAGE if rope else SQS), np.float32)
    for g in range(H // 2):
        pair = slice(g * P, (g + 1) * P)

        def twice(w, at):
            for h in range(2):
                one = w[:, g * P + h * 64:g * P + (h + 1) * 64]
                out[g, :, at + h * P:at + h * P + 64] = one
                out[g, :, at + h * P + 64:at + (h + 1) * P] = one

        twice(wq, SQ)
        out[g, 0:wk.shape[0], SK:SK + P] = wk[:, pair]
        out[g, 0:wv.shape[0], SV:SV + P] = wv[:, pair]
        out[g, :, SO:SO + P] = wo[pair, :]
        if rope:
            twice(_swapped(wq), SQS)
            out[g, 0:wk.shape[0], SKS:SKS + P] = _swapped(wk)[:, pair]
    return out


def _spread(w):
    import numpy as np
    lead = w.shape[:-1]
    v = w.reshape(*lead, 4, 4, 1, 8)
    return np.broadcast_to(v, (*lead, 4, 4, 4, 8)).reshape(*lead, 4, P)


def kernel(**inputs):
    import numpy as np
    import concourse.bacc as bacc
    from concourse.bass_utils import run_bass_kernel_spmd

    i = {k: np.asarray(v) for k, v in inputs.items()}

    def w(layer, name):
        return i[f"L{layer}_xcond_{name}"]

    f32 = np.float32
    l1w, l1b = np.split(w(1, "W_ada"), 6, axis=1), np.split(w(1, "b_ada"), 6)
    l3w, l3b = np.split(w(3, "adaln_w").T, 9, axis=1), np.split(w(3, "adaln_b"), 9)
    mods = [(w(0, "g1_w"), w(0, "g1_b")), (w(0, "b1_w"), w(0, "b1_b"))] * 2
    mods += [(w(0, "g2_w"), w(0, "g2_b")), (w(0, "b2_w"), w(0, "b2_b"))]
    for n in range(3):
        mods += [(l1w[2 * n + 1], l1b[2 * n + 1]), (l1w[2 * n], l1b[2 * n])]
    for n in range(1, 4):
        for half in range(2):
            mods.append((w(2, f"n{n}_w")[:, half * P:(half + 1) * P], w(2, f"n{n}_b")[half * P:(half + 1) * P]))
    for n in range(3):
        mods += [(l3w[3 * n + 1], l3b[3 * n + 1]), (l3w[3 * n], l3b[3 * n])]
    mods += [(l3w[3 * n + 2], l3b[3 * n + 2]) for n in range(3)]

    zero, zeros, eye = np.zeros(P, f32), np.zeros((P, P), f32), np.eye(P, dtype=f32)
    qkv, qkv_b = w(1, "W_qkv"), w(1, "b_qkv")
    ca, ca_b = w(3, "ca_in_w").T, w(3, "ca_in_b")

    def on_diagonal(v):
        out = np.zeros((P, P), f32)
        out[np.arange(P), np.arange(P)] = np.tile(v, H)
        return out

    narrow = [
        (qkv[:, 0:P], qkv_b[0:P], qkv[:, P:2 * P], qkv_b[P:2 * P], qkv[:, 2 * P:], qkv_b[2 * P:], w(1, "W_proj")),
        (w(1, "W_q"), zero, w(1, "W_k"), zero, w(1, "W_v"), zero, w(1, "W_out")),
        (on_diagonal(w(3, "qn_w")), np.tile(w(3, "qn_b"), H), on_diagonal(w(3, "kn_w")), np.tile(w(3, "kn_b"), H),
         eye, zero, zeros),
        (ca[:, 0:P], ca_b[0:P], ca[:, P:2 * P], ca_b[P:2 * P], ca[:, 2 * P:], ca_b[2 * P:], w(3, "ca_out_w").T),
    ]

    cols = np.zeros((P, C_END), f32)
    for m, (_, bias) in enumerate(mods):
        cols[:, C_MODB + m] = bias
    cols[:, C_LNW:C_LNW + 12] = 1
    for s, n in ((0, 1), (1, 1), (2, 2)):
        cols[:, C_LNW + s], cols[:, C_LNB + s] = w(0, f"ln{n}_w"), w(0, f"ln{n}_b")
    cols[0:DC, C_CLNW], cols[0:DC, C_CLNB] = w(0, "ca_lnc_w"), w(0, "ca_lnc_b")
    cols[:, C_SRCB], cols[:, C_SRCB + 1] = w(1, "b_ctx"), w(3, "cond_b")
    half = FF * P
    b_ff2 = w(2, "ff_b1")
    for l, bias in ((0, w(0, "ff_b1")), (1, w(1, "b_fc1")), (2, np.concatenate([b_ff2[half:], b_ff2[:half]]))):
        cols[:, C_FFB + l * 8:C_FFB + l * 8 + len(bias) // P] = bias.reshape(-1, P).T
    for n, (_, bq, _, bk, _, _, _) in enumerate(narrow):
        cols[:, C_QB + 4 * n:C_QB + 4 * n + 4] = _spread(bq).T
        cols[:, C_KB + 4 * n:C_KB + 4 * n + 4] = _spread(bk).T
    r = np.arange(P)
    cols[(r // 8) % 2 == 1, C_NEGK] = -1
    cols[(r // 8) % 4 >= 2, C_NEGQ] = -1
    for h in range(4):
        cols[r // 32 == h, C_HEAD + h] = 1
    cols[:, C_COND:C_COND + B] = i["cond_1024"].T

    rows = np.zeros((1, R_END), f32)
    outs = {0: w(0, "sa_bo"), 1: w(0, "ca_bo"), 2: w(0, "ff_b2"), 3: w(1, "b_proj"), 4: w(1, "b_out"), 5: w(1, "b_fc2"),
            6: w(2, "o1_b"), 7: w(2, "o2_b"), 8: w(2, "ff_b2"), 10: w(3, "ca_out_b")}
    for s, bias in outs.items():
        rows[0, R_OUT + s * P:R_OUT + (s + 1) * P] = bias
    for n, one in enumerate(narrow):
        rows[0, R_VB + n * P:R_VB + (n + 1) * P] = one[5]

    squares = np.zeros((P, K_END), f32)
    squares[:, K_ID:K_ID + P] = eye
    for h in range(4):
        squares[32 * h + 8, K_SEL + 32 * h:K_SEL + 32 * h + 32] = 1
        for g in range(4):
            for d in range(8):
                squares[32 * h + d, K_SELP + g * P + (4 * g + h) * 8 + d] = 1

    narrow_w = np.zeros((P, 4, NCOLS), f32)
    for n, (wq, _, wk, _, wv, _, wo) in enumerate(narrow):
        narrow_w[:, n, NQ:NQ + 4 * P] = _spread(wq).reshape(P, -1)
        narrow_w[:, n, NK:NK + 4 * P] = _spread(wk).reshape(P, -1)
        narrow_w[:, n, NV:NV + P] = wv
        for g in range(4):
            for h in range(4):
                narrow_w[32 * h:32 * h + 8, n, NO + g * P:NO + (g + 1) * P] = wo[(4 * g + h) * 8:(4 * g + h) * 8 + 8]

    inv = (f32(1.0) / f32(10000.0) ** (np.arange(0, 64, 2, dtype=f32) / f32(64))).astype(f32)
    angle = np.arange(M, dtype=f32)[None, :] * inv[(r % 64) // 2][:, None]
    rope_sin = np.sin(angle).astype(f32)
    rope_sin[r % 2 == 0] = -rope_sin[r % 2 == 0]

    ff2 = [w(0, "ff_w2"), w(1, "W_fc2"), w(2, "ff_w2"), w(3, "w2").T]
    g2 = w(2, "ff_w1")
    wkv0, ckv0 = w(0, "sa_wkv"), w(0, "ca_wkv")
    mid = H * 64
    arrays = {
        "x": i["x"], "ctx": i["ctx_768"], "cols": cols, "rows": rows, "squares": squares,
        "mod_w": np.concatenate([m for m, _ in mods], axis=1),
        "rope_cos": np.cos(angle).astype(f32), "rope_sin": rope_sin,
        "narrow_w": narrow_w.reshape(P, -1),
        "src_w": np.concatenate([w(1, "W_ctx"), w(3, "cond_w").T], axis=1),
        "ff1_w": np.concatenate([w(0, "ff_w1"), w(1, "W_fc1"), g2[:, half:], g2[:, :half], w(3, "w1").T, w(3, "w3").T], axis=1),
        "ff2_w": np.stack([m.reshape(FF, P, P).transpose(1, 0, 2) for m in ff2], axis=1).reshape(P, -1),
        "wide0": _wide_blob(w(0, "sa_wq"), wkv0[:, :mid], wkv0[:, mid:], w(0, "sa_wo"), True),
        "wide1": _wide_blob(w(0, "ca_wq"), ckv0[:, :mid], ckv0[:, mid:], w(0, "ca_wo"), True),
        "wide6": _wide_blob(w(2, "q1"), w(2, "k1"), w(2, "v1"), w(2, "o1_w"), False),
        "wide7": _wide_blob(w(2, "q2"), w(2, "k2"), w(2, "v2"), w(2, "o2_w"), False),
    }
    arrays = {k: np.ascontiguousarray(v) for k, v in arrays.items()}
    nc = bacc.Bacc("TRN2", target_bir_lowering=False, num_devices=1)
    drams = {k: nc.dram_tensor(f"in_{k}", v.shape, mybir.dt.from_np(v.dtype), kind="ExternalInput").ap()
             for k, v in arrays.items()}
    drams["out"] = nc.dram_tensor("out", (B, N, D), F32, kind="ExternalOutput").ap()
    build(nc, drams)
    got = run_bass_kernel_spmd(nc, [{f"in_{k}": v for k, v in arrays.items()}], core_ids=[0])
    return got.results[0]["out"]
```

```python
from contextlib import ExitStack

import concourse.bass as bass
from concourse import mybir

F32 = mybir.dt.float32
BF16 = mybir.dt.bfloat16
F16 = mybir.dt.float16
ALU = mybir.AluOpType
ACT = mybir.ActivationFunctionType
AX = mybir.AxisListType

P = 128
B, N, D = 8, 256, 128
M, DC = 1601, 96
H = 16
QT = N // P
CT = -(-M // P)
LAST = M - (CT - 1) * P
MP = CT * P
FF = 4
BANK = 512
EPS0, EPS1 = 1e-5, 1e-6


class Attention:

    def __init__(self, sub, wide, cross, rope=False, src=None, vbias=False):
        self.sub, self.wide, self.cross, self.rope = sub, wide, cross, rope
        self.src, self.vbias = src, vbias
        self.heads = 2 if wide else 4
        self.groups = H // self.heads
        self.keys = M if cross else N
        self.kt = -(-self.keys // P)
        self.scale = float((64 if wide else 8) ** -0.5)
        self.dk = DC if (cross and wide) else D
        self.kc = [(a, min(BANK, self.keys - a)) for a in range(0, self.keys, BANK)]
        jobs = []
        for o in range(1 + len(self.kc)):
            jobs.append(("op", o, 0))
            if rope:
                jobs.append(("op", o, 1))
        self.ops = 1 + len(self.kc)
        per = 4 if wide else self.kt
        self.vjobs = [(t, min(per, self.kt - t)) for t in range(0, self.kt, per)]
        vals = [("val", v, 0) for v in range(len(self.vjobs))]
        if cross:
            jobs += vals
            for h in range(self.heads):
                for q in range(QT):
                    jobs += [("max", (h, q), k) for k in range(len(self.kc))]
        else:
            jobs += [("max", (h, None), 0) for h in range(self.heads)] + vals
        self.jobs = jobs
        kinds = [kind for kind, _, _ in jobs]
        self.last_max = len(kinds) - 1 - kinds[::-1].index("max")
        self.last_val = len(kinds) - 1 - kinds[::-1].index("val")
        self.span = {k: range(kinds.index(k), kinds.index(k) + kinds.count(k)) for k in ("op", "val", "max")}
        full = [t for t in range(self.kt) if (t + 1) * P <= self.keys]
        rest = [t for t in range(self.kt) if (t + 1) * P > self.keys]
        if wide:
            self.chunks = [[[(h, i), (h, i + 1)] for h in range(2)] for i in full[::2]]
            self.chunks += [[[(0, t), (1, t)]] for t in rest]
        else:
            self.chunks = [[[(0, t), (1, t)], [(2, t), (3, t)]] for t in range(self.kt)]
        self.weigh = []
        for banks in self.chunks:
            blocks = [(h, k, 2 * i + m) for i, bank in enumerate(banks) for m, (h, k) in enumerate(bank)]
            tiles = sorted({k for _, k, _ in blocks})
            self.weigh.append([[one for one in blocks if one[1] == k] for k in tiles])
        C = len(self.chunks)
        self.head = min(2, C)
        self.steps = []
        for c in range(C):
            if c + self.head < C:
                self.steps += [("scores", c + self.head, i) for i in range(len(self.chunks[c + self.head]))]
            self.steps += [("values", c, i) for i in range(len(self.weigh[c]))]
        if self.head > 1:
            self.steps = []
            for c in range(2, C + 2):
                if c - 2 < C:
                    self.steps += [("values", c - 2, i) for i in range(len(self.weigh[c - 2]))]
                if c < C:
                    self.steps += [("scores", c, i) for i in range(len(self.chunks[c]))]
        cost = [self.cost(*one) for one in jobs]
        spread = max(1, len(self.steps) - 1)
        upto, total = [sum(cost[:j]) for j in range(len(jobs))], sum(cost)
        self.cuts = [sum(c < total * i / spread for c in upto) for i in range(spread + 1)]
        self.cuts[-1] = len(jobs)
        self.cuts += [len(jobs)] * (len(self.steps) + 1 - len(self.cuts))

    def cost(self, kind, i, k):
        if kind == "val":
            return BANK
        if kind == "max":
            return self.kc[k][1] if self.cross else BANK
        w = (2 * N if self.wide else N) if i == 0 else self.kc[i - 1][1]
        if self.rope:
            return 4 * w if k else w
        return 2 * w

    def rows(self, t):
        return min(P, self.keys - t * P)

    def sum_steps(self, c):
        return sum(1 if i == 0 or len(banks) == 1 else 2 for i, banks in enumerate(self.chunks[:c]))

    def slot_uses(self, r):
        return len(self.jobs[r::2])


WIDE = {0: Attention(0, True, False, rope=True), 1: Attention(1, True, True, rope=True),
        6: Attention(6, True, False), 7: Attention(7, True, True)}
NARROW = {3: Attention(3, False, False, vbias=True), 4: Attention(4, False, True, src=0),
          9: Attention(9, False, False), 10: Attention(10, False, True, src=1, vbias=True)}
ATT = {**WIDE, **NARROW}
FFN = {2: 0, 5: 1, 8: 2, 11: 3}
GATED = {2, 3}
SUBS = range(12)
NARROW_AT = {s: i for i, s in enumerate(NARROW)}
WIDE_AT = {s: i for i, s in enumerate(WIDE)}

SQ, SK, SV, SQS, SKS, SO = 0, 256, 384, 512, 768, 896
STAGE = SO + P

NQ, NK, NO, NV = 0, 4 * P, 8 * P, 12 * P
NCOLS = 12 * P + 4 * 32

N_MOD = 27
C_MODB = 0
C_LNW = C_MODB + N_MOD
C_LNB = C_LNW + 12
C_CLNW = C_LNB + 12
C_CLNB = C_CLNW + 1
C_SRCB = C_CLNB + 1
C_FFB = C_SRCB + 2
C_QB = C_FFB + 4 * 8
C_KB = C_QB + 16
C_NEGK = C_KB + 16
C_NEGQ = C_NEGK + 1
C_HEAD = C_NEGQ + 1
C_COND = C_HEAD + 4
C_END = C_COND + B

R_OUT = 0
R_VB = 12 * P
R_END = R_VB + 4 * P

K_ID, K_SEL, K_SELP = 0, P, 2 * P
K_END = 2 * P + 4 * P

FF1_AT = [0, 512, 1024, 2048]
FF1_COLS = 3072


class Count:

    def __init__(self, sem, phases, credit=0):
        self.sem, self.credit = sem, credit
        self.base, self.inc, total = {}, {}, 0
        for name, groups, inc in phases:
            self.base[name], self.inc[name] = total, inc
            total += groups * inc
        self.total = total

    def at(self, b, phase, g=(0, 0), c=0):
        it, u = g
        inc = self.inc[phase]
        fixed = self.base[phase] + u * inc + c + self.credit
        if isinstance(it, int):
            return b * self.total + (fixed + it * 2 * inc)
        return b * self.total + it * (2 * inc) + fixed


def build(nc, a):
    with ExitStack() as ctx:
        def sb(name, shape, dt=F32):
            return ctx.enter_context(nc.sbuf_tensor(name, shape, dt))

        def psum(name, shape):
            return ctx.enter_context(nc.psum_tensor(name, shape, F32))

        def sem(name):
            return ctx.enter_context(nc.semaphore(name))

        cols = sb("cols", [P, C_END])
        rows = sb("rows", [1, R_END])
        squares = sb("squares", [P, K_END])
        ident = squares[:, K_ID:K_ID + P]
        sum_row = squares[:, K_SEL:K_SEL + P]
        head_dims = squares[:, K_SELP:K_SELP + 4 * P].rearrange("p (g d) -> p g d", g=4)
        ones = sb("ones", [P, P])
        ones_bf = sb("ones_bf", [P, P], BF16)
        ident_bf = sb("ident_bf", [P, P], BF16)
        minus_half = sb("minus_half", [P, 32])
        eps0 = sb("eps0", [P, CT])
        eps1 = sb("eps1", [P, 32])
        rope_cos = sb("rope_cos", [P, M])
        rope_sin = sb("rope_sin", [P, M])
        narrow_w = sb("narrow_w", [P, 4, NCOLS])
        src_w = sb("src_w", [DC, 2, P])
        ff1_w = sb("ff1_w", [P, FF1_COLS])
        ff2_w = sb("ff2_w", [P, 4, FF, P])
        mod_ab = sb("mod_ab", [P, B, N_MOD])
        x_in = sb("x_in", [P, QT, D])
        ctx_in = sb("ctx_in", [P, CT, DC])
        x = sb("x", [P, QT, D])
        x_out = sb("x_out", [P, QT, D])
        ab = sb("ab", [P, N_MOD])
        ctx_t = sb("ctx_t", [DC, MP])
        ctx_norm_t = sb("ctx_norm_t", [DC, MP])
        src_t = sb("src_t", [P, MP])
        ctx_stats = sb("ctx_stats", [P, CT, 6])
        ctx_mv = sb("ctx_mv", [P, CT, 2])
        ctx_var = sb("ctx_var", [P, CT])
        ctx_rstd = sb("ctx_rstd", [P, CT])
        stats = sb("stats", [P, QT, 6])
        mv = sb("mv", [P, QT, 2])
        var = sb("var", [P, QT])
        rstd = sb("rstd", [P, QT])
        xn = sb("xn", [P, QT, D])
        h_t = sb("h_t", [D, N])
        gated_wo = sb("gated_wo", [P, 2, 4, P])
        gated_w2 = sb("gated_w2", [P, FF, P])
        gated_bo = sb("gated_bo", [1, P])
        hn_sum = sb("hn_sum", [P, 32])
        hn_var = sb("hn_var", [P, 32])
        hn_rstd = sb("hn_rstd", [P, 32])
        n_t = sb("n_t", [D, N])
        stage = sb("stage", [P, 2, SO])
        wo_stage = sb("wo_stage", [P, 2, P])
        kop = sb("kop", [P, 2, 2, MP], F16)
        qop = sb("qop", [P, 2, 4, N], F16)
        qsplit = sb("qsplit", [P, N], F16)
        wide_v = sb("wide_v", [P, 2, CT, P])
        weight_sum = sb("weight_sum", [P, 2, N])
        narrow_v = sb("narrow_v", [P, 2, CT, 4, 32])
        raw = sb("raw", [P, 2, BANK])
        raw_swap = sb("raw_swap", [P, BANK])
        max_part = sb("max_part", [P, 2, 8, 4])
        max_neg = sb("max_neg", [P, 2, 8])
        shift = sb("shift", [P, 2, 4, N], BF16)
        probs = sb("probs", [P, 2, 2 * BANK])
        o_raw = sb("o_raw", [P, N])
        o_inv = sb("o_inv", [P, N])
        attn = sb("attn", [P, 2, N])
        ff_h = sb("ff_h", [P, FF, N])
        ff_g = sb("ff_g", [P, FF, N])

        ctx_norm = probs[:, :, :].rearrange("p s k -> p (s k)")[:, 0:CT * DC].rearrange("p (t d) -> p t d", d=DC)
        high = raw_swap[:, :].bitcast(F16).rearrange("p (s k) -> p s k", s=2)
        ff_h_flat = ff_h[:, :, :].rearrange("p f n -> p (f n)")
        ff_g_flat = ff_g[:, :, :].rearrange("p f n -> p (f n)")
        gate_diag = ff_g_flat[:, 0:3 * P].rearrange("p (a d) -> p a d", a=3)
        gate_rows = ff_h_flat[:, 0:3 * P].rearrange("p (a d) -> p a d", a=3)
        hn = ff_h_flat[:, 0:N].rearrange("p (h d) -> p h d", d=8)
        hn_cen = ff_g_flat[:, 0:N].rearrange("p (h d) -> p h d", d=8)
        hn_sq = ff_g_flat[:, N:2 * N].rearrange("p (h d) -> p h d", d=8)

        scores = psum("scores", [P, 2, 2 * BANK])
        ring = psum("ring", [P, 2, BANK])
        o_acc = psum("o_acc", [P, BANK])
        y_acc = psum("y_acc", [P, BANK])

        mod_w = wide_v[:, :, :, :].rearrange("p u t c -> p (u t) c")
        mod_w_rest = attn[:, :, :].rearrange("p u (t c) -> p (u t) c", c=P)
        N_MOD_FIRST = 2 * CT
        cond_silu = o_raw[:, 0:B]
        mod_raw = ff_h_flat[:, 0:N_MOD * B].rearrange("p (m b) -> p m b", b=B)
        mod_scale = ff_g_flat[:, 0:12 * B].rearrange("p (m b) -> p m b", b=B)

        ring_phases = {"prep": (1, 8), "gate": (1, 1)}

        def phases(of):
            order = ["prep", "gate"]
            for s in SUBS:
                order += [("ln", s)]
                if s == 9:
                    order += ["headnorm"]
                if s in ATT and ATT[s].src is not None:
                    order += [("src", s)]
                order += [("att", s) if s in ATT else ("ff", s)]
            return [(p, *of(p)) for p in order if of(p)]

        def ring_jobs(r):
            def of(p):
                if p == "prep":
                    return 1, 4
                if p == "gate":
                    return (1, 1) if r == 1 else None
                if p == "headnorm":
                    return 1, 1
                kind, s = p
                if kind == "ln":
                    return (1, 1) if r == 0 else None
                if kind == "src":
                    return 1, 2
                if kind == "ff":
                    return 1, (1 if FFN[s] < 2 else 2)
                return ATT[s].groups, ATT[s].slot_uses(r)
            return of

        def all_ring_jobs(p):
            n = [ring_jobs(r)(p) for r in range(2)]
            n = [x for x in n if x]
            return n[0][0], sum(x[1] for x in n)

        def attentions(per):
            def of(p):
                if isinstance(p, tuple) and p[0] == "att" and per(ATT[p[1]]):
                    return ATT[p[1]].groups, per(ATT[p[1]])
            return of

        def only(kind, n=1):
            def of(p):
                if p == kind or (isinstance(p, tuple) and p[0] == kind):
                    return 1, n
            return of

        def count(name, of, credit=0):
            return Count(sem(name), phases(of), credit)

        job_full = count("job_full", all_ring_jobs)
        slot_free = [count(f"slot_free{r}", ring_jobs(r), 1) for r in range(2)]
        op_ready = count("op_ready", attentions(lambda t: t.ops), 1)
        rope_sum = count("rope_sum", attentions(lambda t: t.ops if t.rope else 0))
        rope_high = count("rope_high", attentions(lambda t: t.ops if t.rope else 0))
        q_split = count("q_split", attentions(lambda t: 0 if t.wide else 1))
        max_ready = count("max_ready", attentions(lambda t: 1))
        shift_ready = count("shift_ready", attentions(lambda t: 1))
        scores_full = count("scores_full", attentions(lambda t: len(t.chunks)))
        exp_done = count("exp_done", attentions(lambda t: len(t.chunks)), 2)
        av_done = count("av_done", attentions(lambda t: len(t.chunks)), 2)
        o_copied = count("o_copied", attentions(lambda t: 0 if t.wide else 1))
        sums_spread = count("sums_spread", attentions(lambda t: 0 if t.wide else 1))
        inv_ready = count("inv_ready", attentions(lambda t: 1))
        attn_ready = count("attn_ready", attentions(lambda t: 1), 1)
        weight_step = count("weight_step", attentions(lambda t: t.sum_steps(len(t.chunks)) if t.wide else 0), 2)
        wide_sums = count("wide_sums", attentions(lambda t: 1 if t.wide else 0), 1)
        wide_projected = count("wide_projected", attentions(lambda t: 1 if t.wide else 0), 2)
        stage_used = count("stage_used", attentions(lambda t: 1 if t.wide else 0), 2)
        narrow_projected = count("narrow_projected", attentions(lambda t: 0 if t.wide else 1))
        stage_in = [count(f"stage_in{u}", attentions(lambda t: 8 if t.wide else 0)) for u in range(2)]
        wo_in = [count(f"wo_in{u}", attentions(lambda t: 8 if t.wide else 0)) for u in range(2)]
        x_in_done = count("x_in_done", only("prep", 16))
        ctx_in_done = count("ctx_in_done", only("prep", 32))
        x_done = Count(sem("x_done"), [("x", 1, 12)])
        x_out_ready = Count(sem("x_out_ready"), [("x", 1, 1)], 1)
        x_out_sent = Count(sem("x_out_sent"), [("x", 1, 16)])
        x_out_free = Count(sem("x_out_free"), [("x", 1, 1)], 1)
        ab_ready = count("ab_ready", only("prep"))
        ctx_stat = count("ctx_stat", only("prep"))
        ctx_mv_ready = count("ctx_mv_ready", only("prep"))
        ctx_var_ready = count("ctx_var_ready", only("prep"))
        ctx_rstd_ready = count("ctx_rstd_ready", only("prep"))
        ctx_norm_ready = count("ctx_norm_ready", only("prep"))
        stat = count("stat", only("ln"))
        mv_ready = count("mv_ready", only("ln"))
        var_ready = count("var_ready", only("ln"))
        rstd_ready = count("rstd_ready", only("ln"))
        xn_ready = count("xn_ready", only("ln"))
        ff_done = count("ff_done", only("ff"))
        diag_ready = count("diag_ready", only("gate"))
        gated_ready = count("gated_ready", only("gate"))
        hn_step = count("hn_step", only("headnorm", 5))
        hn_rstd_ready = count("hn_rstd_ready", only("headnorm", 2))
        const_in = sem("const_in")
        init_done = sem("init_done")
        cond_ready = sem("cond_ready")
        mod_full = sem("mod_full")
        mod_step = sem("mod_step")
        waited_sp, waited_dve = sem("waited_sp"), sem("waited_dve")
        N_CONST = 10

        block = ctx.enter_context(nc.Block())

        def groups(eng, t, first, pair):
            first((0, 0), (0, 1))
            last = t.groups // 2 - 1
            if t.groups > 4:
                with eng.Fori(0, last) as it:
                    pair((it, 0), (it, 1), (it + 1, 0))
                    pair((it, 1), (it + 1, 0), (it + 1, 1))
            else:
                for it in range(last):
                    pair((it, 0), (it, 1), (it + 1, 0))
                    pair((it, 1), (it + 1, 0), (it + 1, 1))
            pair((last, 0), (last, 1), None)
            pair((last, 1), None, None)

        def between(t, n, n1, n2, job):
            if t.cross:
                if n1 is not None and n >= 0:
                    for j in range(t.cuts[n], t.cuts[n + 1]):
                        job(n1, j)
                return
            todo = [(n1, j) for j in t.span["val"]] if n1 is not None else []
            todo += [(n2, j) for j in t.span["op"]] if n2 is not None else []
            parts = len(t.steps) + 1
            for g, j in todo[-(-len(todo) * (n + 1) // parts):-(-len(todo) * (n + 2) // parts)]:
                job(g, j)

        def maxima(t, n2, job):
            if not t.cross and n2 is not None:
                for j in t.span["max"]:
                    job(n2, j)

        def operands_of(t, g, n1, job, do_head):
            for j in range(len(t.jobs)):
                job(g, j)
            if not t.cross:
                for j in t.span["op"]:
                    job(n1, j)
            do_head(g)
            maxima(t, n1, job)

        def src_of(t):
            if not t.cross:
                return n_t if t.sub == 9 else h_t
            if t.src is not None:
                return src_t
            return ctx_norm_t if t.sub == 1 else ctx_t

        @block.sync
        def _(sp):
            for dst, name in ((cols[:, :], "cols"), (rows[:, :], "rows"), (squares[:, :], "squares"),
                              (rope_cos[:, :], "rope_cos"), (rope_sin[:, :], "rope_sin"),
                              (narrow_w[:, :, :].rearrange("p a c -> p (a c)"), "narrow_w"),
                              (src_w[:, :, :].rearrange("p a c -> p (a c)"), "src_w"),
                              (ff1_w[:, :], "ff1_w")):
                sp.dma_start(dst, a[name]).then_inc(const_in, 16)
            mods = a["mod_w"].rearrange("p (m c) -> p m c", c=P)
            sp.dma_start(mod_w, mods[:, 0:N_MOD_FIRST, :]).then_inc(const_in, 16)
            sp.dma_start(mod_w_rest[:, 0:N_MOD - N_MOD_FIRST, :], mods[:, N_MOD_FIRST:, :]).then_inc(const_in, 16)
            sp.dma_start(ff2_w[:, :, :, :].rearrange("p l f d -> p (l f d)"), a["ff2_w"]).then_inc(const_in, 16)

            def load(b):
                sp.dma_start(x_in[:, :, :], a["x"][b, :, :].rearrange("(t p) d -> p t d", p=P))\
                    .then_inc(x_in_done.sem, 16)
                full = (CT - 1) * P
                sp.dma_start(ctx_in[:, 0:CT - 1, :], a["ctx"][b, 0:full, :].rearrange("(t p) d -> p t d", p=P))\
                    .then_inc(ctx_in_done.sem, 16)
                sp.dma_start(ctx_in[0:LAST, CT - 1, :], a["ctx"][b, full:M, :]).then_inc(ctx_in_done.sem, 16)

            def weights(b, t):
                w = SO if t.rope else SQS
                blob = a[f"wide{t.sub}"]

                def one(g):
                    sp.wait_ge(stage_used.sem, stage_used.at(b, ("att", t.sub), g, -1))
                    sp.sem_inc(waited_sp, 1)
                    sp.dma_start(stage[:, g[1], 0:w], blob[g[0] * 2 + g[1], :, 0:w]).then_inc(stage_in[g[1]].sem, 16)
                    sp.wait_ge(wide_projected.sem, wide_projected.at(b, ("att", t.sub), g, -1))
                    sp.sem_inc(waited_sp, 1)
                    sp.dma_start(wo_stage[:, g[1], :], blob[g[0] * 2 + g[1], :, w:w + P]).then_inc(wo_in[g[1]].sem, 16)

                with sp.Fori(0, t.groups // 2) as it:
                    one((it, 0))
                    one((it, 1))

            def sample(b, more):
                for s in WIDE:
                    weights(b, WIDE[s])
                if more:
                    sp.wait_ge(job_full.sem, job_full.at(b, "prep", c=8))
                    sp.sem_inc(waited_sp, 1)
                    load(b + 1)
                sp.wait_ge(x_out_ready.sem, x_out_ready.at(b, "x", c=1))
                sp.sem_inc(waited_sp, 1)
                sp.dma_start(a["out"][b, :, :].rearrange("(t p) d -> p t d", p=P), x_out[:, :, :])\
                    .then_inc(x_out_sent.sem, 16)
                sp.wait_ge(x_out_sent.sem, x_out_sent.at(b, "x", c=16))
                sp.sem_inc(x_out_free.sem, 1)

            sp.sem_inc(x_out_free.sem, 1)
            load(0)
            with sp.Fori(0, B - 1) as b:
                sample(b, True)
            sample(B - 1, False)

        @block.gpsimd
        def _(pool):
            pool.memset(ones[:, :], 1.0)
            pool.memset(ones_bf[:, :], 1.0)
            pool.memset(minus_half[:, :], -0.5)
            pool.memset(eps0[:, :], EPS0)
            pool.memset(eps1[:, :], EPS1)
            pool.memset(ctx_mv[:, :, :], 1.0)
            pool.memset(narrow_v[:, :, :, :, :], 1.0).then_inc(init_done, 2)
            pool.wait_ge(init_done, 2)
            pool.sem_inc(weight_step.sem, 2)

            def add_weights(b, t):
                ph = ("att", t.sub)
                C = len(t.chunks)

                def group(g):
                    for c in range(C):
                        s = chunk_slot(t, g, c)
                        n = t.rows(t.chunks[c][0][0][1])
                        total = weight_sum[0:n, :, :]
                        block = probs[0:n, s, :].rearrange("p (h m n) -> p h m n", h=2, m=2)
                        pool.wait_ge(exp_done.sem, exp_done.at(b, ph, g, c + 1))
                        if c == 0:
                            pool.wait_ge(wide_sums.sem, wide_sums.at(b, ph, g, 0))
                            pool.tensor_tensor(total, block[:, :, 0, :], block[:, :, 1, :], ALU.add)\
                                .then_inc(weight_step.sem, 1)
                            continue
                        if len(t.chunks[c]) == 1:
                            adds = [probs[0:n, s, 0:BANK].rearrange("p (h n) -> p h n", h=2)]
                        else:
                            adds = [block[:, :, m, :] for m in range(2)]
                        for m, one in enumerate(adds):
                            pool.wait_ge(weight_step.sem, weight_step.at(b, ph, g, t.sum_steps(c) + m))
                            pool.tensor_tensor(total, total, one, ALU.add).then_inc(weight_step.sem, 1)

                with pool.Fori(0, t.groups // 2) as it:
                    group((it, 0))
                    group((it, 1))

            with pool.Fori(0, B) as b:
                pool.wait_ge(ctx_mv_ready.sem, ctx_mv_ready.at(b, "prep", c=1))
                pool.tensor_tensor(ctx_var[:, :], ctx_mv[:, :, 1], eps0[:, 0:CT], ALU.add).then_inc(ctx_var_ready.sem, 1)
                pool.wait_ge(ctx_var_ready.sem, ctx_var_ready.at(b, "prep", c=1))
                pool.tensor_tensor(ctx_rstd[:, :], ctx_var[:, :], minus_half[:, 0:CT], ALU.pow)\
                    .then_inc(ctx_rstd_ready.sem, 1)
                for s in SUBS:
                    eps = eps0 if s // 3 in (0, 2) else eps1
                    pool.wait_ge(mv_ready.sem, mv_ready.at(b, ("ln", s), c=1))
                    pool.tensor_tensor(var[:, :], mv[:, :, 1], eps[:, 0:QT], ALU.add).then_inc(var_ready.sem, 1)
                    pool.wait_ge(var_ready.sem, var_ready.at(b, ("ln", s), c=1))
                    pool.tensor_tensor(rstd[:, :], var[:, :], minus_half[:, 0:QT], ALU.pow).then_inc(rstd_ready.sem, 1)
                    if s == 9:
                        pool.wait_ge(hn_step.sem, hn_step.at(b, "headnorm", c=4))
                        pool.tensor_tensor(hn_var[:, :], hn_var[:, :], eps1[:, :], ALU.add)\
                            .then_inc(hn_rstd_ready.sem, 1)
                        pool.wait_ge(hn_rstd_ready.sem, hn_rstd_ready.at(b, "headnorm", c=1))
                        pool.tensor_tensor(hn_rstd[:, :], hn_var[:, :], minus_half[:, 0:32], ALU.pow)\
                            .then_inc(hn_rstd_ready.sem, 1)
                    if s in WIDE:
                        add_weights(b, WIDE[s])

        @block.tensor
        def _(pe):
            def mm(out, lhs, rhs, start, stop):
                return pe.matmul(out, lhs, rhs, start=start, stop=stop, skip_group_check=True)

            pe.sem_inc(av_done.sem, 2)
            pe.sem_inc(wide_projected.sem, 2)
            pe.sem_inc(wide_sums.sem, 1)
            pe.wait_ge(const_in, 16 * (N_CONST + 1))
            pe.wait_ge(cond_ready, 1)
            for m in range(N_MOD):
                silu = 6 <= m < 12 or m >= 18
                w = mod_w[:, m, :] if m < N_MOD_FIRST else mod_w_rest[:, m - N_MOD_FIRST, :]
                last = mm(scores[:, 0, m * B:(m + 1) * B], w,
                          cond_silu if silu else cols[:, C_COND:C_COND + B], True, True)
            last.then_inc(mod_full, 1)
            pe.wait_ge(init_done, 2)

            def take_slot(b, phase, j, g=(0, 0), r=None):
                r = j % 2 if r is None else r
                pe.wait_ge(slot_free[r].sem, slot_free[r].at(b, phase, g, j // 2))
                return ring[:, r, :]

            def stored(b, phase, j, g=(0, 0), r=None):
                r = j % 2 if r is None else r
                pe.wait_ge(slot_free[r].sem, slot_free[r].at(b, phase, g, j // 2 + 1))

            def prep(b):
                pe.wait_ge(ctx_in_done.sem, ctx_in_done.at(b, "prep", c=32))
                for j in range(8):
                    if j == 4:
                        pe.wait_ge(ctx_norm_ready.sem, ctx_norm_ready.at(b, "prep", c=1))
                    src = ctx_in if j < 4 else ctx_norm
                    out = take_slot(b, "prep", j)
                    for i, t in enumerate(range(4 * (j % 4), min(4 * (j % 4) + 4, CT))):
                        n = P if t < CT - 1 else LAST
                        last = pe.transpose(out[0:DC, i * P:i * P + n], src[0:n, t, :], ident[0:n, 0:n])
                    last.then_inc(job_full.sem, 1)
                for j in (6, 7):
                    stored(b, "prep", j)

            def gate(b):
                pe.wait_ge(diag_ready.sem, diag_ready.at(b, "gate", c=1))
                out = take_slot(b, "gate", 0, r=1)
                mm(out[:, 0:3 * P], ones[:, :], gate_diag[:, :, :].rearrange("p a d -> p (a d)"), True, True)\
                    .then_inc(job_full.sem, 1)

            def layernorm(b, s):
                pe.wait_ge(xn_ready.sem, xn_ready.at(b, ("ln", s), c=1))
                out = take_slot(b, ("ln", s), 0)
                for q in range(QT):
                    last = pe.transpose(out[:, q * P:(q + 1) * P], xn[:, q, :], ident)
                last.then_inc(job_full.sem, 1)
                stored(b, ("ln", s), 0)

            def headnorm(b):
                out = take_slot(b, "headnorm", 0, r=1)
                for q in range(QT):
                    last = pe.transpose(out[:, q * P:(q + 1) * P], h_t[:, q * P:(q + 1) * P], ident)
                last.then_inc(job_full.sem, 1)
                pe.wait_ge(hn_step.sem, hn_step.at(b, "headnorm", c=5))
                out = take_slot(b, "headnorm", 0)
                flat = hn[:, :, :].rearrange("p (t h) d -> p t (h d)", t=QT)
                for q in range(QT):
                    last = pe.transpose(out[:, q * P:(q + 1) * P], flat[:, q, :], ident)
                last.then_inc(job_full.sem, 1)
                stored(b, "headnorm", 0)

            def source(b, s):
                for j, (k, w) in enumerate(ATT[s].kc):
                    out = take_slot(b, ("src", s), j)
                    mm(out[:, 0:w], src_w[:, ATT[s].src, :], ctx_t[:, k:k + w], True, True).then_inc(job_full.sem, 1)
                for j in (2, 3):
                    stored(b, ("src", s), j)

            def init_y(s, bias):
                for q in range(QT):
                    mm(y_acc[:, q * P:(q + 1) * P], ones[0:1, :], bias, q == 0, False)

            def attention(b, t):
                ph = ("att", t.sub)
                C = len(t.chunks)
                src = src_of(t)
                qsrc = n_t if t.sub == 9 else h_t
                vsrc = h_t if t.sub == 9 else src
                if t.sub >= 9:
                    pe.wait_ge(gated_ready.sem, gated_ready.at(b, "gate", c=1))
                init_y(t.sub, gated_bo[:, :] if t.sub == 10 else rows[:, R_OUT + t.sub * P:R_OUT + (t.sub + 1) * P])

                def weight(g, col, n):
                    if t.wide:
                        return stage[0:n, g[1], col:col + P]
                    i = 2 * g[0] + g[1]
                    base = {SQ: NQ, SK: NK}[col] + i * P
                    return narrow_w[0:n, NARROW_AT[t.sub], base:base + P]

                def job(g, j):
                    kind, i, k = t.jobs[j]
                    u = g[1]
                    if t.wide and j == 0:
                        pe.wait_ge(stage_in[u].sem, stage_in[u].at(b, ph, (g[0], 0), 16))
                    out = take_slot(b, ph, j, g)
                    if kind == "op" and i == 0:
                        if t.wide:
                            for h in range(2):
                                last = mm(out[:, h * N:(h + 1) * N], weight(g, (SQS if k else SQ) + h * P, D),
                                          qsrc[:, :], True, True)
                        else:
                            last = mm(out[:, 0:N], weight(g, SQ, D), qsrc[:, :], True, True)
                    elif kind == "op":
                        a0, w = t.kc[i - 1]
                        last = mm(out[:, 0:w], weight(g, SKS if k else SK, t.dk), src[0:t.dk, a0:a0 + w], True, True)
                    elif kind == "val" and t.wide:
                        t0, nt = t.vjobs[i]
                        for m in range(nt):
                            n = t.rows(t0 + m)
                            last = mm(out[0:n, m * P:(m + 1) * P], src[0:t.dk, (t0 + m) * P:(t0 + m) * P + n],
                                      stage[0:t.dk, u, SV:SV + P], True, True)
                    elif kind == "val":
                        gi = 2 * g[0] + g[1]
                        wv = narrow_w[:, NARROW_AT[t.sub], NV + gi * 32:NV + gi * 32 + 32]
                        if t.vbias:
                            c0 = R_VB + NARROW_AT[t.sub] * P + gi * 32
                            bias = rows[:, c0:c0 + 32].unsqueeze(1).broadcast_to([1, t.kt, 32])
                            mm(out[:, 0:t.kt * 32], ones[0:1, :], bias, True, False)
                        for m in range(t.kt):
                            n = t.rows(m)
                            last = mm(out[0:n, m * 32:(m + 1) * 32], vsrc[:, m * P:m * P + n], wv,
                                      not t.vbias, m == t.kt - 1)
                    else:
                        h, q = i
                        kh = h if t.wide else 0
                        if j == 0 or t.jobs[j - 1][0] != "max":
                            pe.wait_ge(op_ready.sem, op_ready.at(b, ph, g, t.ops))
                        a0, w = t.kc[k]
                        for m, qq in enumerate(range(QT) if q is None else [q]):
                            last = mm(out[:, m * w:(m + 1) * w], qop[:, u, h, qq * P:(qq + 1) * P],
                                      kop[:, u, kh, a0:a0 + w], True, True)
                    last.then_inc(job_full.sem, 1)

                def make_scores(g, c, i):
                    u = g[1]
                    if c == 0 and i == 0:
                        pe.wait_ge(shift_ready.sem, shift_ready.at(b, ph, g, 1))
                    if i == 0:
                        pe.wait_ge(exp_done.sem, exp_done.at(b, ph, g, c - 1))
                    bank = t.chunks[c][i]
                    (h0, k0), (h1, k1) = bank
                    n = t.rows(k0)
                    out = scores[0:n, slot(g, c), i * BANK:(i + 1) * BANK]
                    if h0 == h1:
                        rhs = shift[:, u, h0, :].unsqueeze(1).broadcast_to([P, 2, N])
                    else:
                        rhs = shift[:, u, h0:h0 + 2, :]
                    mm(out, ones_bf[:, 0:n], rhs, True, False)
                    if t.wide:
                        for m, (h, k) in enumerate(bank):
                            for part in range(2):
                                last = mm(out[:, m * N:(m + 1) * N], kop[:, u, h, k * P:k * P + n],
                                          qop[:, u, 2 * part + h, :], False, part == 1)
                    else:
                        last = mm(out, kop[:, u, 0, k0 * P:k0 * P + n], qop[:, u, h0:h0 + 2, :], False, True)
                    if i == len(t.chunks[c]) - 1:
                        last.then_inc(scores_full.sem, 1)

                def slot(g, c):
                    return chunk_slot(t, g, c)

                def weigh_values(g, c, i):
                    u = g[1]
                    if c == 0 and i == 0:
                        stored(b, ph, t.last_val, g)
                        pe.wait_ge(attn_ready.sem, attn_ready.at(b, ph, g, 0))
                    if i == 0:
                        pe.wait_ge(exp_done.sem, exp_done.at(b, ph, g, c + 1))
                    for h, k, block in t.weigh[c][i]:
                        n = t.rows(k)
                        w = probs[0:n, slot(g, c), block * N:(block + 1) * N]
                        if t.wide:
                            vals, to = wide_v[0:n, u, k, h * 64:(h + 1) * 64], o_acc[h * 64:(h + 1) * 64, 0:N]
                        else:
                            vals, to = narrow_v[0:n, u, k, h, :], o_acc[h * 32:(h + 1) * 32, 0:N]
                        last = mm(to, vals, w, k == 0, k == t.kt - 1)
                    if i == len(t.weigh[c]) - 1:
                        last.then_inc(av_done.sem, 1)

                def spread_sums(g):
                    if t.wide:
                        pe.wait_ge(weight_step.sem, weight_step.at(b, ph, g, t.sum_steps(C)))
                        for h in range(2):
                            last = mm(o_acc[h * 64:(h + 1) * 64, N:2 * N], ones[:, 0:64], weight_sum[:, h, :], True, True)
                        last.then_inc(wide_sums.sem, 1)
                    else:
                        pe.wait_ge(o_copied.sem, o_copied.at(b, ph, g, 1))
                        mm(o_acc[:, N:2 * N], sum_row, o_raw[:, :], True, True).then_inc(sums_spread.sem, 1)

                def project(g):
                    u = g[1]
                    if not t.wide:
                        gi = 2 * g[0] + g[1]
                        wo = narrow_w[:, NARROW_AT[t.sub], NO + gi * P:NO + (gi + 1) * P]
                        if t.sub >= 9:
                            wo = gated_wo[:, t.sub - 9, gi, :]
                    else:
                        wo = wo_stage[:, u, :]
                        pe.wait_ge(wo_in[u].sem, wo_in[u].at(b, ph, (g[0], 0), 16))
                    pe.wait_ge(attn_ready.sem, attn_ready.at(b, ph, g, 1))
                    for q in range(QT):
                        last = mm(y_acc[:, q * P:(q + 1) * P], attn[:, u, q * P:(q + 1) * P], wo, False, False)
                    last.then_inc((wide_projected if t.wide else narrow_projected).sem, 1)

                def head(g, c):
                    if g is not None and c < t.head:
                        for i in range(len(t.chunks[c])):
                            make_scores(g, c, i)

                def heads(g):
                    head(g, 0)
                    head(g, 1)

                def first(g, n1):
                    operands_of(t, g, n1, job, heads)

                def pair(g, n1, n2):
                    between(t, -1, n1, n2, job)
                    for n, (kind, c, i) in enumerate(t.steps):
                        (make_scores if kind == "scores" else weigh_values)(g, c, i)
                        between(t, n, n1, n2, job)
                    head(n1, 0)
                    spread_sums(g)
                    head(n1, 1)
                    maxima(t, n2, job)
                    project(g)

                groups(pe, t, first, pair)

            def feed_forward(b, s):
                l = FFN[s]
                ph = ("ff", s)
                bias = rows[:, R_OUT + s * P:R_OUT + (s + 1) * P]
                init_y(s, bias)
                w1 = ff1_w[:, FF1_AT[l]:FF1_AT[l] + (512 if l < 2 else 1024)].rearrange("p (c d) -> p c d", d=P)
                for j in range(2 if l < 2 else 4):
                    out = take_slot(b, ph, j)
                    c0 = 2 * j if l < 2 else 2 * (j // 2) + FF * (j % 2)
                    for m in range(2):
                        last = mm(out[:, m * N:(m + 1) * N], w1[:, c0 + m, :], h_t[:, :], True, True)
                    last.then_inc(job_full.sem, 1)
                if l == 3:
                    pe.wait_ge(gated_ready.sem, gated_ready.at(b, "gate", c=1))
                for c in range(FF):
                    if c % 2 == 0:
                        stored(b, ph, c // 2 if l < 2 else c + 1)
                    w2 = gated_w2[:, c, :] if l == 3 else ff2_w[:, l, c, :]
                    for q in range(QT):
                        last = mm(y_acc[:, q * P:(q + 1) * P], ff_h[:, c, q * P:(q + 1) * P], w2, False, c == FF - 1)
                last.then_inc(ff_done.sem, 1)

            with pe.Fori(0, B) as b:
                prep(b)
                gate(b)
                for s in SUBS:
                    layernorm(b, s)
                    if s == 9:
                        headnorm(b)
                    if s in ATT:
                        if ATT[s].src is not None:
                            source(b, s)
                        attention(b, ATT[s])
                    else:
                        feed_forward(b, s)

        @block.scalar
        def _(act):
            act.sem_inc(exp_done.sem, 2)
            act.sem_inc(stage_used.sem, 2)
            act.wait_ge(const_in, 16 * (N_CONST + 1))
            act.activation(cond_silu, cols[:, C_COND:C_COND + B], ACT.Silu).then_inc(cond_ready, 1)

            def copy(out, src, **kw):
                return act.activation(out, src, ACT.Identity, **kw)

            def prep(b):
                for j in range(8):
                    act.wait_ge(job_full.sem, job_full.at(b, "prep", c=j + 1))
                    dst = (ctx_t if j < 4 else ctx_norm_t)
                    a0 = (j % 4) * BANK
                    w = min(BANK, M - a0)
                    src = ring[0:DC, j % 2, 0:w]
                    if j < 4:
                        last = copy(dst[:, a0:a0 + w], src)
                    else:
                        last = copy(dst[:, a0:a0 + w], src, scale=cols[0:DC, C_CLNW:C_CLNW + 1],
                                    bias=cols[0:DC, C_CLNB:C_CLNB + 1])
                    last.then_inc(slot_free[j % 2].sem, 1)

            def source(b, s):
                t = ATT[s]
                for j, (k, w) in enumerate(t.kc):
                    act.wait_ge(job_full.sem, job_full.at(b, ("src", s), c=j + 1))
                    copy(src_t[:, k:k + w], ring[:, j % 2, 0:w], bias=cols[:, C_SRCB + t.src:C_SRCB + t.src + 1])\
                        .then_inc(slot_free[j % 2].sem, 1)

            def attention(b, t):
                ph = ("att", t.sub)
                C = len(t.chunks)

                def job(g, j):
                    kind, i, k = t.jobs[j]
                    u, r = g[1], j % 2
                    if kind == "max" or (kind == "op" and t.rope and k == 0):
                        return
                    if kind == "op" and t.rope:
                        act.wait_ge(rope_sum.sem, rope_sum.at(b, ph, g, i + 1))
                        if i == 0:
                            last = copy(qop[:, u, 0:2, :].rearrange("p h n -> p (h n)"), raw[:, 0, :])
                        else:
                            a0, w = t.kc[i - 1]
                            v = raw[:, i % 2, 0:w]
                            copy(kop[0:64, u, 0, a0:a0 + w], v[0:64, :])
                            last = copy(kop[64:128, u, 1, a0:a0 + w], v[64:128, :])
                        last.then_inc(rope_high.sem, 1)
                        return
                    act.wait_ge(job_full.sem, job_full.at(b, ph, g, j + 1))
                    if kind == "op":
                        if i == 0:
                            act.wait_ge(op_ready.sem, op_ready.at(b, ph, g, 0))
                        if i >= 2:
                            act.wait_ge(op_ready.sem, op_ready.at(b, ph, g, i - 1))
                        a0, w = (0, 2 * N if t.wide else N) if i == 0 else t.kc[i - 1]
                        out = ring[:, r, 0:w]
                        if t.wide:
                            copy(raw[:, i % 2, 0:w], out)
                            if i == 0:
                                last = copy(qop[:, u, 0:2, :].rearrange("p h n -> p (h n)"), out)
                            else:
                                copy(kop[0:64, u, 0, a0:a0 + w], out[0:64, :])
                                last = copy(kop[64:128, u, 1, a0:a0 + w], out[64:128, :])
                        else:
                            col = (C_QB if i == 0 else C_KB) + NARROW_AT[t.sub] * 4 + 2 * g[0] + g[1]
                            copy(raw[:, i % 2, 0:w], out, bias=cols[:, col:col + 1])
                            last = copy(high[:, i % 2, 0:w], out, bias=cols[:, col:col + 1])
                        last.then_inc(slot_free[r].sem, 1)
                    else:
                        t0, nt = t.vjobs[i]
                        whole = sum(t.rows(t0 + m) == P for m in range(nt))
                        for m0, m1, n in ((0, whole, P), (whole, nt, t.rows(t0 + nt - 1))):
                            if m1 == m0:
                                continue
                            if t.wide:
                                src = ring[0:n, r, m0 * P:m1 * P].rearrange("p (m c) -> p m c", c=P)
                                dst = wide_v[0:n, u, t0 + m0:t0 + m1, :]
                            else:
                                src = ring[0:n, r, m0 * 32:m1 * 32].rearrange("p (m h c) -> p m h c", h=4, c=8)
                                dst = narrow_v[0:n, u, m0:m1, :, 0:8]
                            last = copy(dst, src)
                        last.then_inc(slot_free[r].sem, 1)
                        if t.wide and j == t.last_val:
                            act.sem_inc(stage_used.sem, 1)

                def exps(g, c):
                    act.wait_ge(scores_full.sem, scores_full.at(b, ph, g, c + 1))
                    act.wait_ge(av_done.sem, av_done.at(b, ph, g, c - 1))
                    if t.wide:
                        done = t.sum_steps(c - 1) if c >= 1 else -1
                        act.wait_ge(weight_step.sem, weight_step.at(b, ph, g, done))
                    n = t.rows(t.chunks[c][0][0][1])
                    w = len(t.chunks[c]) * BANK
                    s = chunk_slot(t, g, c)
                    act.activation(probs[0:n, s, 0:w], scores[0:n, s, 0:w], ACT.Exp, scale=t.scale)\
                        .then_inc(exp_done.sem, 1)

                def head(g):
                    if g is not None:
                        for c in range(t.head):
                            exps(g, c)

                def first(g, n1):
                    operands_of(t, g, n1, job, head)

                def pair(g, n1, n2):
                    between(t, -1, n1, n2, job)
                    for n, (kind, c, i) in enumerate(t.steps):
                        if kind == "scores" and i == len(t.chunks[c]) - 1:
                            exps(g, c)
                        between(t, n, n1, n2, job)
                    if not t.wide:
                        act.wait_ge(av_done.sem, av_done.at(b, ph, g, C))
                        copy(o_raw[:, :], o_acc[:, 0:N]).then_inc(o_copied.sem, 1)
                    head(n1)

                groups(act, t, first, pair)

            def feed_forward(b, s):
                l = FFN[s]
                ph = ("ff", s)
                func = [ACT.Gelu, ACT.Gelu_apprx_tanh, ACT.Gelu, ACT.Silu][l]
                for j in range(2) if l < 2 else (0, 2):
                    act.wait_ge(job_full.sem, job_full.at(b, ph, c=j + 1))
                    for m in range(2):
                        c = 2 * j + m if l < 2 else j + m
                        col = C_FFB + l * 8 + c
                        dst = ff_h if l < 2 else ff_g
                        last = act.activation(dst[:, c, :], ring[:, j % 2, m * N:(m + 1) * N], func,
                                              bias=cols[:, col:col + 1])
                    last.then_inc(slot_free[j % 2].sem, 1)

            with act.Fori(0, B) as b:
                prep(b)
                for s in SUBS:
                    if s in ATT:
                        if ATT[s].src is not None:
                            source(b, s)
                        attention(b, ATT[s])
                    else:
                        feed_forward(b, s)

        @block.vector
        def _(dve):
            dve.sem_inc(slot_free[0].sem, 1)
            dve.sem_inc(slot_free[1].sem, 1)
            dve.sem_inc(op_ready.sem, 1)
            dve.sem_inc(attn_ready.sem, 1)
            dve.sem_inc(x_out_ready.sem, 1)
            dve.wait_ge(const_in, 16 * (N_CONST + 1))
            dve.wait_ge(init_done, 2)
            dve.tensor_copy(ident_bf[:, :], ident)

            def wide_cols(c, n):
                return cols[:, c:c + n].unsqueeze(2).broadcast_to([P, n, B])

            by_mod = mod_ab[:, :, :].rearrange("p b m -> p m b")
            dve.wait_ge(mod_full, 1)
            mod_psum = scores[:, 0, 0:N_MOD * B].rearrange("p (m b) -> p m b", b=B)
            dve.tensor_tensor(mod_raw, mod_psum, wide_cols(C_MODB, N_MOD), ALU.add).then_inc(mod_step, 1)
            dve.wait_ge(mod_step, 1)
            dve.tensor_scalar(mod_scale, mod_raw[:, 0:24:2, :], 1.0, None, ALU.add).then_inc(mod_step, 1)
            dve.wait_ge(mod_step, 2)
            dve.tensor_tensor(by_mod[:, 0:24:2, :], mod_scale, wide_cols(C_LNW, 12), ALU.mult)
            dve.tensor_copy(by_mod[:, 24:27, :], mod_raw[:, 24:27, :])
            dve.tensor_tensor(mod_scale, mod_scale, wide_cols(C_LNB, 12), ALU.mult).then_inc(mod_step, 1)
            dve.wait_ge(mod_step, 3)
            dve.tensor_tensor(by_mod[:, 1:24:2, :], mod_scale, mod_raw[:, 1:24:2, :], ALU.add).then_inc(mod_step, 1)
            dve.wait_ge(mod_step, 4)

            def prep(b):
                dve.tensor_copy(ab[:, :], mod_ab[:, b, :]).then_inc(ab_ready.sem, 1)
                dve.wait_ge(x_out_ready.sem, x_out_ready.at(b, "x", c=0))
                dve.wait_ge(x_in_done.sem, x_in_done.at(b, "prep", c=16))
                dve.tensor_copy(x[:, :, :], x_in[:, :, :]).then_inc(x_done.sem, 1)
                dve.wait_ge(ctx_in_done.sem, ctx_in_done.at(b, "prep", c=32))
                tiles = [(t, P if t < CT - 1 else LAST) for t in range(CT)]
                for t, n in tiles:
                    last = dve.bn_stats(ctx_stats[0:n, t, :], ctx_in[0:n, t, :])
                last.then_inc(ctx_stat.sem, 1)
                dve.wait_ge(ctx_stat.sem, ctx_stat.at(b, "prep", c=1))
                dve.sem_inc(waited_dve, 1)
                for t, n in tiles:
                    last = dve.bn_aggr(ctx_mv[0:n, t, :], ctx_stats[0:n, t, :])
                last.then_inc(ctx_mv_ready.sem, 1)
                dve.wait_ge(ctx_mv_ready.sem, ctx_mv_ready.at(b, "prep", c=1))
                dve.wait_ge(ctx_rstd_ready.sem, ctx_rstd_ready.at(b, "prep", c=1))
                for t, n in tiles:
                    last = dve.tensor_scalar(ctx_norm[0:n, t, :], ctx_in[0:n, t, :], ctx_mv[0:n, t, 0:1],
                                             ctx_rstd[0:n, t:t + 1], ALU.subtract, ALU.mult)
                last.then_inc(ctx_norm_ready.sem, 1)

            def gate(b):
                dve.wait_ge(ab_ready.sem, ab_ready.at(b, "prep", c=1))
                dve.tensor_tensor(gate_diag[:, :, :], ident.unsqueeze(1).broadcast_to([P, 3, P]),
                                  ab[:, 24:27].unsqueeze(2).broadcast_to([P, 3, P]), ALU.mult)\
                    .then_inc(diag_ready.sem, 1)
                dve.wait_ge(job_full.sem, job_full.at(b, "gate", c=1))
                dve.tensor_copy(gate_rows[:, :, :], ring[:, 1, 0:3 * P].rearrange("p (a d) -> p a d", a=3))\
                    .then_inc(slot_free[1].sem, 1)
                dve.wait_ge(slot_free[1].sem, slot_free[1].at(b, "gate", c=1))

                def gated(out, w, i):
                    return dve.tensor_tensor(out, w, gate_rows[:, i, :].unsqueeze(1).broadcast_to([P, 4, P]), ALU.mult)

                gated(gated_wo[:, 0, :, :], head_dims, 0)
                gated(gated_wo[:, 1, :, :], narrow_w[:, NARROW_AT[10], NO:NO + 4 * P].rearrange("p (g d) -> p g d", g=4), 1)
                gated(gated_w2[:, :, :], ff2_w[:, 3, :, :], 2)
                dve.tensor_tensor(gated_bo[:, :], rows[:, R_OUT + 10 * P:R_OUT + 11 * P], gate_rows[0:1, 1, :], ALU.mult)\
                    .then_inc(gated_ready.sem, 1)

            def layernorm(b, s):
                ph = ("ln", s)
                dve.wait_ge(x_done.sem, x_done.at(b, "x", c=s + 1))
                for q in range(QT):
                    last = dve.bn_stats(stats[:, q, :], x[:, q, :])
                last.then_inc(stat.sem, 1)
                dve.wait_ge(stat.sem, stat.at(b, ph, c=1))
                dve.sem_inc(waited_dve, 1)
                for q in range(QT):
                    last = dve.bn_aggr(mv[:, q, :], stats[:, q, :])
                last.then_inc(mv_ready.sem, 1)
                dve.wait_ge(mv_ready.sem, mv_ready.at(b, ph, c=1))
                dve.wait_ge(rstd_ready.sem, rstd_ready.at(b, ph, c=1))
                for q in range(QT):
                    last = dve.tensor_scalar(xn[:, q, :], x[:, q, :], mv[:, q, 0:1], rstd[:, q:q + 1],
                                             ALU.subtract, ALU.mult)
                last.then_inc(xn_ready.sem, 1)
                dve.wait_ge(job_full.sem, job_full.at(b, ph, c=1))
                dve.wait_ge(ab_ready.sem, ab_ready.at(b, "prep", c=1))
                dve.tensor_scalar(h_t[:, :], ring[:, 0, 0:N], ab[:, 2 * s:2 * s + 1], ab[:, 2 * s + 1:2 * s + 2],
                                  ALU.mult, ALU.add).then_inc(slot_free[0].sem, 1)

            def headnorm(b):
                def step(n):
                    dve.wait_ge(hn_step.sem, hn_step.at(b, "headnorm", c=n))

                def spread(v):
                    return v[:, :].unsqueeze(2).broadcast_to([P, 32, 8])

                dve.wait_ge(job_full.sem, job_full.at(b, "headnorm", c=1))
                dve.tensor_copy(hn[:, :, :], ring[:, 1, 0:N].rearrange("p (h d) -> p h d", d=8))\
                    .then_inc(slot_free[1].sem, 1)
                dve.wait_ge(slot_free[1].sem, slot_free[1].at(b, "headnorm", c=1))
                dve.tensor_reduce(hn_sum[:, :], hn[:, :, :], AX.X, ALU.add).then_inc(hn_step.sem, 1)
                step(1)
                dve.scalar_tensor_tensor(hn_cen[:, :, :], spread(hn_sum), -1.0 / 8, hn[:, :, :], ALU.mult, ALU.add)\
                    .then_inc(hn_step.sem, 1)
                step(2)
                dve.scalar_tensor_tensor(hn_sq[:, :, :], hn_cen[:, :, :], 1.0 / 8, hn_cen[:, :, :], ALU.mult, ALU.mult)\
                    .then_inc(hn_step.sem, 1)
                step(3)
                dve.tensor_reduce(hn_var[:, :], hn_sq[:, :, :], AX.X, ALU.add).then_inc(hn_step.sem, 1)
                dve.wait_ge(hn_rstd_ready.sem, hn_rstd_ready.at(b, "headnorm", c=2))
                dve.tensor_tensor(hn[:, :, :], hn_cen[:, :, :], spread(hn_rstd), ALU.mult)\
                    .then_inc(hn_step.sem, 1)
                dve.wait_ge(job_full.sem, job_full.at(b, "headnorm", c=2))
                dve.tensor_copy(n_t[:, :], ring[:, 0, 0:N]).then_inc(slot_free[0].sem, 1)

            def attention(b, t):
                ph = ("att", t.sub)
                C = len(t.chunks)
                nq = t.heads * QT
                parts = len(t.kc) if t.cross else 1

                def job(g, j):
                    kind, i, k = t.jobs[j]
                    u, r = g[1], j % 2
                    if t.rope and kind != "op" and t.jobs[j - 1][0] == "op":
                        low_parts(g, t.ops - 1)
                    if kind == "val":
                        return
                    if kind == "max":
                        h, q = i
                        dve.wait_ge(job_full.sem, job_full.at(b, ph, g, j + 1))
                        w = t.kc[k][1]
                        if q is None:
                            src = ring[:, r, 0:QT * w].rearrange("p (q k) -> p q k", q=QT)
                            dst = max_part[:, u, 2 * h:2 * h + 2, 0]
                        else:
                            src, dst = ring[:, r, 0:w], max_part[:, u, 2 * h + q, k:k + 1]
                        dve.tensor_reduce(dst, src, AX.X, ALU.max).then_inc(slot_free[r].sem, 1)
                        return
                    if not t.rope:
                        dve.wait_ge(slot_free[r].sem, slot_free[r].at(b, ph, g, j // 2 + 1))
                        low_parts(g, i)
                        return
                    a0, w = columns(i)
                    v = raw[:, i % 2, 0:w]
                    dve.wait_ge(job_full.sem, job_full.at(b, ph, g, j + 1))
                    if k:
                        dve.wait_ge(rope_sum.sem, rope_sum.at(b, ph, g, i))
                    else:
                        dve.wait_ge(op_ready.sem, op_ready.at(b, ph, g, max(i - 1, 0)))
                    table = rope_sin if k else rope_cos
                    tab, src = table[:, a0:a0 + w], ring[:, r, 0:w]
                    dst = raw_swap[:, 0:w] if k else v
                    if i == 0:
                        tab = table[:, 0:N].unsqueeze(1).broadcast_to([P, 2, N])
                        src = src.rearrange("p (h n) -> p h n", h=2)
                        dst = dst.rearrange("p (h n) -> p h n", h=2)
                    dve.tensor_tensor(dst, src, tab, ALU.mult).then_inc(slot_free[r].sem, 1)
                    if k == 0:
                        return
                    for rr, jj in ((r, j), (1 - r, j - 1)):
                        dve.wait_ge(slot_free[rr].sem, slot_free[rr].at(b, ph, g, jj // 2 + 1))
                    dve.tensor_tensor(v, v, raw_swap[:, 0:w], ALU.add).then_inc(rope_sum.sem, 1)
                    if i >= 1:
                        low_parts(g, i - 1)

                def columns(i):
                    return (0, 2 * N if t.wide else N) if i == 0 else t.kc[i - 1]

                def low_parts(g, i):
                    u = g[1]
                    a0, w = columns(i)
                    v = raw[:, i % 2, 0:w]
                    if t.rope:
                        dve.wait_ge(rope_high.sem, rope_high.at(b, ph, g, i + 1))
                    if t.wide and i == 0:
                        last = dve.tensor_tensor(qop[:, u, 2:4, :].rearrange("p h n -> p (h n)"), v,
                                                 qop[:, u, 0:2, :].rearrange("p h n -> p (h n)"), ALU.subtract)
                    elif t.wide:
                        dve.tensor_tensor(kop[64:128, u, 0, a0:a0 + w], v[0:64, :], kop[0:64, u, 0, a0:a0 + w],
                                          ALU.subtract)
                        last = dve.tensor_tensor(kop[0:64, u, 1, a0:a0 + w], v[64:128, :],
                                                 kop[64:128, u, 1, a0:a0 + w], ALU.subtract)
                    elif i == 0:
                        dve.scalar_tensor_tensor(qsplit[:, :], high[:, 0, 0:w], cols[:, C_NEGQ:C_NEGQ + 1], v,
                                                 ALU.mult, ALU.add).then_inc(q_split.sem, 1)
                        dve.wait_ge(q_split.sem, q_split.at(b, ph, g, 1))
                        for h in range(4):
                            last = dve.tensor_scalar(qop[:, u, h, :], qsplit[:, :], cols[:, C_HEAD + h:C_HEAD + h + 1],
                                                     None, ALU.mult)
                    else:
                        last = dve.scalar_tensor_tensor(kop[:, u, 0, a0:a0 + w], high[:, i % 2, 0:w],
                                                        cols[:, C_NEGK:C_NEGK + 1], v, ALU.mult, ALU.add)
                    last.then_inc(op_ready.sem, 1)

                def shifts(g):
                    u = g[1]
                    j = t.last_max
                    dve.wait_ge(slot_free[j % 2].sem, slot_free[j % 2].at(b, ph, g, j // 2 + 1))
                    dve.tensor_reduce(max_neg[:, u, 0:nq], max_part[:, u, 0:nq, 0:parts], AX.X, ALU.max, negate=True)\
                        .then_inc(max_ready.sem, 1)
                    dve.wait_ge(max_ready.sem, max_ready.at(b, ph, g, 1))
                    dve.tensor_tensor(shift[:, u, 0:t.heads, :].rearrange("p h (q k) -> p (h q) k", q=QT),
                                      ident_bf[:, :].unsqueeze(1).broadcast_to([P, nq, P]),
                                      max_neg[:, u, 0:nq].unsqueeze(2).broadcast_to([P, nq, P]), ALU.mult)\
                        .then_inc(shift_ready.sem, 1)

                def normalise(g):
                    u = g[1]
                    if t.wide:
                        dve.wait_ge(wide_sums.sem, wide_sums.at(b, ph, g, 1))
                        dve.reciprocal(o_inv[:, :], o_acc[:, N:2 * N]).then_inc(inv_ready.sem, 1)
                        dve.wait_ge(inv_ready.sem, inv_ready.at(b, ph, g, 1))
                        dve.tensor_tensor(attn[:, u, :], o_acc[:, 0:N], o_inv[:, :], ALU.mult).then_inc(attn_ready.sem, 1)
                    else:
                        dve.wait_ge(sums_spread.sem, sums_spread.at(b, ph, g, 1))
                        dve.reciprocal(o_inv[:, :], o_acc[:, N:2 * N]).then_inc(inv_ready.sem, 1)
                        dve.wait_ge(inv_ready.sem, inv_ready.at(b, ph, g, 1))
                        dve.tensor_tensor(attn[:, u, :], o_raw[:, :], o_inv[:, :], ALU.mult).then_inc(attn_ready.sem, 1)

                def first(g, n1):
                    operands_of(t, g, n1, job, shifts)
                    if not t.cross:
                        shifts(n1)

                def pair(g, n1, n2):
                    for n in range(-1, len(t.steps)):
                        between(t, n, n1, n2, job)
                    if t.cross and n1 is not None:
                        shifts(n1)
                    normalise(g)
                    if not t.cross and n2 is not None:
                        maxima(t, n2, job)
                        shifts(n2)

                groups(dve, t, first, pair)
                projected = wide_projected if t.wide else narrow_projected
                dve.wait_ge(projected.sem, projected.at(b, ph, (t.groups // 2 - 1, 1), 1))
                add_y(b, t.sub)

            def add_y(b, s):
                y = y_acc[:, 0:QT * D].rearrange("p (q d) -> p q d", q=QT)
                if s == SUBS[-1]:
                    dve.wait_ge(x_out_free.sem, x_out_free.at(b, "x", c=0))
                    dve.tensor_tensor(x_out[:, :, :], x[:, :, :], y, ALU.add).then_inc(x_out_ready.sem, 1)
                else:
                    dve.tensor_tensor(x[:, :, :], x[:, :, :], y, ALU.add).then_inc(x_done.sem, 1)

            def feed_forward(b, s):
                l = FFN[s]
                ph = ("ff", s)
                if l >= 2:
                    for j in (1, 3):
                        dve.wait_ge(job_full.sem, job_full.at(b, ph, c=j + 1))
                        dve.wait_ge(slot_free[0].sem, slot_free[0].at(b, ph, c=j // 2 + 1))
                        for m in range(2):
                            c = j - 1 + m
                            col = C_FFB + l * 8 + FF + c
                            last = dve.scalar_tensor_tensor(ff_h[:, c, :], ring[:, 1, m * N:(m + 1) * N],
                                                            cols[:, col:col + 1], ff_g[:, c, :], ALU.add, ALU.mult)
                        last.then_inc(slot_free[1].sem, 1)
                dve.wait_ge(ff_done.sem, ff_done.at(b, ph, c=1))
                add_y(b, s)

            with dve.Fori(0, B) as b:
                prep(b)
                gate(b)
                for s in SUBS:
                    layernorm(b, s)
                    if s == 9:
                        headnorm(b)
                    if s in ATT:
                        attention(b, ATT[s])
                    else:
                        feed_forward(b, s)


def chunk_slot(t, g, c):
    return (c + g[1] * len(t.chunks)) % 2



def _pad(w, n):
    import numpy as np
    out = np.zeros((n, *w.shape[1:]), np.float32)
    out[:w.shape[0]] = w
    return out


def _swapped(w):
    return w.reshape(w.shape[0], -1, 2)[:, :, ::-1].reshape(w.shape)


def _wide_blob(wq, wk, wv, wo, rope):
    import numpy as np
    out = np.zeros((H // 2, P, STAGE if rope else SQS + P), np.float32)
    for g in range(H // 2):
        pair = slice(g * P, (g + 1) * P)

        def twice(w, at):
            for h in range(2):
                one = w[:, g * P + h * 64:g * P + (h + 1) * 64]
                out[g, :, at + h * P:at + h * P + 64] = one
                out[g, :, at + h * P + 64:at + (h + 1) * P] = one

        twice(wq, SQ)
        out[g, 0:wk.shape[0], SK:SK + P] = wk[:, pair]
        out[g, 0:wv.shape[0], SV:SV + P] = wv[:, pair]
        out[g, :, -P:] = wo[pair, :]
        if rope:
            twice(_swapped(wq), SQS)
            out[g, 0:wk.shape[0], SKS:SKS + P] = _swapped(wk)[:, pair]
    return out


def _spread(w):
    import numpy as np
    lead = w.shape[:-1]
    v = w.reshape(*lead, 4, 4, 1, 8)
    return np.broadcast_to(v, (*lead, 4, 4, 4, 8)).reshape(*lead, 4, P)


def kernel(**inputs):
    import numpy as np
    import concourse.bacc as bacc
    from concourse.bass_utils import run_bass_kernel_spmd

    i = {k: np.asarray(v) for k, v in inputs.items()}

    def w(layer, name):
        return i[f"L{layer}_xcond_{name}"]

    f32 = np.float32
    l1w, l1b = np.split(w(1, "W_ada"), 6, axis=1), np.split(w(1, "b_ada"), 6)
    l3w, l3b = np.split(w(3, "adaln_w").T, 9, axis=1), np.split(w(3, "adaln_b"), 9)
    mods = [(w(0, "g1_w"), w(0, "g1_b")), (w(0, "b1_w"), w(0, "b1_b"))] * 2
    mods += [(w(0, "g2_w"), w(0, "g2_b")), (w(0, "b2_w"), w(0, "b2_b"))]
    for n in range(3):
        mods += [(l1w[2 * n + 1], l1b[2 * n + 1]), (l1w[2 * n], l1b[2 * n])]
    for n in range(1, 4):
        for half in range(2):
            mods.append((w(2, f"n{n}_w")[:, half * P:(half + 1) * P], w(2, f"n{n}_b")[half * P:(half + 1) * P]))
    for n in range(3):
        mods += [(l3w[3 * n + 1], l3b[3 * n + 1]), (l3w[3 * n], l3b[3 * n])]
    mods += [(l3w[3 * n + 2], l3b[3 * n + 2]) for n in range(3)]

    zero, zeros, eye = np.zeros(P, f32), np.zeros((P, P), f32), np.eye(P, dtype=f32)
    qkv, qkv_b = w(1, "W_qkv"), w(1, "b_qkv")
    ca, ca_b = w(3, "ca_in_w").T, w(3, "ca_in_b")

    def on_diagonal(v):
        out = np.zeros((P, P), f32)
        out[np.arange(P), np.arange(P)] = np.tile(v, H)
        return out

    narrow = [
        (qkv[:, 0:P], qkv_b[0:P], qkv[:, P:2 * P], qkv_b[P:2 * P], qkv[:, 2 * P:], qkv_b[2 * P:], w(1, "W_proj")),
        (w(1, "W_q"), zero, w(1, "W_k"), zero, w(1, "W_v"), zero, w(1, "W_out")),
        (on_diagonal(w(3, "qn_w")), np.tile(w(3, "qn_b"), H), on_diagonal(w(3, "kn_w")), np.tile(w(3, "kn_b"), H),
         eye, zero, zeros),
        (ca[:, 0:P], ca_b[0:P], ca[:, P:2 * P], ca_b[P:2 * P], ca[:, 2 * P:], ca_b[2 * P:], w(3, "ca_out_w").T),
    ]

    cols = np.zeros((P, C_END), f32)
    for m, (_, bias) in enumerate(mods):
        cols[:, C_MODB + m] = bias
    cols[:, C_LNW:C_LNW + 12] = 1
    for s, n in ((0, 1), (1, 1), (2, 2)):
        cols[:, C_LNW + s], cols[:, C_LNB + s] = w(0, f"ln{n}_w"), w(0, f"ln{n}_b")
    cols[0:DC, C_CLNW], cols[0:DC, C_CLNB] = w(0, "ca_lnc_w"), w(0, "ca_lnc_b")
    cols[:, C_SRCB], cols[:, C_SRCB + 1] = w(1, "b_ctx"), w(3, "cond_b")
    half = FF * P
    b_ff2 = w(2, "ff_b1")
    for l, bias in ((0, w(0, "ff_b1")), (1, w(1, "b_fc1")), (2, np.concatenate([b_ff2[half:], b_ff2[:half]]))):
        cols[:, C_FFB + l * 8:C_FFB + l * 8 + len(bias) // P] = bias.reshape(-1, P).T
    for n, (_, bq, _, bk, _, _, _) in enumerate(narrow):
        cols[:, C_QB + 4 * n:C_QB + 4 * n + 4] = _spread(bq).T
        cols[:, C_KB + 4 * n:C_KB + 4 * n + 4] = _spread(bk).T
    r = np.arange(P)
    cols[(r // 8) % 2 == 1, C_NEGK] = -1
    cols[(r // 8) % 4 >= 2, C_NEGQ] = -1
    for h in range(4):
        cols[r // 32 == h, C_HEAD + h] = 1
    cols[:, C_COND:C_COND + B] = i["cond_1024"].T

    rows = np.zeros((1, R_END), f32)
    outs = {0: w(0, "sa_bo"), 1: w(0, "ca_bo"), 2: w(0, "ff_b2"), 3: w(1, "b_proj"), 4: w(1, "b_out"), 5: w(1, "b_fc2"),
            6: w(2, "o1_b"), 7: w(2, "o2_b"), 8: w(2, "ff_b2"), 10: w(3, "ca_out_b")}
    for s, bias in outs.items():
        rows[0, R_OUT + s * P:R_OUT + (s + 1) * P] = bias
    for n, one in enumerate(narrow):
        rows[0, R_VB + n * P:R_VB + (n + 1) * P] = one[5]

    squares = np.zeros((P, K_END), f32)
    squares[:, K_ID:K_ID + P] = eye
    for h in range(4):
        squares[32 * h + 8, K_SEL + 32 * h:K_SEL + 32 * h + 32] = 1
        for g in range(4):
            for d in range(8):
                squares[32 * h + d, K_SELP + g * P + (4 * g + h) * 8 + d] = 1

    narrow_w = np.zeros((P, 4, NCOLS), f32)
    for n, (wq, _, wk, _, wv, _, wo) in enumerate(narrow):
        narrow_w[:, n, NQ:NQ + 4 * P] = _spread(wq).reshape(P, -1)
        narrow_w[:, n, NK:NK + 4 * P] = _spread(wk).reshape(P, -1)
        narrow_w[:, n, NV:NV + P] = wv
        for g in range(4):
            for h in range(4):
                narrow_w[32 * h:32 * h + 8, n, NO + g * P:NO + (g + 1) * P] = wo[(4 * g + h) * 8:(4 * g + h) * 8 + 8]

    inv = (f32(1.0) / f32(10000.0) ** (np.arange(0, 64, 2, dtype=f32) / f32(64))).astype(f32)
    angle = np.arange(M, dtype=f32)[None, :] * inv[(r % 64) // 2][:, None]
    rope_sin = np.sin(angle).astype(f32)
    rope_sin[r % 2 == 0] = -rope_sin[r % 2 == 0]

    ff2 = [w(0, "ff_w2"), w(1, "W_fc2"), w(2, "ff_w2"), w(3, "w2").T]
    g2 = w(2, "ff_w1")
    wkv0, ckv0 = w(0, "sa_wkv"), w(0, "ca_wkv")
    mid = H * 64
    arrays = {
        "x": i["x"], "ctx": i["ctx_768"], "cols": cols, "rows": rows, "squares": squares,
        "mod_w": np.concatenate([m for m, _ in mods], axis=1),
        "rope_cos": np.cos(angle).astype(f32), "rope_sin": rope_sin,
        "narrow_w": narrow_w.reshape(P, -1),
        "src_w": np.concatenate([w(1, "W_ctx"), w(3, "cond_w").T], axis=1),
        "ff1_w": np.concatenate([w(0, "ff_w1"), w(1, "W_fc1"), g2[:, half:], g2[:, :half], w(3, "w1").T, w(3, "w3").T], axis=1),
        "ff2_w": np.stack([m.reshape(FF, P, P).transpose(1, 0, 2) for m in ff2], axis=1).reshape(P, -1),
        "wide0": _wide_blob(w(0, "sa_wq"), wkv0[:, :mid], wkv0[:, mid:], w(0, "sa_wo"), True),
        "wide1": _wide_blob(w(0, "ca_wq"), ckv0[:, :mid], ckv0[:, mid:], w(0, "ca_wo"), True),
        "wide6": _wide_blob(w(2, "q1"), w(2, "k1"), w(2, "v1"), w(2, "o1_w"), False),
        "wide7": _wide_blob(w(2, "q2"), w(2, "k2"), w(2, "v2"), w(2, "o2_w"), False),
    }
    arrays = {k: np.ascontiguousarray(v) for k, v in arrays.items()}
    nc = bacc.Bacc("TRN2", target_bir_lowering=False, num_devices=1)
    drams = {k: nc.dram_tensor(f"in_{k}", v.shape, mybir.dt.from_np(v.dtype), kind="ExternalInput").ap()
             for k, v in arrays.items()}
    drams["out"] = nc.dram_tensor("out", (B, N, D), F32, kind="ExternalOutput").ap()
    build(nc, drams)
    got = run_bass_kernel_spmd(nc, [{f"in_{k}": v for k, v in arrays.items()}], core_ids=[0])
    return got.results[0]["out"]
```

```python
from contextlib import ExitStack

import concourse.bass as bass
from concourse import mybir

F32 = mybir.dt.float32
BF16 = mybir.dt.bfloat16
F16 = mybir.dt.float16
ALU = mybir.AluOpType
ACT = mybir.ActivationFunctionType
AX = mybir.AxisListType

P = 128
B, N, D = 8, 256, 128
M, DC = 1601, 96
H = 16
QT = N // P
CT = -(-M // P)
LAST = M - (CT - 1) * P
MP = CT * P
FF = 4
BANK = 512
RING, SCORES, PROBS = 3, 3, 4
EPS0, EPS1 = 1e-5, 1e-6


class Attention:

    def __init__(self, sub, wide, cross, rope=False, src=None, vbias=False):
        self.sub, self.wide, self.cross, self.rope = sub, wide, cross, rope
        self.src, self.vbias = src, vbias
        self.heads = 2 if wide else 4
        self.units = 2 * (H // self.heads)
        self.keys = M if cross else N
        self.kt = -(-self.keys // P)
        self.scale = float((64 if wide else 8) ** -0.5)
        self.dk = DC if (cross and wide) else D
        pieces = -(-self.keys // BANK)
        cuts = [-(-self.keys * i // pieces) for i in range(pieces + 1)]
        self.kc = [(a, b - a) for a, b in zip(cuts, cuts[1:])]
        self.fold = cross and not wide
        self.ahead = not (cross and wide)
        jobs = []
        for o in range(1 + len(self.kc)):
            jobs.append(("op", o, 0))
            if rope:
                jobs.append(("op", o, 1))
        self.ops = 1 + len(self.kc)
        per = 4 if cross or not wide else 1
        self.vjobs = [(t, min(per, self.kt - t)) for t in range(0, self.kt, per)]
        vals = [("val", v, 0) for v in range(len(self.vjobs))] if wide else []
        if cross:
            maxima = [("max", (h, q), k) for h in range(self.heads) for q in range(QT) for k in range(len(self.kc))]
        else:
            maxima = [("max", (h, None), 0) for h in range(self.heads)]
        if self.fold:
            maxima.append(("shift", 0, 0))
        jobs += maxima + vals if self.ahead else vals + maxima
        self.jobs = jobs
        kinds = [kind for kind, _, _ in jobs]
        self.last_max = len(kinds) - 1 - kinds[::-1].index("max")
        self.first_max = kinds.index("max")
        self.last_val = len(kinds) - 1 - kinds[::-1].index("val") if wide else None
        self.shift_job = kinds.index("shift") if self.fold else None
        pairs = [(h, h + 1) for h in range(0, self.heads, 2)]
        self.chunks = [[(h, t) for h in pair] for t in range(self.kt) for pair in pairs]
        self.per_tile = len(pairs)
        self.late = 0 if not cross else 2
        self.weigh = [[(h, c, m) for c in range(t * self.per_tile, (t + 1) * self.per_tile)
                       for m, (h, _) in enumerate(self.chunks[c])] for t in range(self.kt)]
        self.head = made = min(SCORES, len(self.chunks))
        self.steps = []
        for t in range(self.kt):
            self.steps.append(("values", t))
            upto = min((t + 1) * self.per_tile + SCORES, len(self.chunks))
            self.steps += [("scores", c) for c in range(made, upto)]
            made = max(made, upto)

    def last_like(self, c, slots):
        return len(self.chunks) - 1 - (len(self.chunks) - 1 - c) % slots

    def tiles_of(self, c):
        return c // self.per_tile + 1

    def cost(self, kind, i, k):
        if kind == "val":
            return 500
        if self.fold and kind == "op":
            return 400
        if kind == "max":
            return self.kc[k][1] if self.cross else BANK
        if kind == "shift":
            return 500
        w = (2 * N if self.wide else N) if i == 0 else self.kc[i - 1][1]
        if self.rope:
            return 4 * w if k else w
        return 2 * w

    def last_unit(self, u):
        n = self.units - 2 + u
        return n // 4, n % 4

    def rows(self, t):
        return min(P, self.keys - t * P)

    def sum_steps(self, c):
        return max(c, 1)

    def slot_uses(self, r):
        return len(self.jobs[r::RING])


WIDE = {0: Attention(0, True, False, rope=True), 1: Attention(1, True, True, rope=True),
        6: Attention(6, True, False), 7: Attention(7, True, True)}
NARROW = {3: Attention(3, False, False, vbias=True), 4: Attention(4, False, True, src=0),
          9: Attention(9, False, False), 10: Attention(10, False, True, src=1, vbias=True)}
ATT = {**WIDE, **NARROW}
FFN = {2: 0, 5: 1, 8: 2, 11: 3}
END = 12
NARROW_AT = {s: i for i, s in enumerate(NARROW)}
ATTS = [ATT[s] for s in sorted(ATT)]


def prelude(s):
    out = []
    if s == 1:
        out += [("ctx", s, j) for j in range(8)] + [("gate", s, 0)]
    if s in ATT and ATT[s].src is not None:
        out += [("src", s, j) for j in range(len(ATT[s].kc))]
        out += [("val", s, j) for j in range(len(ATT[s].vjobs))]
    if s - 1 in FFN:
        hidden = 2 if FFN[s - 1] < 2 else 4
        out += [("ln", s - 1, 0)] + [("ff", s - 1, j) for j in range(hidden)] + [("ffout", s - 1, 0)]
    if s != END:
        out.append(("ln", s, 0))
    if s in NARROW and not NARROW[s].cross:
        out += [("val", s, j) for j in range(len(NARROW[s].vjobs))]
    if s == 9:
        out += [("hn", s, 0), ("hn", s, 1)]
    return out


LATENCY = {"ctx": 700, "gate": 700, "src": 500, "val": 900, "ln": 5000, "ff": 1200, "ffout": 1500, "hn": 4000}


def spread_over(t, costs):
    steps = len(t.steps)
    n = max(1, steps - (5 if not t.ahead else 1))
    total, at, due = sum(c for c, _ in costs), 0, []
    for c, wait in costs:
        due.append(at + wait)
        at += c
    cuts = [sum(d < total * i / n for d in due) for i in range(1, n)]
    return cuts + [len(costs)] * (steps - n + 1)


SQ, SK, SV, SQS, SKS, SO = 0, 256, 384, 512, 768, 896
STAGE = SO + P

NQ, NK, NO, NV = 0, 4 * P, 8 * P, 12 * P
NCOLS = 12 * P + 4 * 32

N_MOD = 27
C_MODB = 0
C_LNW = C_MODB + N_MOD
C_LNB = C_LNW + 12
C_CLNW = C_LNB + 12
C_CLNB = C_CLNW + 1
C_SRCB = C_CLNB + 1
C_FFB = C_SRCB + 2
C_QB = C_FFB + 4 * 8
C_KB = C_QB + 16
C_NEGK = C_KB + 16
C_NEGQ = C_NEGK + 1
C_HEAD = C_NEGQ + 1
C_COND = C_HEAD + 4
C_END = C_COND + B

R_OUT = 0
R_VB = 12
R_END = 16
R_PARTS = (0, 32, 64)
R_COLS = -(-R_END // 3) * P


K_ID, K_SEL, K_PART = 0, P, 2 * P
K_END = 3 * P
SHIFT = 64.0

FF1_AT = [0, 512, 1024, 2048]
FF1_COLS = 3072


class Count:

    def __init__(self, sem, of, credit=0):
        self.sem, self.credit = sem, credit
        self.base, self.inc, self.gap, total = {}, {}, {}, 0
        for t in ATTS:
            s = t.sub
            pre, att = of(("pre", s, 0)), of(("att", s))
            self.base["pre", s, 0], self.base["att", s] = total, total + pre
            self.base["pre", s, 1] = total + pre + att
            self.inc["att", s], self.gap["att", s] = att, of(("pre", s, 1))
            total += pre + t.units * att + self.gap["att", s]
        for u in range(2):
            self.base["pre", END, u] = total
            total += of(("pre", END, u))
        self.total = total

    def pre(self, b, s, u, c):
        return b * self.total + (self.base["pre", s, u] + c + self.credit)

    def at(self, b, t, g, c=0):
        i, v = g
        ph = ("att", t.sub)
        inc = self.inc[ph]
        fixed = self.base[ph] + v * inc + c + self.credit
        if not isinstance(i, int):
            return b * self.total + i * (4 * inc) + (fixed + self.gap[ph])
        return b * self.total + (fixed + 4 * i * inc + (self.gap[ph] if (i, v) != (0, 0) else 0))


def build(nc, a):
    with ExitStack() as ctx:
        def sb(name, shape, dt=F32):
            return ctx.enter_context(nc.sbuf_tensor(name, shape, dt))

        def psum(name, shape):
            return ctx.enter_context(nc.psum_tensor(name, shape, F32))

        def sem(name):
            return ctx.enter_context(nc.semaphore(name))

        cols = sb("cols", [P, C_END])
        rows = sb("rows", [R_PARTS[-1] + 1, R_COLS])
        squares = sb("squares", [P, K_END])
        ident = squares[:, K_ID:K_ID + P]
        ident_part = squares[:, K_PART:K_PART + P]
        sum_row = squares[:, K_SEL:K_SEL + P]
        ones = sb("ones", [P, P])
        ones_bf = sb("ones_bf", [P, P], BF16)
        ident_bf = sb("ident_bf", [P, P], BF16)
        minus_half = sb("minus_half", [P, 32])
        eps0 = sb("eps0", [P, CT])
        eps1 = sb("eps1", [P, 32])
        rope_cos = sb("rope_cos", [P, M])
        rope_sin = sb("rope_sin", [P, M])
        narrow_w = sb("narrow_w", [P, 4, NCOLS])
        src_w = sb("src_w", [DC, 2, P])
        ff1_w = sb("ff1_w", [P, FF1_COLS])
        ff2_w = sb("ff2_w", [P, 4, FF, P])
        mod_ab = sb("mod_ab", [P, B // 2, 2, N_MOD])
        x_in = sb("x_in", [P, 2, QT, D])
        ctx_in = sb("ctx_in", [P, 2, CT, DC])
        x = sb("x", [P, 2, QT, D])
        x_out = sb("x_out", [P, 2, QT, D])
        ab = sb("ab", [P, 2, N_MOD])
        gate_rows = sb("gate_rows", [P, 2, 3, P])
        ctx_t = sb("ctx_t", [DC, 2, MP])
        src_t = sb("src_t", [P, 2, MP])
        ctx_stats = sb("ctx_stats", [P, CT, 6])
        ctx_mv = sb("ctx_mv", [P, CT, 2])
        ctx_var = sb("ctx_var", [P, CT])
        ctx_rstd = sb("ctx_rstd", [P, CT])
        stats = sb("stats", [P, QT, 6])
        mv = sb("mv", [P, QT, 2])
        var = sb("var", [P, QT])
        rstd = sb("rstd", [P, QT])
        xn = sb("xn", [P, QT, D])
        h_t = sb("h_t", [D, 2, N])
        hn_sum = sb("hn_sum", [P, 32])
        hn_var = sb("hn_var", [P, 32])
        hn_rstd = sb("hn_rstd", [P, 32])
        n_t = sb("n_t", [D, 2, N])
        stage = sb("stage", [P, 2, SO])
        wo_stage = sb("wo_stage", [P, 2, P])
        kop = sb("kop", [P, 2, 2, MP], F16)
        qop = sb("qop", [P, 4, 4, N], F16)
        qsplit = sb("qsplit", [P, N], F16)
        wide_v = sb("wide_v", [P, 2, CT, P])
        weight_sum = sb("weight_sum", [P, 2, N])
        narrow_v = sb("narrow_v", [P, 2, CT, 4, 32])
        raw = sb("raw", [P, 2, BANK])
        raw_swap = sb("raw_swap", [P, BANK])
        max_part = sb("max_part", [P, 2, 8, 4])
        max_neg = sb("max_neg", [P, 2, 8])
        shift = sb("shift", [P, 2, 4, N], BF16)
        max_cols = sb("max_cols", [P, QT, P])
        probs = sb("probs", [P, PROBS, BANK])
        o_raw = sb("o_raw", [P, N])
        o_inv = sb("o_inv", [P, N])
        attn = sb("attn", [P, 2, N])
        ff_h = sb("ff_h", [P, FF, N])
        ff_g = sb("ff_g", [P, FF, N])

        high = raw_swap[:, :].bitcast(F16).rearrange("p (s k) -> p s k", s=2)
        ff_h_flat = ff_h[:, :, :].rearrange("p f n -> p (f n)")
        ff_g_flat = ff_g[:, :, :].rearrange("p f n -> p (f n)")
        gate_diag = ff_g_flat[:, 0:3 * P].rearrange("p (a d) -> p a d", a=3)
        hn = ff_h_flat[:, 0:N].rearrange("p (h d) -> p h d", d=8)
        hn_cen = ff_g_flat[:, 0:N].rearrange("p (h d) -> p h d", d=8)
        hn_sq = ff_g_flat[:, N:2 * N].rearrange("p (h d) -> p h d", d=8)

        scores = psum("scores", [P, SCORES, BANK])
        ring = psum("ring", [P, RING, BANK])
        o_acc = psum("o_acc", [P, BANK])
        y_acc = psum("y_acc", [P, 2, N])

        mod_w = wide_v[:, :, :, :].rearrange("p u t c -> p (u t) c")
        mod_w_rest = attn[:, :, :].rearrange("p u (t c) -> p (u t) c", c=P)
        N_MOD_FIRST = 2 * CT
        cond_silu = o_raw[:, 0:B]
        mod_flat = mod_ab[:, :, :, :].rearrange("p b u m -> p (b u) m")
        mod_raw = ff_h_flat[:, 0:N_MOD * B].rearrange("p (m b) -> p m b", b=B)
        mod_scale = ff_g_flat[:, 0:12 * B].rearrange("p (m b) -> p m b", b=B)

        def units(per):
            def of(p):
                return per(ATT[p[1]]) if p[0] == "att" else 0
            return of

        def steps(kind, n=1, step=None):
            def of(p):
                if p[0] == "att":
                    return 0
                return n * sum(k == kind and step in (None, j) for k, _, j in prelude(p[1]))
            return of

        def ring_jobs(r):
            def of(p):
                if p[0] == "att":
                    return ATT[p[1]].slot_uses(r)
                return len(prelude(p[1])[r::RING])
            return of

        def pass_end(n):
            return lambda p: n if p == ("pre", END, 1) else 0

        def count(name, of, credit=0):
            return Count(sem(name), of, credit)

        job_full = count("job_full", lambda p: sum(ring_jobs(r)(p) for r in range(RING)))
        slot_free = [count(f"slot_free{r}", ring_jobs(r), 1) for r in range(RING)]
        op_ready = count("op_ready", units(lambda t: t.ops), 1)
        rope_sum = count("rope_sum", units(lambda t: t.ops if t.rope else 0), 1)
        rope_high = count("rope_high", units(lambda t: t.ops if t.rope else 0))
        q_split = count("q_split", units(lambda t: 0 if t.wide else 1))
        values_set = count("values_set", units(lambda t: 0 if t.wide else 1))
        max_ready = count("max_ready", units(lambda t: 1))
        shift_ready = count("shift_ready", units(lambda t: 0 if t.fold else 1))
        scores_full = count("scores_full", units(lambda t: len(t.chunks)))
        exp_done = count("exp_done", units(lambda t: len(t.chunks)), 1)
        av_done = count("av_done", units(lambda t: t.kt), 1)
        o_copied = count("o_copied", units(lambda t: 1), 1)
        sums_spread = count("sums_spread", units(lambda t: 0 if t.wide else 1))
        inv_ready = count("inv_ready", units(lambda t: 1))
        attn_ready = count("attn_ready", units(lambda t: 1), 1)
        weight_step = count("weight_step", units(lambda t: t.sum_steps(t.kt - 1) if t.wide else 0), 1)
        wide_sums = count("wide_sums", units(lambda t: 1 if t.wide else 0), 1)
        wide_projected = count("wide_projected", units(lambda t: 1 if t.wide else 0), 3)
        stage_used = count("stage_used", units(lambda t: 1 if t.wide else 0), 3)
        narrow_projected = count("narrow_projected", units(lambda t: 0 if t.wide else 1))
        stage_in = [count(f"stage_in{w}", units(lambda t: 4 if t.wide else 0)) for w in range(2)]
        wo_in = [count(f"wo_in{w}", units(lambda t: 4 if t.wide else 0)) for w in range(2)]
        x_in_done = count("x_in_done", pass_end(32))
        ctx_in_done = count("ctx_in_done", pass_end(64))
        x_done = count("x_done", lambda p: int(p[0] == "pre"))
        y_gated = count("y_gated", lambda p: {10: 1, END: 1}.get(p[1], 0) if p[0] == "pre" else 0)
        x_out_ready = count("x_out_ready", lambda p: int(p[:2] == ("pre", END)), 2)
        x_out_sent = count("x_out_sent", lambda p: 16 * (p[:2] == ("pre", END)))
        x_out_free = count("x_out_free", lambda p: int(p[:2] == ("pre", END)), 2)
        ab_ready = count("ab_ready", lambda p: int(p == ("pre", 0, 0)))
        ctx_stat = count("ctx_stat", steps("ctx", 1, 0))
        ctx_mv_ready = count("ctx_mv_ready", steps("ctx", 1, 0))
        ctx_var_ready = count("ctx_var_ready", steps("ctx", 1, 0))
        ctx_rstd_ready = count("ctx_rstd_ready", steps("ctx", 1, 0))
        ctx_norm_ready = count("ctx_norm_ready", steps("ctx", 1, 0))
        stat = count("stat", steps("ln"))
        mv_ready = count("mv_ready", steps("ln"))
        var_ready = count("var_ready", steps("ln"))
        rstd_ready = count("rstd_ready", steps("ln"))
        xn_ready = count("xn_ready", steps("ln"))
        diag_ready = count("diag_ready", steps("gate"))
        hn_step = count("hn_step", steps("hn", 5, 0))
        hn_rstd_ready = count("hn_rstd_ready", steps("hn", 2, 0))
        const_in = sem("const_in")
        init_done = sem("init_done")
        cond_ready = sem("cond_ready")
        mod_full = sem("mod_full")
        mod_step = sem("mod_step")
        waited_sp, waited_dve = sem("waited_sp"), sem("waited_dve")
        N_CONST = 10

        block = ctx.enter_context(nc.Block())

        def unit(t, n):
            return (n // 4, n % 4) if 0 <= n < t.units else None

        def is_first(g):
            return isinstance(g[0], int) and tuple(g) == (0, 0)

        def pre_items(s, u):
            return [("pre", s, u, m) for m in range(len(prelude(s)))]

        def job_items(t, g, kinds=("op", "val", "max", "shift")):
            return [("job", t, g, j) for j, (kind, _, _) in enumerate(t.jobs) if kind in kinds]

        def plan(t, g, n1, n2, nxt):
            steps = len(t.steps)
            if n1 is None or is_first(g):
                if n1 is None:
                    items = pre_items(nxt.sub if nxt else END, 0) + (job_items(nxt, (0, 0)) if nxt else [])
                else:
                    items = pre_items(t.sub, 1) + job_items(t, n1)
                    if t.ahead:
                        items += job_items(t, n2, ("op",))
                cuts = [0] * (steps - 1) + [len(items)]
            else:
                items = job_items(t, n1)
                if t.ahead:
                    items = job_items(t, n1, ("max", "shift", "val") if t.cross else ("val",))
                if t.ahead and n2 is not None:
                    items += job_items(t, n2, ("op",))
                cuts = [-(-len(items) * (n + 2) // (steps + 1)) for n in range(steps)]
            before = 0
            if t.cross:
                cuts = spread_over(t, [item_cost(one) for one in items])
                before = RING if items and items[0][0] == "job" else 0
                cuts = [max(before, c) for c in cuts]
            cuts = [0, before] + cuts
            return [items[a0:a1] for a0, a1 in zip(cuts, cuts[1:])]

        def item_cost(one):
            if one[0] == "pre":
                kind = prelude(one[1])[one[3]][0]
                return LATENCY[kind], LATENCY[kind] if kind in ("ln", "hn", "ffout") else 0
            t, j = one[1], one[3]
            cost = t.cost(*t.jobs[j])
            return cost, cost if t.jobs[j][0] == "shift" else 0

        def prepared(t, g, n1, nxt):
            if n1 is not None:
                return t, n1
            return (nxt, (0, 0)) if nxt else None

        def uses(eng, t, prev, nxt, one):
            def peeled(n):
                one(t, [unit(t, n + k) for k in range(-1, 3)], (prev, nxt))

            if not t.wide:
                for n in range(t.units):
                    peeled(n)
                return
            peeled(0)
            peeled(1)
            with eng.Fori(0, t.units // 4 - 1) as i:
                def at(v):
                    return (i, v) if v < 4 else (i + 1, v - 4)

                for v in range(2, 6):
                    one(t, [at(v + k) for k in range(-1, 3)], (prev, nxt))
            for n in range(t.units - 2, t.units):
                peeled(n)

        def whole_pass(eng, item, start, one, end=lambda t: None):
            for it in pre_items(0, 0) + job_items(ATTS[0], (0, 0)):
                item(it)
            start(ATTS[0], (0, 0))
            for n, t in enumerate(ATTS):
                uses(eng, t, ATTS[n - 1] if n else None, ATTS[n + 1] if n + 1 < len(ATTS) else None, one)
            end(ATTS[-1])
            for it in pre_items(END, 1):
                item(it)

        def maxima_ahead(t, n2):
            return job_items(t, n2, ("max",)) if not t.cross and n2 is not None else []

        def keys_from(t, u):
            if not t.cross:
                return (n_t if t.sub == 9 else h_t)[:, u, :]
            if t.src is not None or t.sub == 1:
                return src_t[:, u, :]
            return ctx_t[:, u, :]

        def bias_row(r):
            p0, c0 = R_PARTS[r % 3], r // 3 * P
            return ones[p0:p0 + 1, :], rows[p0:p0 + 1, c0:c0 + P]

        def norms_before(s, m):
            return sum(kind == "ln" for kind, _, _ in prelude(s)[:m])

        def attention_before(s):
            return ATTS[-1] if s == END else ATTS[[t.sub for t in ATTS].index(s) - 1]

        def projected(t):
            return wide_projected if t.wide else narrow_projected

        @block.sync
        def _(sp):
            for dst, name in ((cols[:, :], "cols"), (rows[:, :], "rows"), (squares[:, :], "squares"),
                              (rope_cos[:, :], "rope_cos"), (rope_sin[:, :], "rope_sin"),
                              (narrow_w[:, :, :].rearrange("p a c -> p (a c)"), "narrow_w"),
                              (src_w[:, :, :].rearrange("p a c -> p (a c)"), "src_w"),
                              (ff1_w[:, :], "ff1_w")):
                sp.dma_start(dst, a[name]).then_inc(const_in, 16)
            mods = a["mod_w"].rearrange("p (m c) -> p m c", c=P)
            sp.dma_start(mod_w, mods[:, 0:N_MOD_FIRST, :]).then_inc(const_in, 16)
            sp.dma_start(mod_w_rest[:, 0:N_MOD - N_MOD_FIRST, :], mods[:, N_MOD_FIRST:, :]).then_inc(const_in, 16)
            sp.dma_start(ff2_w[:, :, :, :].rearrange("p l f d -> p (l f d)"), a["ff2_w"]).then_inc(const_in, 16)
            tokens = a["x"].rearrange("(b u) (t p) d -> b u p t d", u=2, p=P)
            context = a["ctx"].rearrange("(b u) m d -> b u m d", u=2)
            result = a["out"].rearrange("(b u) (t p) d -> b u p t d", u=2, p=P)

            def load(b):
                full = (CT - 1) * P
                for u in range(2):
                    sp.dma_start(x_in[:, u, :, :], tokens[b, u, :, :, :]).then_inc(x_in_done.sem, 16)
                for u in range(2):
                    sp.dma_start(ctx_in[:, u, 0:CT - 1, :], context[b, u, 0:full, :].rearrange("(t p) d -> p t d", p=P))\
                        .then_inc(ctx_in_done.sem, 16)
                    sp.dma_start(ctx_in[0:LAST, u, CT - 1, :], context[b, u, full:M, :]).then_inc(ctx_in_done.sem, 16)

            def weights(b, t):
                w = SO if t.rope else SQS
                blob = a[f"wide{t.sub}"]

                def one(i, slot):
                    sp.wait_ge(stage_used.sem, stage_used.at(b, t, (i, 2 * slot), -2))
                    sp.sem_inc(waited_sp, 1)
                    sp.dma_start(stage[:, slot, 0:w], blob[i * 2 + slot, :, 0:w]).then_inc(stage_in[slot].sem, 16)
                    sp.wait_ge(wide_projected.sem, wide_projected.at(b, t, (i, 2 * slot), -2))
                    sp.sem_inc(waited_sp, 1)
                    sp.dma_start(wo_stage[:, slot, :], blob[i * 2 + slot, :, w:w + P]).then_inc(wo_in[slot].sem, 16)

                one(0, 0)
                one(0, 1)
                with sp.Fori(1, t.units // 4) as i:
                    one(i, 0)
                    one(i, 1)

            def one_pass(b, more):
                for s in WIDE:
                    weights(b, WIDE[s])
                if more:
                    sp.wait_ge(job_full.sem, job_full.pre(b, 1, 1, 8))
                    sp.sem_inc(waited_sp, 1)
                    load(b + 1)
                for u in range(2):
                    sp.wait_ge(x_out_ready.sem, x_out_ready.pre(b, END, u, 1))
                    sp.sem_inc(waited_sp, 1)
                    sp.dma_start(result[b, u, :, :, :], x_out[:, u, :, :]).then_inc(x_out_sent.sem, 16)
                sp.wait_ge(x_out_sent.sem, x_out_sent.pre(b, END, 1, 16))
                sp.sem_inc(x_out_free.sem, 2)

            sp.sem_inc(x_out_free.sem, 2)
            load(0)
            with sp.Fori(0, B // 2 - 1) as b:
                one_pass(b, True)
            one_pass(B // 2 - 1, False)

        @block.gpsimd
        def _(pool):
            pool.memset(ones[:, :], 1.0)
            pool.memset(ones_bf[:, :], 1.0)
            pool.memset(minus_half[:, :], -0.5)
            pool.memset(eps0[:, :], EPS0)
            pool.memset(eps1[:, :], EPS1)
            pool.memset(ctx_mv[:, :, :], 1.0)
            pool.memset(max_cols[:, :, :], 0.0)
            pool.memset(narrow_v[:, :, :, :, :], 1.0).then_inc(init_done, 2)
            pool.wait_ge(init_done, 2)
            pool.sem_inc(weight_step.sem, 1)

            def program(b):
                def item(one):
                    if one[0] != "pre":
                        return
                    _, sp, u, m = one
                    kind, s, j = prelude(sp)[m]
                    if kind == "ctx" and j == 0:
                        pool.wait_ge(ctx_mv_ready.sem, ctx_mv_ready.pre(b, sp, u, 1))
                        pool.tensor_tensor(ctx_var[:, :], ctx_mv[:, :, 1], eps0[:, 0:CT], ALU.add)\
                            .then_inc(ctx_var_ready.sem, 1)
                        pool.wait_ge(ctx_var_ready.sem, ctx_var_ready.pre(b, sp, u, 1))
                        pool.tensor_tensor(ctx_rstd[:, :], ctx_var[:, :], minus_half[:, 0:CT], ALU.pow)\
                            .then_inc(ctx_rstd_ready.sem, 1)
                    elif kind == "ln":
                        n = norms_before(sp, m) + 1
                        eps = eps0 if s // 3 in (0, 2) else eps1
                        pool.wait_ge(mv_ready.sem, mv_ready.pre(b, sp, u, n))
                        pool.tensor_tensor(var[:, :], mv[:, :, 1], eps[:, 0:QT], ALU.add).then_inc(var_ready.sem, 1)
                        pool.wait_ge(var_ready.sem, var_ready.pre(b, sp, u, n))
                        pool.tensor_tensor(rstd[:, :], var[:, :], minus_half[:, 0:QT], ALU.pow).then_inc(rstd_ready.sem, 1)
                    elif kind == "hn" and j == 0:
                        pool.wait_ge(hn_step.sem, hn_step.pre(b, sp, u, 4))
                        pool.tensor_tensor(hn_var[:, :], hn_var[:, :], eps1[:, :], ALU.add)\
                            .then_inc(hn_rstd_ready.sem, 1)
                        pool.wait_ge(hn_rstd_ready.sem, hn_rstd_ready.pre(b, sp, u, 1))
                        pool.tensor_tensor(hn_rstd[:, :], hn_var[:, :], minus_half[:, 0:32], ALU.pow)\
                            .then_inc(hn_rstd_ready.sem, 1)

                def add_weights(t, g, c):
                    if c == 0:
                        return
                    n = t.rows(t.chunks[c][0][1])
                    total = weight_sum[0:n, :, :].rearrange("p h n -> p (h n)")
                    pool.wait_ge(exp_done.sem, exp_done.at(b, t, g, c + 1))
                    if c == 1:
                        pool.wait_ge(wide_sums.sem, wide_sums.at(b, t, g, 0))
                        before = probs[0:n, 0, :]
                    else:
                        pool.wait_ge(weight_step.sem, weight_step.at(b, t, g, t.sum_steps(c - 1)))
                        before = total
                    pool.tensor_tensor(total, before, probs[0:n, c % PROBS, :], ALU.add).then_inc(weight_step.sem, 1)

                def use(t, units_, around):
                    (_, g, n1, n2), nxt = units_, around[1]
                    if t.wide:
                        for c in range(t.head):
                            add_weights(t, g, c)
                    todo = plan(t, g, n1, n2, nxt)
                    for one in todo[0]:
                        item(one)
                    for (kind, c), items in zip(t.steps, todo[1:]):
                        if t.wide and kind == "scores":
                            add_weights(t, g, c)
                        for one in items:
                            item(one)

                whole_pass(pool, item, lambda t, g: None, use)

            with pool.Fori(0, B // 2) as b:
                program(b)

        @block.tensor
        def _(pe):
            def mm(out, lhs, rhs, start, stop):
                return pe.matmul(out, lhs, rhs, start=start, stop=stop, skip_group_check=True)

            pe.sem_inc(av_done.sem, 1)
            pe.sem_inc(wide_projected.sem, 3)
            pe.sem_inc(wide_sums.sem, 1)
            pe.wait_ge(const_in, 16 * (N_CONST + 1))
            pe.wait_ge(cond_ready, 1)
            for m in range(N_MOD):
                silu = 6 <= m < 12 or m >= 18
                w = mod_w[:, m, :] if m < N_MOD_FIRST else mod_w_rest[:, m - N_MOD_FIRST, :]
                last = mm(scores[:, 0, m * B:(m + 1) * B], w,
                          cond_silu if silu else cols[:, C_COND:C_COND + B], True, True)
            last.then_inc(mod_full, 1)
            pe.wait_ge(init_done, 2)

            def program(b):
                def stored(sp, u, m):
                    pe.wait_ge(slot_free[m % RING].sem, slot_free[m % RING].pre(b, sp, u, m // RING + 1))

                def pre(sp, u, m):
                    kind, s, j = prelude(sp)[m]
                    if kind == "ctx" and j == 0:
                        pe.wait_ge(ctx_in_done.sem, ctx_in_done.pre(b, END, 1, 64))
                    elif kind == "ctx" and j == 4:
                        pe.wait_ge(ctx_norm_ready.sem, ctx_norm_ready.pre(b, sp, u, 1))
                    elif kind == "gate":
                        pe.wait_ge(diag_ready.sem, diag_ready.pre(b, sp, u, 1))
                    elif kind == "ln":
                        pe.wait_ge(xn_ready.sem, xn_ready.pre(b, sp, u, norms_before(sp, m) + 1))
                    elif (kind == "ff" or kind == "val" and not ATT[s].cross) and j == 0:
                        stored(sp, u, m - 1)
                    elif kind == "val" and j == 0:
                        for one in range(m - RING, m):
                            stored(sp, u, one)
                    elif kind == "hn" and j == 1:
                        pe.wait_ge(hn_step.sem, hn_step.pre(b, sp, u, 5))
                    pe.wait_ge(slot_free[m % RING].sem, slot_free[m % RING].pre(b, sp, u, m // RING))
                    out = ring[:, m % RING, :]
                    if kind == "ctx":
                        for i, t in enumerate(range(4 * (j % 4), min(4 * (j % 4) + 4, CT))):
                            n = P if t < CT - 1 else LAST
                            last = pe.transpose(out[0:DC, i * P:i * P + n], ctx_in[0:n, u, t, :], ident[0:n, 0:n])
                    elif kind == "gate":
                        last = mm(out[:, 0:3 * P], ones[:, :], gate_diag[:, :, :].rearrange("p a d -> p (a d)"), True, True)
                    elif kind == "src":
                        k, w = ATT[s].kc[j]
                        last = mm(out[:, 0:w], src_w[:, ATT[s].src, :], ctx_t[:, u, k:k + w], True, True)
                    elif kind == "val":
                        t = ATT[s]
                        t0, nt = t.vjobs[j]
                        src = src_t if t.cross else h_t
                        if t.vbias:
                            one, bias = bias_row(R_VB + NARROW_AT[s])
                            mm(out[:, 0:nt * P], one, bias.unsqueeze(1).broadcast_to([1, nt, P]), True, False)
                        for i in range(nt):
                            n = t.rows(t0 + i)
                            last = mm(out[0:n, i * P:(i + 1) * P], src[:, u, (t0 + i) * P:(t0 + i) * P + n],
                                      narrow_w[:, NARROW_AT[s], NV:NV + P], not t.vbias, i == nt - 1)
                    elif kind == "ln":
                        for q in range(QT):
                            last = pe.transpose(out[:, q * P:(q + 1) * P], xn[:, q, :], ident)
                    elif kind == "hn":
                        flat = hn[:, :, :].rearrange("p (t h) d -> p t (h d)", t=QT)
                        for q in range(QT):
                            src = flat[:, q, :] if j else h_t[:, u, q * P:(q + 1) * P]
                            last = pe.transpose(out[:, q * P:(q + 1) * P], src, ident)
                    elif kind == "ff":
                        l = FFN[s]
                        w1 = ff1_w[:, FF1_AT[l]:FF1_AT[l] + (512 if l < 2 else 1024)].rearrange("p (c d) -> p c d", d=P)
                        c0 = 2 * j if l < 2 else 2 * (j // 2) + FF * (j % 2)
                        for c in range(2):
                            last = mm(out[:, c * N:(c + 1) * N], w1[:, c0 + c, :], h_t[:, u, :], True, True)
                    else:
                        l = FFN[s]
                        hidden = 2 if l < 2 else 4
                        for q in range(QT):
                            mm(out[:, q * P:(q + 1) * P], *bias_row(R_OUT + s), q == 0, False)
                        for c in range(FF):
                            if c % 2 == 0:
                                stored(sp, u, m - hidden + (c // 2 if l < 2 else c + 1))
                            for q in range(QT):
                                last = mm(out[:, q * P:(q + 1) * P], ff_h[:, c, q * P:(q + 1) * P], ff2_w[:, l, c, :],
                                          False, c == FF - 1)
                    last.then_inc(job_full.sem, 1)

                def weight(t, g, col, n):
                    if t.wide:
                        return stage[0:n, g[1] // 2, col:col + P]
                    i = 2 * g[0] + g[1] // 2
                    base = {SQ: NQ, SK: NK}[col] + i * P
                    return narrow_w[0:n, NARROW_AT[t.sub], base:base + P]

                def job(t, g, j):
                    kind, i, k = t.jobs[j]
                    u, r = g[1] % 2, j % RING
                    src = keys_from(t, u)
                    if j == 0:
                        if isinstance(g[0], int) and g[0] == 0 and g[1] < 2:
                            n = len(prelude(t.sub))
                            for m in range(max(0, n - RING), n):
                                stored(t.sub, u, m)
                        if t.wide:
                            pe.wait_ge(stage_in[g[1] // 2].sem, stage_in[g[1] // 2].at(b, t, (g[0], 0), 16))
                    pe.wait_ge(slot_free[r].sem, slot_free[r].at(b, t, g, j // RING))
                    out = ring[:, r, :]
                    t0, nt = t.vjobs[i] if kind == "val" else (0, 0)
                    if kind == "op" and i == 0:
                        qsrc = (n_t if t.sub == 9 else h_t)[:, u, :]
                        if t.wide:
                            for h in range(2):
                                last = mm(out[:, h * N:(h + 1) * N], weight(t, g, (SQS if k else SQ) + h * P, D), qsrc,
                                          True, True)
                        else:
                            last = mm(out[:, 0:N], weight(t, g, SQ, D), qsrc, True, True)
                    elif kind == "op":
                        a0, w = t.kc[i - 1]
                        last = mm(out[:, 0:w], weight(t, g, SKS if k else SK, t.dk), src[0:t.dk, a0:a0 + w], True, True)
                    elif kind == "val":
                        for m in range(nt):
                            n = t.rows(t0 + m)
                            last = mm(out[0:n, m * P:(m + 1) * P], src[0:t.dk, (t0 + m) * P:(t0 + m) * P + n],
                                      stage[0:t.dk, g[1] // 2, SV:SV + P], True, True)
                    elif kind == "shift":
                        pe.wait_ge(max_ready.sem, max_ready.at(b, t, g, 1))
                        for q in range(QT):
                            last = mm(out[:, q * P:(q + 1) * P], max_cols[:, q, :], ident_part, True, True)
                    else:
                        h, q = i
                        kh, at = (h, u) if t.wide else (g[1] // 2, g[1])
                        if t.jobs[j - 1][0] != "max":
                            pe.wait_ge(op_ready.sem, op_ready.at(b, t, g, t.ops))
                        a0, w = t.kc[k]
                        for m, qq in enumerate(range(QT) if q is None else [q]):
                            last = mm(out[:, m * w:(m + 1) * w], qop[:, at, h, qq * P:(qq + 1) * P],
                                      kop[:, u, kh, a0:a0 + w], True, True)
                    last.then_inc(job_full.sem, 1)

                def item(one):
                    (pre if one[0] == "pre" else job)(*one[1:])

                def make_scores(t, g, c):
                    u = g[1] % 2
                    if c == 0:
                        if not t.fold:
                            pe.wait_ge(shift_ready.sem, shift_ready.at(b, t, g, 1))
                        else:
                            j = t.shift_job
                            pe.wait_ge(slot_free[j % RING].sem, slot_free[j % RING].at(b, t, g, j // RING + 1))
                    if c >= SCORES:
                        done = c - SCORES + 1
                    else:
                        done = 0 if is_first(g) else t.last_like(c, SCORES) + 1 - len(t.chunks)
                    pe.wait_ge(exp_done.sem, exp_done.at(b, t, g, done))
                    (h0, k), _ = t.chunks[c]
                    n = t.rows(k)
                    out = scores[0:n, c % SCORES, :]
                    if not t.fold:
                        mm(out, ones_bf[:, 0:n], shift[:, u, h0:h0 + 2, :], True, False)
                    if t.wide:
                        for h in range(2):
                            for part in range(2):
                                last = mm(out[:, h * N:(h + 1) * N], kop[:, u, h, k * P:k * P + n],
                                          qop[:, u, 2 * part + h, :], False, part == 1)
                    else:
                        last = mm(out, kop[:, u, g[1] // 2, k * P:k * P + n], qop[:, g[1], h0:h0 + 2, :], t.fold, True)
                    last.then_inc(scores_full.sem, 1)

                def weigh_values(t, g, k):
                    u = g[1] % 2
                    if k == 0:
                        if t.wide:
                            j = t.last_val
                            pe.wait_ge(slot_free[j % RING].sem, slot_free[j % RING].at(b, t, g, j // RING + 1))
                        else:
                            pe.wait_ge(values_set.sem, values_set.at(b, t, g, 1))
                        if t.wide:
                            pe.wait_ge(o_copied.sem, o_copied.at(b, t, g, 0))
                        else:
                            pe.wait_ge(inv_ready.sem, inv_ready.at(b, t, g, 0))
                    pe.wait_ge(exp_done.sem, exp_done.at(b, t, g, (k + 1) * t.per_tile))
                    n = t.rows(k)
                    for h, c, m in t.weigh[k]:
                        w = probs[0:n, c % PROBS, m * N:(m + 1) * N]
                        if t.wide:
                            vals, to = wide_v[0:n, u, k, h * 64:(h + 1) * 64], o_acc[h * 64:(h + 1) * 64, 0:N]
                        else:
                            vals, to = narrow_v[0:n, u, k, h, :], o_acc[h * 32:(h + 1) * 32, 0:N]
                        last = mm(to, vals, w, k == 0, k == t.kt - 1)
                    last.then_inc(av_done.sem, 1)

                def spread_sums(t, g):
                    if t.wide:
                        pe.wait_ge(weight_step.sem, weight_step.at(b, t, g, t.sum_steps(t.kt - 1)))
                        for h in range(2):
                            last = mm(o_acc[h * 64:(h + 1) * 64, N:2 * N], ones[:, 0:64], weight_sum[:, h, :], True, True)
                        last.then_inc(wide_sums.sem, 1)
                    else:
                        pe.wait_ge(o_copied.sem, o_copied.at(b, t, g, 1))
                        mm(o_acc[:, N:2 * N], sum_row, o_raw[:, :], True, True).then_inc(sums_spread.sem, 1)

                def init_y(t):
                    for u in range(2):
                        for q in range(QT):
                            mm(y_acc[:, u, q * P:(q + 1) * P], *bias_row(R_OUT + t.sub), u == 0 and q == 0, False)

                def project(t, g):
                    u = g[1] % 2
                    if is_first(g):
                        init_y(t)
                    if t.wide:
                        w = g[1] // 2
                        wo = wo_stage[:, w, :]
                        pe.wait_ge(wo_in[w].sem, wo_in[w].at(b, t, (g[0], 0), 16))
                    else:
                        gi = 2 * g[0] + g[1] // 2
                        wo = narrow_w[:, NARROW_AT[t.sub], NO + gi * P:NO + (gi + 1) * P]
                    pe.wait_ge(attn_ready.sem, attn_ready.at(b, t, g, 1))
                    for q in range(QT):
                        last = mm(y_acc[:, u, q * P:(q + 1) * P], attn[:, u, q * P:(q + 1) * P], wo, False, False)
                    last.then_inc(projected(t).sem, 1)

                def head(t, g, c):
                    if c < t.head:
                        make_scores(t, g, c)

                def start(t, g):
                    for c in range(t.head):
                        head(t, g, c)

                def use(t, units_, around):
                    (g0, g, n1, n2), (prev, nxt) = units_, around
                    todo = plan(t, g, n1, n2, nxt)
                    for one in todo[0]:
                        item(one)
                    if g0 is None and prev:
                        project(prev, prev.last_unit(1))
                    for n, ((kind, c), items) in enumerate(zip(t.steps, todo[1:])):
                        (make_scores if kind == "scores" else weigh_values)(t, g, c)
                        for one in items:
                            item(one)
                        if n == t.late and g0 is not None:
                            project(t, g0)
                    after = prepared(t, g, n1, nxt)
                    if after:
                        head(*after, 0)
                    spread_sums(t, g)
                    for c in range(1, SCORES):
                        if after:
                            head(*after, c)
                    for one in maxima_ahead(t, n2):
                        item(one)

                def end(t):
                    project(t, t.last_unit(1))

                whole_pass(pe, item, start, use, end)

            with pe.Fori(0, B // 2) as b:
                program(b)

        @block.scalar
        def _(act):
            act.sem_inc(exp_done.sem, 1)
            act.sem_inc(o_copied.sem, 1)
            act.sem_inc(stage_used.sem, 3)
            act.wait_ge(const_in, 16 * (N_CONST + 1))
            act.activation(cond_silu, cols[:, C_COND:C_COND + B], ACT.Silu).then_inc(cond_ready, 1)

            def copy(out, src, **kw):
                return act.activation(out, src, ACT.Identity, **kw)

            def program(b):
                def store_values(t, u, r, j):
                    t0, nt = t.vjobs[j]
                    whole = sum(t.rows(t0 + m) == P for m in range(nt))
                    for m0, m1, n in ((0, whole, P), (whole, nt, t.rows(t0 + nt - 1))):
                        if m1 > m0:
                            last = copy(wide_v[0:n, u, t0 + m0:t0 + m1, :],
                                        ring[0:n, r, m0 * P:m1 * P].rearrange("p (m c) -> p m c", c=P))
                    return last

                def set_values(t, g):
                    u = g[1] % 2
                    done = {m % RING: m for m, (kind, _, _) in enumerate(prelude(t.sub)) if kind == "val"}
                    for r, m in done.items():
                        act.wait_ge(slot_free[r].sem, slot_free[r].pre(b, t.sub, u, m // RING + 1))
                    c0 = (2 * g[0] + g[1] // 2) * 32
                    for k0, k1, n in ((0, t.keys // P, P), (t.keys // P, t.kt, t.rows(t.kt - 1))):
                        if k1 > k0:
                            last = copy(narrow_v[0:n, u, k0:k1, :, 0:8],
                                        wide_v[0:n, u, k0:k1, c0:c0 + 32].rearrange("p m (h c) -> p m h c", c=8))
                    last.then_inc(values_set.sem, 1)

                def pre(sp, u, m):
                    kind, s, j = prelude(sp)[m]
                    if kind not in ("ctx", "src", "val", "ff") or (kind == "ff" and FFN[s] >= 2 and j % 2):
                        return
                    act.wait_ge(job_full.sem, job_full.pre(b, sp, u, m + 1))
                    out = ring[:, m % RING, :]
                    if kind == "ctx":
                        a0 = (j % 4) * BANK
                        w = min(BANK, M - a0)
                        if j < 4:
                            last = copy(ctx_t[:, u, a0:a0 + w], out[0:DC, 0:w])
                        else:
                            last = copy(src_t[0:DC, u, a0:a0 + w], out[0:DC, 0:w], scale=cols[0:DC, C_CLNW:C_CLNW + 1],
                                        bias=cols[0:DC, C_CLNB:C_CLNB + 1])
                    elif kind == "val":
                        last = store_values(ATT[s], u, m % RING, j)
                    elif kind == "src":
                        k, w = ATT[s].kc[j]
                        col = C_SRCB + ATT[s].src
                        last = copy(src_t[:, u, k:k + w], out[:, 0:w], bias=cols[:, col:col + 1])
                    else:
                        l = FFN[s]
                        func = [ACT.Gelu, ACT.Gelu_apprx_tanh, ACT.Gelu, ACT.Silu][l]
                        for n in range(2):
                            c = 2 * j + n if l < 2 else j + n
                            col = C_FFB + l * 8 + c
                            dst = ff_h if l < 2 else ff_g
                            last = act.activation(dst[:, c, :], out[:, n * N:(n + 1) * N], func, bias=cols[:, col:col + 1])
                    last.then_inc(slot_free[m % RING].sem, 1)

                def job(t, g, j):
                    kind, i, k = t.jobs[j]
                    u, r = g[1] % 2, j % RING
                    if not t.wide and j == t.first_max:
                        set_values(t, g)
                    if kind == "max" or (kind == "op" and t.rope and k == 0):
                        return
                    if kind == "op" and t.rope:
                        act.wait_ge(rope_sum.sem, rope_sum.at(b, t, g, i + 1))
                        if i == 0:
                            last = copy(qop[:, u, 0:2, :].rearrange("p h n -> p (h n)"), raw[:, 0, :])
                        else:
                            a0, w = t.kc[i - 1]
                            v = raw[:, i % 2, 0:w]
                            copy(kop[0:64, u, 0, a0:a0 + w], v[0:64, :])
                            last = copy(kop[64:128, u, 1, a0:a0 + w], v[64:128, :])
                        last.then_inc(rope_high.sem, 1)
                        return
                    act.wait_ge(job_full.sem, job_full.at(b, t, g, j + 1))
                    if kind == "shift":
                        for h in range(4):
                            last = copy(qop[32 * h:32 * h + 1, g[1], h, :], ring[32 * h:32 * h + 1, r, 0:N])
                        last.then_inc(slot_free[r].sem, 1)
                        return
                    if kind == "op":
                        if i == 0:
                            act.wait_ge(op_ready.sem, op_ready.at(b, t, g, 0))
                        if i >= 2:
                            act.wait_ge(op_ready.sem, op_ready.at(b, t, g, i - 1))
                        a0, w = (0, 2 * N if t.wide else N) if i == 0 else t.kc[i - 1]
                        out = ring[:, r, 0:w]
                        if t.wide:
                            copy(raw[:, i % 2, 0:w], out)
                            if i == 0:
                                last = copy(qop[:, u, 0:2, :].rearrange("p h n -> p (h n)"), out)
                            else:
                                copy(kop[0:64, u, 0, a0:a0 + w], out[0:64, :])
                                last = copy(kop[64:128, u, 1, a0:a0 + w], out[64:128, :])
                        else:
                            col = (C_QB if i == 0 else C_KB) + NARROW_AT[t.sub] * 4 + 2 * g[0] + g[1] // 2
                            copy(raw[:, i % 2, 0:w], out, bias=cols[:, col:col + 1])
                            last = copy(high[:, i % 2, 0:w], out, bias=cols[:, col:col + 1])
                        last.then_inc(slot_free[r].sem, 1)
                        return
                    store_values(t, u, r, i).then_inc(slot_free[r].sem, 1)
                    if j == t.last_val:
                        act.sem_inc(stage_used.sem, 1)

                def item(one):
                    (pre if one[0] == "pre" else job)(*one[1:])

                def exps(t, g, c):
                    act.wait_ge(scores_full.sem, scores_full.at(b, t, g, c + 1))
                    if c >= PROBS:
                        used, fewer = c - PROBS, (0, 0)
                    else:
                        used, fewer = t.last_like(c, PROBS), (t.kt, t.sum_steps(t.kt - 1))
                    if c < PROBS and is_first(g):
                        weighed = added = 0
                    else:
                        weighed, added = t.tiles_of(used) - fewer[0], t.sum_steps(used) - fewer[1]
                    act.wait_ge(av_done.sem, av_done.at(b, t, g, weighed))
                    if t.wide or (c < PROBS and is_first(g)):
                        act.wait_ge(weight_step.sem, weight_step.at(b, t, g, added))
                    n = t.rows(t.chunks[c][0][1])
                    act.activation(probs[0:n, c % PROBS, :], scores[0:n, c % SCORES, :], ACT.Exp, scale=t.scale)\
                        .then_inc(exp_done.sem, 1)

                def start(t, g):
                    for c in range(t.head):
                        exps(t, g, c)

                def use(t, units_, around):
                    (_, g, n1, n2), nxt = units_, around[1]
                    todo = plan(t, g, n1, n2, nxt)
                    for one in todo[0]:
                        item(one)
                    for (kind, c), items in zip(t.steps, todo[1:]):
                        if kind == "scores":
                            exps(t, g, c)
                        for one in items:
                            item(one)
                    after = prepared(t, g, n1, nxt)
                    if t.wide:
                        if after:
                            exps(*after, 0)
                        act.wait_ge(wide_sums.sem, wide_sums.at(b, t, g, 1))
                        copy(o_inv[:, :], o_acc[:, N:2 * N])
                    else:
                        act.wait_ge(av_done.sem, av_done.at(b, t, g, t.kt))
                    copy(o_raw[:, :], o_acc[:, 0:N]).then_inc(o_copied.sem, 1)
                    if after:
                        for c in range(1 if t.wide else 0, after[0].head):
                            exps(*after, c)
                    for one in maxima_ahead(t, n2):
                        item(one)

                whole_pass(act, item, start, use)

            with act.Fori(0, B // 2) as b:
                program(b)

        @block.vector
        def _(dve):
            for r in range(RING):
                dve.sem_inc(slot_free[r].sem, 1)
            dve.sem_inc(op_ready.sem, 1)
            dve.sem_inc(rope_sum.sem, 1)
            dve.sem_inc(attn_ready.sem, 1)
            dve.sem_inc(x_out_ready.sem, 2)
            dve.wait_ge(const_in, 16 * (N_CONST + 1))
            dve.wait_ge(init_done, 2)
            dve.tensor_copy(ident_bf[:, :], ident)

            def wide_cols(c, n):
                return cols[:, c:c + n].unsqueeze(2).broadcast_to([P, n, B])

            by_mod = mod_flat.rearrange("p b m -> p m b")
            dve.wait_ge(mod_full, 1)
            mod_psum = scores[:, 0, 0:N_MOD * B].rearrange("p (m b) -> p m b", b=B)
            dve.tensor_tensor(mod_raw, mod_psum, wide_cols(C_MODB, N_MOD), ALU.add).then_inc(mod_step, 1)
            dve.wait_ge(mod_step, 1)
            dve.tensor_scalar(mod_scale, mod_raw[:, 0:24:2, :], 1.0, None, ALU.add).then_inc(mod_step, 1)
            dve.wait_ge(mod_step, 2)
            dve.tensor_tensor(by_mod[:, 0:24:2, :], mod_scale, wide_cols(C_LNW, 12), ALU.mult)
            dve.tensor_copy(by_mod[:, 24:27, :], mod_raw[:, 24:27, :])
            dve.tensor_tensor(mod_scale, mod_scale, wide_cols(C_LNB, 12), ALU.mult).then_inc(mod_step, 1)
            dve.wait_ge(mod_step, 3)
            dve.tensor_tensor(by_mod[:, 1:24:2, :], mod_scale, mod_raw[:, 1:24:2, :], ALU.add).then_inc(mod_step, 1)
            dve.wait_ge(mod_step, 4)

            def program(b):
                def gate_of(u, s):
                    return gate_rows[:, u, s - 9, :].unsqueeze(1).broadcast_to([P, QT, P])

                def tokens(sp, u):
                    to = x[:, u, :, :]
                    if sp == 0:
                        dve.wait_ge(x_out_ready.sem, x_out_ready.pre(b, END, 1 if u == 0 else u, -1))
                        if u == 0:
                            dve.tensor_copy(ab[:, :, :], mod_ab[:, b, :, :]).then_inc(ab_ready.sem, 1)
                        dve.wait_ge(x_in_done.sem, x_in_done.pre(b, END, 1, 32))
                        dve.tensor_copy(to, x_in[:, u, :, :]).then_inc(x_done.sem, 1)
                        return
                    t = attention_before(sp)
                    dve.wait_ge(projected(t).sem, projected(t).at(b, t, t.last_unit(u), 1))
                    y = y_acc[:, u, :].rearrange("p (q d) -> p q d", q=QT)
                    if t.sub >= 9:
                        dve.tensor_tensor(xn[:, :, :], y, gate_of(u, t.sub), ALU.mult).then_inc(y_gated.sem, 1)
                        dve.wait_ge(y_gated.sem, y_gated.pre(b, sp, u, 1))
                        y = xn[:, :, :]
                    dve.tensor_tensor(to, to, y, ALU.add).then_inc(x_done.sem, 1)

                def layernorm(sp, u, m, s):
                    n = norms_before(sp, m) + 1
                    if n == 1:
                        tokens(sp, u)
                        dve.wait_ge(x_done.sem, x_done.pre(b, sp, u, 1))
                    else:
                        dve.wait_ge(slot_free[(m - 1) % RING].sem, slot_free[(m - 1) % RING].pre(b, sp, u, (m - 1) // RING + 1))
                    dve.sem_inc(waited_dve, 1)
                    for q in range(QT):
                        last = dve.bn_stats(stats[:, q, :], x[:, u, q, :])
                    last.then_inc(stat.sem, 1)
                    dve.wait_ge(stat.sem, stat.pre(b, sp, u, n))
                    dve.sem_inc(waited_dve, 1)
                    for q in range(QT):
                        last = dve.bn_aggr(mv[:, q, :], stats[:, q, :])
                    last.then_inc(mv_ready.sem, 1)
                    dve.wait_ge(mv_ready.sem, mv_ready.pre(b, sp, u, n))
                    dve.wait_ge(rstd_ready.sem, rstd_ready.pre(b, sp, u, n))
                    for q in range(QT):
                        last = dve.tensor_scalar(xn[:, q, :], x[:, u, q, :], mv[:, q, 0:1], rstd[:, q:q + 1],
                                                 ALU.subtract, ALU.mult)
                    last.then_inc(xn_ready.sem, 1)
                    dve.wait_ge(job_full.sem, job_full.pre(b, sp, u, m + 1))
                    dve.wait_ge(ab_ready.sem, ab_ready.pre(b, 0, 0, 1))
                    dve.tensor_scalar(h_t[:, u, :], ring[:, m % RING, 0:N], ab[:, u, 2 * s:2 * s + 1],
                                      ab[:, u, 2 * s + 1:2 * s + 2], ALU.mult, ALU.add).then_inc(slot_free[m % RING].sem, 1)

                tiles = [(t, P if t < CT - 1 else LAST) for t in range(CT)]

                def context(sp, u, m, j):
                    if j == 0:
                        dve.wait_ge(ctx_in_done.sem, ctx_in_done.pre(b, END, 1, 64))
                        dve.sem_inc(waited_dve, 1)
                        for t, n in tiles:
                            last = dve.bn_stats(ctx_stats[0:n, t, :], ctx_in[0:n, u, t, :])
                        last.then_inc(ctx_stat.sem, 1)
                        dve.wait_ge(ctx_stat.sem, ctx_stat.pre(b, sp, u, 1))
                        dve.sem_inc(waited_dve, 1)
                        for t, n in tiles:
                            last = dve.bn_aggr(ctx_mv[0:n, t, :], ctx_stats[0:n, t, :])
                        last.then_inc(ctx_mv_ready.sem, 1)
                    elif j == 4:
                        dve.wait_ge(ctx_mv_ready.sem, ctx_mv_ready.pre(b, sp, u, 1))
                        dve.wait_ge(ctx_rstd_ready.sem, ctx_rstd_ready.pre(b, sp, u, 1))
                        dve.wait_ge(job_full.sem, job_full.pre(b, sp, u, m))
                        for t, n in tiles:
                            rows_ = ctx_in[0:n, u, t, :]
                            last = dve.tensor_scalar(rows_, rows_, ctx_mv[0:n, t, 0:1], ctx_rstd[0:n, t:t + 1],
                                                     ALU.subtract, ALU.mult)
                        last.then_inc(ctx_norm_ready.sem, 1)

                def gate(sp, u, m):
                    dve.wait_ge(ab_ready.sem, ab_ready.pre(b, 0, 0, 1))
                    dve.tensor_tensor(gate_diag[:, :, :], ident.unsqueeze(1).broadcast_to([P, 3, P]),
                                      ab[:, u, 24:27].unsqueeze(2).broadcast_to([P, 3, P]), ALU.mult)\
                        .then_inc(diag_ready.sem, 1)
                    dve.wait_ge(job_full.sem, job_full.pre(b, sp, u, m + 1))
                    dve.tensor_copy(gate_rows[:, u, :, :], ring[:, m % RING, 0:3 * P].rearrange("p (a d) -> p a d", a=3))\
                        .then_inc(slot_free[m % RING].sem, 1)

                def headnorm(sp, u, m, j):
                    def step(n):
                        dve.wait_ge(hn_step.sem, hn_step.pre(b, sp, u, n))

                    def spread(v):
                        return v[:, :].unsqueeze(2).broadcast_to([P, 32, 8])

                    r = m % RING
                    dve.wait_ge(job_full.sem, job_full.pre(b, sp, u, m + 1))
                    if j == 1:
                        dve.tensor_copy(n_t[:, u, :], ring[:, r, 0:N]).then_inc(slot_free[r].sem, 1)
                        return
                    dve.tensor_copy(hn[:, :, :], ring[:, r, 0:N].rearrange("p (h d) -> p h d", d=8))\
                        .then_inc(slot_free[r].sem, 1)
                    dve.wait_ge(slot_free[r].sem, slot_free[r].pre(b, sp, u, m // RING + 1))
                    dve.tensor_reduce(hn_sum[:, :], hn[:, :, :], AX.X, ALU.add).then_inc(hn_step.sem, 1)
                    step(1)
                    dve.scalar_tensor_tensor(hn_cen[:, :, :], spread(hn_sum), -1.0 / 8, hn[:, :, :], ALU.mult, ALU.add)\
                        .then_inc(hn_step.sem, 1)
                    step(2)
                    dve.scalar_tensor_tensor(hn_sq[:, :, :], hn_cen[:, :, :], 1.0 / 8, hn_cen[:, :, :], ALU.mult, ALU.mult)\
                        .then_inc(hn_step.sem, 1)
                    step(3)
                    dve.tensor_reduce(hn_var[:, :], hn_sq[:, :, :], AX.X, ALU.add).then_inc(hn_step.sem, 1)
                    dve.wait_ge(hn_rstd_ready.sem, hn_rstd_ready.pre(b, sp, u, 2))
                    dve.tensor_tensor(hn[:, :, :], hn_cen[:, :, :], spread(hn_rstd), ALU.mult)\
                        .then_inc(hn_step.sem, 1)

                def feed_forward(sp, u, m, s, j):
                    if FFN[s] < 2 or j % 2 == 0:
                        return
                    dve.wait_ge(job_full.sem, job_full.pre(b, sp, u, m + 1))
                    dve.wait_ge(slot_free[(m - 1) % RING].sem, slot_free[(m - 1) % RING].pre(b, sp, u, (m - 1) // RING + 1))
                    for n in range(2):
                        c = j - 1 + n
                        col = C_FFB + FFN[s] * 8 + FF + c
                        last = dve.scalar_tensor_tensor(ff_h[:, c, :], ring[:, m % RING, n * N:(n + 1) * N],
                                                        cols[:, col:col + 1], ff_g[:, c, :], ALU.add, ALU.mult)
                    last.then_inc(slot_free[m % RING].sem, 1)

                def ff_output(sp, u, m, s):
                    r = m % RING
                    dve.wait_ge(job_full.sem, job_full.pre(b, sp, u, m + 1))
                    y = ring[:, r, 0:QT * D].rearrange("p (q d) -> p q d", q=QT)
                    if sp != END:
                        dve.tensor_tensor(x[:, u, :, :], x[:, u, :, :], y, ALU.add).then_inc(slot_free[r].sem, 1)
                        return
                    dve.tensor_tensor(xn[:, :, :], y, gate_of(u, s), ALU.mult).then_inc(slot_free[r].sem, 1)
                    dve.wait_ge(slot_free[r].sem, slot_free[r].pre(b, sp, u, m // RING + 1))
                    dve.wait_ge(x_out_free.sem, x_out_free.pre(b, END, u, -1))
                    dve.tensor_tensor(x_out[:, u, :, :], x[:, u, :, :], xn[:, :, :], ALU.add).then_inc(x_out_ready.sem, 1)

                def pre(sp, u, m):
                    kind, s, j = prelude(sp)[m]
                    if kind == "ctx":
                        context(sp, u, m, j)
                    elif kind == "gate":
                        gate(sp, u, m)
                    elif kind == "ln":
                        layernorm(sp, u, m, s)
                    elif kind == "hn":
                        headnorm(sp, u, m, j)
                    elif kind == "ff":
                        feed_forward(sp, u, m, s, j)
                    elif kind == "ffout":
                        ff_output(sp, u, m, s)

                def columns(t, i):
                    return (0, 2 * N if t.wide else N) if i == 0 else t.kc[i - 1]

                def low_parts(t, g, i):
                    u = g[1] % 2
                    a0, w = columns(t, i)
                    v = raw[:, i % 2, 0:w]
                    if t.rope:
                        dve.wait_ge(rope_high.sem, rope_high.at(b, t, g, i + 1))
                    if t.wide and i == 0:
                        last = dve.tensor_tensor(qop[:, u, 2:4, :].rearrange("p h n -> p (h n)"), v,
                                                 qop[:, u, 0:2, :].rearrange("p h n -> p (h n)"), ALU.subtract)
                    elif t.wide:
                        dve.tensor_tensor(kop[64:128, u, 0, a0:a0 + w], v[0:64, :], kop[0:64, u, 0, a0:a0 + w],
                                          ALU.subtract)
                        last = dve.tensor_tensor(kop[0:64, u, 1, a0:a0 + w], v[64:128, :],
                                                 kop[64:128, u, 1, a0:a0 + w], ALU.subtract)
                    elif i == 0:
                        dve.scalar_tensor_tensor(qsplit[:, :], high[:, 0, 0:w], cols[:, C_NEGQ:C_NEGQ + 1], v,
                                                 ALU.mult, ALU.add).then_inc(q_split.sem, 1)
                        dve.wait_ge(q_split.sem, q_split.at(b, t, g, 1))
                        for h in range(4):
                            last = dve.tensor_scalar(qop[:, g[1], h, :], qsplit[:, :], cols[:, C_HEAD + h:C_HEAD + h + 1],
                                                     None, ALU.mult)
                    else:
                        last = dve.scalar_tensor_tensor(kop[:, u, g[1] // 2, a0:a0 + w], high[:, i % 2, 0:w],
                                                        cols[:, C_NEGK:C_NEGK + 1], v, ALU.mult, ALU.add)
                    last.then_inc(op_ready.sem, 1)

                def job(t, g, j):
                    kind, i, k = t.jobs[j]
                    u, r = g[1] % 2, j % RING
                    if t.rope and t.cross and kind == "val" and i == 0:
                        low_parts(t, g, t.ops - 1)
                    if kind == "val":
                        return
                    if kind == "shift":
                        maxima(t, g, max_cols[:, :, :].rearrange("p q (h r) -> p h q r", r=32)[:, :, :, 0])
                        return
                    if kind == "max":
                        h, q = i
                        dve.wait_ge(job_full.sem, job_full.at(b, t, g, j + 1))
                        w = t.kc[k][1]
                        if q is None:
                            src = ring[:, r, 0:QT * w].rearrange("p (q k) -> p q k", q=QT)
                            dst = max_part[:, u, 2 * h:2 * h + 2, 0]
                        else:
                            src, dst = ring[:, r, 0:w], max_part[:, u, 2 * h + q, k:k + 1]
                        dve.tensor_reduce(dst, src, AX.X, ALU.max).then_inc(slot_free[r].sem, 1)
                        return
                    if not t.rope:
                        dve.wait_ge(slot_free[r].sem, slot_free[r].at(b, t, g, j // RING + 1))
                        low_parts(t, g, i)
                        return
                    a0, w = columns(t, i)
                    v = raw[:, i % 2, 0:w]
                    dve.wait_ge(job_full.sem, job_full.at(b, t, g, j + 1))
                    if k:
                        dve.wait_ge(rope_sum.sem, rope_sum.at(b, t, g, i))
                    else:
                        dve.wait_ge(op_ready.sem, op_ready.at(b, t, g, max(i - 1, 0)))
                    table = rope_sin if k else rope_cos
                    tab, src = table[:, a0:a0 + w], ring[:, r, 0:w]
                    dst = raw_swap[:, 0:w] if k else v
                    if i == 0:
                        tab = table[:, 0:N].unsqueeze(1).broadcast_to([P, 2, N])
                        src = src.rearrange("p (h n) -> p h n", h=2)
                        dst = dst.rearrange("p (h n) -> p h n", h=2)
                    dve.tensor_tensor(dst, src, tab, ALU.mult).then_inc(slot_free[r].sem, 1)
                    if k == 0:
                        return
                    for rr, jj in ((r, j), ((j - 1) % RING, j - 1)):
                        dve.wait_ge(slot_free[rr].sem, slot_free[rr].at(b, t, g, jj // RING + 1))
                    dve.tensor_tensor(v, v, raw_swap[:, 0:w], ALU.add).then_inc(rope_sum.sem, 1)
                    if i >= 1:
                        low_parts(t, g, i - 1)
                    if i == t.ops - 1 and not t.cross:
                        low_parts(t, g, i)

                def item(one):
                    (pre if one[0] == "pre" else job)(*one[1:])

                def maxima(t, g, out):
                    nq = t.heads * QT
                    parts = len(t.kc) if t.cross else 1
                    j = t.last_max
                    dve.wait_ge(slot_free[j % RING].sem, slot_free[j % RING].at(b, t, g, j // RING + 1))
                    src = max_part[:, g[1] % 2, 0:nq, 0:parts].rearrange("p (h q) k -> p h q k", q=QT)
                    dve.tensor_reduce(out, src, AX.X, ALU.max, negate=True).then_inc(max_ready.sem, 1)

                def shifts(t, g):
                    if t.fold:
                        return
                    u = g[1] % 2
                    nq = t.heads * QT
                    maxima(t, g, max_neg[:, u, 0:nq].rearrange("p (h q) -> p h q", q=QT))
                    dve.wait_ge(max_ready.sem, max_ready.at(b, t, g, 1))
                    dve.tensor_tensor(shift[:, u, 0:t.heads, :].rearrange("p h (q k) -> p (h q) k", q=QT),
                                      ident_bf[:, :].unsqueeze(1).broadcast_to([P, nq, P]),
                                      max_neg[:, u, 0:nq].unsqueeze(2).broadcast_to([P, nq, P]), ALU.mult)\
                        .then_inc(shift_ready.sem, 1)

                def normalise(t, g):
                    u = g[1] % 2
                    made = o_copied if t.wide else sums_spread
                    dve.wait_ge(made.sem, made.at(b, t, g, 1))
                    dve.reciprocal(o_inv[:, :], o_inv[:, :] if t.wide else o_acc[:, N:2 * N]).then_inc(inv_ready.sem, 1)
                    dve.wait_ge(inv_ready.sem, inv_ready.at(b, t, g, 1))
                    dve.tensor_tensor(attn[:, u, :], o_raw[:, :], o_inv[:, :], ALU.mult)\
                        .then_inc(attn_ready.sem, 1)

                def use(t, units_, around):
                    (_, g, n1, n2), nxt = units_, around[1]
                    for items in plan(t, g, n1, n2, nxt):
                        for one in items:
                            item(one)
                    after = prepared(t, g, n1, nxt)
                    if after and (not t.ahead or n1 is None or is_first(g)):
                        shifts(*after)
                    normalise(t, g)
                    for one in maxima_ahead(t, n2):
                        item(one)
                    if maxima_ahead(t, n2):
                        shifts(t, n2)

                whole_pass(dve, item, shifts, use)

            with dve.Fori(0, B // 2) as b:
                program(b)



def _pad(w, n):
    import numpy as np
    out = np.zeros((n, *w.shape[1:]), np.float32)
    out[:w.shape[0]] = w
    return out


def _swapped(w):
    return w.reshape(w.shape[0], -1, 2)[:, :, ::-1].reshape(w.shape)


def _wide_blob(wq, wk, wv, wo, rope):
    import numpy as np
    out = np.zeros((H // 2, P, STAGE if rope else SQS + P), np.float32)
    for g in range(H // 2):
        pair = slice(g * P, (g + 1) * P)

        def twice(w, at):
            for h in range(2):
                one = w[:, g * P + h * 64:g * P + (h + 1) * 64]
                out[g, :, at + h * P:at + h * P + 64] = one
                out[g, :, at + h * P + 64:at + (h + 1) * P] = one

        twice(wq, SQ)
        out[g, 0:wk.shape[0], SK:SK + P] = wk[:, pair]
        out[g, 0:wv.shape[0], SV:SV + P] = wv[:, pair]
        out[g, :, -P:] = wo[pair, :]
        if rope:
            twice(_swapped(wq), SQS)
            out[g, 0:wk.shape[0], SKS:SKS + P] = _swapped(wk)[:, pair]
    return out


def _spread(w):
    import numpy as np
    lead = w.shape[:-1]
    out = np.zeros((*lead, 4, 4, 4, 8), np.float32)
    out[..., 1:, :] = w.reshape(*lead, 4, 4, 1, 8)
    return out.reshape(*lead, 4, P)


def kernel(**inputs):
    import numpy as np
    import concourse.bacc as bacc
    from concourse.bass_utils import run_bass_kernel_spmd

    i = {k: np.asarray(v) for k, v in inputs.items()}

    def w(layer, name):
        return i[f"L{layer}_xcond_{name}"]

    f32 = np.float32
    l1w, l1b = np.split(w(1, "W_ada"), 6, axis=1), np.split(w(1, "b_ada"), 6)
    l3w, l3b = np.split(w(3, "adaln_w").T, 9, axis=1), np.split(w(3, "adaln_b"), 9)
    mods = [(w(0, "g1_w"), w(0, "g1_b")), (w(0, "b1_w"), w(0, "b1_b"))] * 2
    mods += [(w(0, "g2_w"), w(0, "g2_b")), (w(0, "b2_w"), w(0, "b2_b"))]
    for n in range(3):
        mods += [(l1w[2 * n + 1], l1b[2 * n + 1]), (l1w[2 * n], l1b[2 * n])]
    for n in range(1, 4):
        for half in range(2):
            mods.append((w(2, f"n{n}_w")[:, half * P:(half + 1) * P], w(2, f"n{n}_b")[half * P:(half + 1) * P]))
    for n in range(3):
        mods += [(l3w[3 * n + 1], l3b[3 * n + 1]), (l3w[3 * n], l3b[3 * n])]
    mods += [(l3w[3 * n + 2], l3b[3 * n + 2]) for n in range(3)]

    zero, eye = np.zeros(P, f32), np.eye(P, dtype=f32)
    qkv, qkv_b = w(1, "W_qkv"), w(1, "b_qkv")
    ca, ca_b = w(3, "ca_in_w").T, w(3, "ca_in_b")

    def on_diagonal(v):
        out = np.zeros((P, P), f32)
        out[np.arange(P), np.arange(P)] = np.tile(v, H)
        return out

    narrow = [
        (qkv[:, 0:P], qkv_b[0:P], qkv[:, P:2 * P], qkv_b[P:2 * P], qkv[:, 2 * P:], qkv_b[2 * P:], w(1, "W_proj")),
        (w(1, "W_q"), zero, w(1, "W_k"), zero, w(1, "W_v"), zero, w(1, "W_out")),
        (on_diagonal(w(3, "qn_w")), np.tile(w(3, "qn_b"), H), on_diagonal(w(3, "kn_w")), np.tile(w(3, "kn_b"), H),
         eye, zero, eye),
        (ca[:, 0:P], ca_b[0:P], ca[:, P:2 * P], ca_b[P:2 * P], ca[:, 2 * P:], ca_b[2 * P:], w(3, "ca_out_w").T),
    ]

    cols = np.zeros((P, C_END), f32)
    for m, (_, bias) in enumerate(mods):
        cols[:, C_MODB + m] = bias
    cols[:, C_LNW:C_LNW + 12] = 1
    for s, n in ((0, 1), (1, 1), (2, 2)):
        cols[:, C_LNW + s], cols[:, C_LNB + s] = w(0, f"ln{n}_w"), w(0, f"ln{n}_b")
    cols[0:DC, C_CLNW], cols[0:DC, C_CLNB] = w(0, "ca_lnc_w"), w(0, "ca_lnc_b")
    cols[:, C_SRCB], cols[:, C_SRCB + 1] = w(1, "b_ctx"), w(3, "cond_b")
    half = FF * P
    b_ff2 = w(2, "ff_b1")
    for l, bias in ((0, w(0, "ff_b1")), (1, w(1, "b_fc1")), (2, np.concatenate([b_ff2[half:], b_ff2[:half]]))):
        cols[:, C_FFB + l * 8:C_FFB + l * 8 + len(bias) // P] = bias.reshape(-1, P).T
    for n, (_, bq, _, bk, _, _, _) in enumerate(narrow):
        cols[:, C_QB + 4 * n:C_QB + 4 * n + 4] = _spread(bq).T
        cols[:, C_KB + 4 * n:C_KB + 4 * n + 4] = _spread(bk).T
        cols[::32, C_KB + 4 * n:C_KB + 4 * n + 4] = SHIFT
    r = np.arange(P)
    cols[(r // 8) % 4 == 2, C_NEGK] = -1
    cols[(r // 8) % 4 == 3, C_NEGQ] = -1
    for h in range(4):
        cols[r // 32 == h, C_HEAD + h] = 1
    cols[:, C_COND:C_COND + B] = i["cond_1024"].T

    rows = np.zeros((R_PARTS[-1] + 1, R_COLS), f32)

    def set_row(r, bias):
        rows[R_PARTS[r % 3], r // 3 * P:(r // 3 + 1) * P] = bias

    outs = {0: w(0, "sa_bo"), 1: w(0, "ca_bo"), 2: w(0, "ff_b2"), 3: w(1, "b_proj"), 4: w(1, "b_out"), 5: w(1, "b_fc2"),
            6: w(2, "o1_b"), 7: w(2, "o2_b"), 8: w(2, "ff_b2"), 10: w(3, "ca_out_b")}
    for s, bias in outs.items():
        set_row(R_OUT + s, bias)
    for n, one in enumerate(narrow):
        set_row(R_VB + n, one[5])

    squares = np.zeros((P, K_END), f32)
    squares[:, K_ID:K_ID + P] = eye
    squares[np.arange(P), K_PART + np.arange(P)] = 1 / SHIFT
    for h in range(4):
        squares[32 * h + 8, K_SEL + 32 * h:K_SEL + 32 * h + 32] = 1

    narrow_w = np.zeros((P, 4, NCOLS), f32)
    for n, (wq, _, wk, _, wv, _, wo) in enumerate(narrow):
        narrow_w[:, n, NQ:NQ + 4 * P] = _spread(wq).reshape(P, -1)
        narrow_w[:, n, NK:NK + 4 * P] = _spread(wk).reshape(P, -1)
        narrow_w[:, n, NV:NV + P] = wv
        for g in range(4):
            for h in range(4):
                narrow_w[32 * h:32 * h + 8, n, NO + g * P:NO + (g + 1) * P] = wo[(4 * g + h) * 8:(4 * g + h) * 8 + 8]

    inv = (f32(1.0) / f32(10000.0) ** (np.arange(0, 64, 2, dtype=f32) / f32(64))).astype(f32)
    angle = np.arange(M, dtype=f32)[None, :] * inv[(r % 64) // 2][:, None]
    rope_sin = np.sin(angle).astype(f32)
    rope_sin[r % 2 == 0] = -rope_sin[r % 2 == 0]

    ff2 = [w(0, "ff_w2"), w(1, "W_fc2"), w(2, "ff_w2"), w(3, "w2").T]
    g2 = w(2, "ff_w1")
    wkv0, ckv0 = w(0, "sa_wkv"), w(0, "ca_wkv")
    mid = H * 64
    arrays = {
        "x": i["x"], "ctx": i["ctx_768"], "cols": cols, "rows": rows, "squares": squares,
        "mod_w": np.concatenate([m for m, _ in mods], axis=1),
        "rope_cos": np.cos(angle).astype(f32), "rope_sin": rope_sin,
        "narrow_w": narrow_w.reshape(P, -1),
        "src_w": np.concatenate([w(1, "W_ctx"), w(3, "cond_w").T], axis=1),
        "ff1_w": np.concatenate([w(0, "ff_w1"), w(1, "W_fc1"), g2[:, half:], g2[:, :half], w(3, "w1").T, w(3, "w3").T], axis=1),
        "ff2_w": np.stack([m.reshape(FF, P, P).transpose(1, 0, 2) for m in ff2], axis=1).reshape(P, -1),
        "wide0": _wide_blob(w(0, "sa_wq"), wkv0[:, :mid], wkv0[:, mid:], w(0, "sa_wo"), True),
        "wide1": _wide_blob(w(0, "ca_wq"), ckv0[:, :mid], ckv0[:, mid:], w(0, "ca_wo"), True),
        "wide6": _wide_blob(w(2, "q1"), w(2, "k1"), w(2, "v1"), w(2, "o1_w"), False),
        "wide7": _wide_blob(w(2, "q2"), w(2, "k2"), w(2, "v2"), w(2, "o2_w"), False),
    }
    arrays = {k: np.ascontiguousarray(v) for k, v in arrays.items()}
    nc = bacc.Bacc("TRN2", target_bir_lowering=False, num_devices=1)
    drams = {k: nc.dram_tensor(f"in_{k}", v.shape, mybir.dt.from_np(v.dtype), kind="ExternalInput").ap()
             for k, v in arrays.items()}
    drams["out"] = nc.dram_tensor("out", (B, N, D), F32, kind="ExternalOutput").ap()
    build(nc, drams)
    got = run_bass_kernel_spmd(nc, [{f"in_{k}": v for k, v in arrays.items()}], core_ids=[0])
    return got.results[0]["out"]
```
